# Optimizing a Trainium2 kernel written in Bass

```python
import numpy as np
import jax
import jax.numpy as jnp

def _softmax(x, axis=-1):
    return jax.nn.softmax(x, axis=axis)

def _gelu(x):
    return jax.nn.gelu(x, approximate=True)

def _silu(x):
    return jax.nn.silu(x)

def _sigmoid(x):
    return jax.nn.sigmoid(x)

def _layernorm(x, axis=-1, eps=1e-05):
    m = jnp.mean(x, axis=axis, keepdims=True)
    v = jnp.var(x, axis=axis, keepdims=True)
    return (x - m) / jnp.sqrt(v + eps)

def _scatter_add(tgt, idx, src, axis=0):
    return tgt.at[idx].add(src)

def _segment_sum(src, seg, n):
    return jax.ops.segment_sum(src, seg, n)
kernel_name = 'mk_decoder_postln_d1_seqx_r2_b32174'

def setup_inputs(seed: int=0):
    np.random.seed(seed)
    _w = jnp.asarray

    def _rec_inputs():
        import jax
        import jax.numpy as jnp
        _rk = jax.random.key(seed)
        x = -0.0003929 + 0.9999 * jax.random.normal(jax.random.fold_in(_rk, 1), (4, 1024, 512), jnp.float32)
        _lenS = 1024 - jax.random.randint(jax.random.fold_in(_rk, 7), (4,), 0, max(1, 1024 // 4) + 1, jnp.int32)
        _lenS2 = 1024 - jax.random.randint(jax.random.fold_in(_rk, 8), (4,), 0, max(1, 1024 // 4) + 1, jnp.int32)
        _ctx_1024P = jax.random.normal(jax.random.fold_in(_rk, 11), (4, 16, 512), jnp.float32)
        _ctx_1024c = jax.random.dirichlet(jax.random.fold_in(_rk, 511), 0.3 * jnp.ones((16,), jnp.float32), (4, 1024))
        _ctx_1024t = jnp.einsum('bsk,bkd->bsd', _ctx_1024c, _ctx_1024P)
        _ctx_1024t = _ctx_1024t * jax.lax.rsqrt(jnp.mean(jnp.square(_ctx_1024t)) + 1e-12) * 0.953939
        ctx_1024 = 2.81802e-05 + 1.00001 * (_ctx_1024t + 0.3 * jax.random.normal(jax.random.fold_in(_rk, 611), (4, 1024, 512), jnp.float32))
        return (x, ctx_1024)
    x, ctx_1024 = _rec_inputs()

    def _L0_attn_setup():
        import jax, jax.numpy as jnp
        import numpy as np
        N_HEAD = 16
        N_FEAT = 512
        CONTEXT_SIZES = (21, 41)
        HEADS_PER_SCALE = N_HEAD // len(CONTEXT_SIZES)
        MAX_C = max(CONTEXT_SIZES)

        def _chunk(x, c):
            pad = (c - 1) // 2
            T = x.shape[1]
            xp = jnp.pad(x, ((0, 0), (pad, pad), (0, 0)))
            idx = jnp.arange(T)[:, None] + jnp.arange(c)[None, :]
            return xp[:, idx, :]
        key = jax.random.key(seed)
        ks = jax.random.split(key, 7)
        B, T, D = (2, 1024, N_FEAT)
        s = 1.0 / np.sqrt(D)
        return {'query': jax.random.normal(ks[0], (B, T, D), jnp.float32), 'key': jax.random.normal(ks[1], (B, T, D), jnp.float32), 'value': jax.random.normal(ks[2], (B, T, D), jnp.float32), 'W_in': jax.random.normal(ks[3], (D, D), jnp.float32) * s, 'W_attn': jax.random.normal(ks[4], (N_HEAD * MAX_C, D), jnp.float32) * s, 'W_out': jax.random.normal(ks[5], (D, D), jnp.float32) * s, 'scale_weights': jnp.ones((len(CONTEXT_SIZES),), jnp.float32) / len(CONTEXT_SIZES)}
    _L0_attn_all = _L0_attn_setup()
    _L0_attn_in = {k: v for k, v in _L0_attn_all.items() if k in ('key', 'value', 'W_in', 'W_attn', 'W_out', 'scale_weights')}
    del _L0_attn_all

    def _L0_xattn_setup():
        import jax, jax.numpy as jnp
        import numpy as np
        B, L, D = (4, 2048, 512)
        key = jax.random.key(seed)
        k1, k2 = jax.random.split(key)
        Q = jax.random.normal(k1, (B, L, D), dtype=jnp.float32)
        K = jax.random.normal(k2, (B, L, D), dtype=jnp.float32)
        return {'Q': Q, 'K': K}
    _L0_xattn_all = _L0_xattn_setup()
    _L0_xattn_in = {k: v for k, v in _L0_xattn_all.items() if k in ()}
    del _L0_xattn_all

    def _L0_ffn_setup():
        import jax, jax.numpy as jnp
        import numpy as np
        D = 512
        E = 8
        key = jax.random.key(seed)
        ks = jax.random.split(key, 7)
        s = 1.0 / np.sqrt(D)
        x = jax.random.normal(ks[0], (4, 1024, D), dtype=jnp.float32)
        Wg = jax.random.uniform(ks[1], (D, E), minval=-s, maxval=s, dtype=jnp.float32)
        bg = jax.random.uniform(ks[2], (E,), minval=-s, maxval=s, dtype=jnp.float32)
        W1 = jax.random.uniform(ks[3], (E, D, D), minval=-s, maxval=s, dtype=jnp.float32)
        b1 = jax.random.uniform(ks[4], (E, D), minval=-s, maxval=s, dtype=jnp.float32)
        W2 = jax.random.uniform(ks[5], (E, D, D), minval=-s, maxval=s, dtype=jnp.float32)
        b2 = jax.random.uniform(ks[6], (E, D), minval=-s, maxval=s, dtype=jnp.float32)
        return {'x': x, 'Wg': Wg, 'bg': bg, 'W1': W1, 'b1': b1, 'W2': W2, 'b2': b2}
    _L0_ffn_all = _L0_ffn_setup()
    _L0_ffn_in = {k: v for k, v in _L0_ffn_all.items() if k in ('Wg', 'bg', 'W1', 'b1', 'W2', 'b2')}
    del _L0_ffn_all
    return {'x': x, 'ctx_1024': ctx_1024, 'L0_attn_key': _L0_attn_in['key'], 'L0_attn_value': _L0_attn_in['value'], 'L0_attn_W_in': _L0_attn_in['W_in'], 'L0_attn_W_attn': _L0_attn_in['W_attn'], 'L0_attn_W_out': _L0_attn_in['W_out'], 'L0_attn_scale_weights': _L0_attn_in['scale_weights'], 'L0_ffn_Wg': _L0_ffn_in['Wg'], 'L0_ffn_bg': _L0_ffn_in['bg'], 'L0_ffn_W1': _L0_ffn_in['W1'], 'L0_ffn_b1': _L0_ffn_in['b1'], 'L0_ffn_W2': _L0_ffn_in['W2'], 'L0_ffn_b2': _L0_ffn_in['b2']}

def reference(x, ctx_1024, L0_attn_key, L0_attn_value, L0_attn_W_in, L0_attn_W_attn, L0_attn_W_out, L0_attn_scale_weights, L0_ffn_Wg, L0_ffn_bg, L0_ffn_W1, L0_ffn_b1, L0_ffn_W2, L0_ffn_b2):
    import jax
    import jax.numpy as jnp

    def _L0_attn_ref(query, key, value, W_in, W_attn, W_out, scale_weights):
        import jax, jax.numpy as jnp
        import numpy as np
        N_HEAD = 16
        N_FEAT = 512
        CONTEXT_SIZES = (21, 41)
        HEADS_PER_SCALE = N_HEAD // len(CONTEXT_SIZES)
        MAX_C = max(CONTEXT_SIZES)

        def _chunk(x, c):
            pad = (c - 1) // 2
            T = x.shape[1]
            xp = jnp.pad(x, ((0, 0), (pad, pad), (0, 0)))
            idx = jnp.arange(T)[:, None] + jnp.arange(c)[None, :]
            return xp[:, idx, :]
        B, T, D = query.shape
        x = jnp.einsum('btd,ed->bte', query, W_in)
        attn = jnp.einsum('btd,ed->bte', jax.nn.relu(x), W_attn)
        sw = jax.nn.softmax(scale_weights)
        out = jnp.zeros_like(query)
        for i, c in enumerate(CONTEXT_SIZES):
            sh = i * HEADS_PER_SCALE
            eh = sh + HEADS_PER_SCALE
            w = attn[:, :, sh * c:eh * c].reshape(B, T, HEADS_PER_SCALE, c)
            w = jax.nn.softmax(w, axis=-1)
            hd = D // HEADS_PER_SCALE
            xc = _chunk(x, c).reshape(B, T, c, HEADS_PER_SCALE, hd)
            out_i = jnp.einsum('bthc,btchd->bthd', w, xc).reshape(B, T, D)
            out = out + sw[i] * out_i
        return jnp.einsum('btd,ed->bte', out, W_out)

    def _L0_xattn_ref(Q, K):
        import jax, jax.numpy as jnp
        import numpy as np
        B, L, D = (4, 2048, 512)
        scores = jnp.einsum('btd,bsd->bts', K, K)
        Lq = Q.shape[1]
        mask = jnp.tril(jnp.ones((Lq, Lq), dtype=scores.dtype))
        scores = scores * mask[None, :, :]
        Q_proj = jnp.einsum('bts,bsd->btd', scores, Q)
        return Q + Q_proj

    def _L0_ffn_ref(x, Wg, bg, W1, b1, W2, b2):
        import jax, jax.numpy as jnp
        import numpy as np
        D = 512
        E = 8
        N, T, d = x.shape
        x_flat = x.reshape(N * T, d)
        logits = x_flat @ Wg + bg
        probs = jax.nn.softmax(logits, axis=-1)
        assignments = jnp.argmax(probs, axis=-1)
        h = jnp.einsum('nd,edh->neh', x_flat, W1) + b1[None]
        h = jax.nn.gelu(h, approximate=False)
        eo = jnp.einsum('neh,ehd->ned', h, W2) + b2[None]
        selected = jnp.take_along_axis(eo, assignments[:, None, None], axis=1)[:, 0, :]
        w = jnp.take_along_axis(probs, assignments[:, None], axis=1)
        out = (w * selected).reshape(N, T, d)
        return out
    x = _layernorm(x + _L0_attn_ref(x, L0_attn_key, L0_attn_value, L0_attn_W_in, L0_attn_W_attn, L0_attn_W_out, L0_attn_scale_weights), axis=-1)
    x = _layernorm(x + _L0_xattn_ref(x, ctx_1024), axis=-1)
    x = _layernorm(x + _L0_ffn_ref(x, L0_ffn_Wg, L0_ffn_bg, L0_ffn_W1, L0_ffn_b1, L0_ffn_W2, L0_ffn_b2), axis=-1)
    return x

_drawn_inputs = setup_inputs


def setup_inputs(seed=0):
    import zlib

    import numpy as np

    out = dict(_drawn_inputs(seed))
    spreads = {'L0_attn_scale_weights': (0.5, 0.6)}
    factors = {'L0_ffn_bg': 5.442, 'L0_ffn_b1': 24.482, 'L0_ffn_b2': 8.0}
    for name, (base, spread) in spreads.items():
        noise = np.random.default_rng([zlib.crc32(name.encode()), seed]).standard_normal(out[name].shape)
        drawn = base * np.exp(spread * noise) if base else spread * noise
        out[name] = jnp.asarray(drawn.astype(out[name].dtype))
    for name, factor in factors.items():
        out[name] = (out[name] * factor).astype(out[name].dtype)
    return out
```

```python
from contextlib import ExitStack

import numpy as np
import concourse.bass as bass
from concourse import mybir

F32 = mybir.dt.float32
F16 = mybir.dt.float16
I32 = mybir.dt.int32
ALU = mybir.AluOpType
ACT = mybir.ActivationFunctionType
AX = mybir.AxisListType.X

P = 128
EPS = 1e-5
WEIGHT_SCALE = 64.0
SCORE_SCALE = 1.0 / 16.0
RING = 3


def decoder_layer(nc, x, xT, ctxT, winT, wattnT, woutT, scale_w, wg, bg, w1, b1, w2, b2, out):
    B, T, D = x.shape
    E = wg.shape[1]
    NT = T // P
    DC = D // P
    NTOK = B * T
    SIZES = (21, 41)
    HEADS = 8
    HD = D // HEADS
    C0, C1 = SIZES
    L0, L1 = HEADS * C0, HEADS * C1
    NL = L0 + L1
    L1_AT = HEADS * C1
    assert wattnT.shape[1] == 2 * HEADS * C1 and NT == 8 and DC == 4

    SIDE = 32
    BAND = P + 2 * SIDE
    SHIFT = SIDE - (C1 - 1) // 2
    BROW = HEADS * BAND
    SKEW = BROW + 1

    REGION = NTOK + P
    SLOTS = 5
    GROUPS = -(-(NTOK // P + E - 1) // SLOTS)
    PAGES = GROUPS * SLOTS
    TAB = PAGES + SLOTS
    ROWS = E * REGION + P
    ROWLEN = D + 4
    NO_TOKEN = 2 * NTOK

    skew_dram = nc.dram_tensor("skew_dram", (2, P * SKEW), F32, kind="Internal").ap()
    sorted_dram = nc.dram_tensor("sorted_dram", (ROWS, ROWLEN), F32, kind="Internal").ap()

    out_rows = out.rearrange("b t d -> (b t) d")

    ctx = ExitStack()
    with ctx:
        def sb(name, shape, dt, stack=ctx):
            return stack.enter_context(nc.sbuf_tensor(name, shape, dt))

        def sem(name):
            return ctx.enter_context(nc.semaphore(name))

        banks = [ctx.enter_context(nc.psum_tensor(f"bank{i}", [P, 512], F32)) for i in range(8)]

        ident = sb("ident", [P, P], F32)
        ident16 = sb("ident16", [P, P], F16)
        half_neg = sb("half_neg", [P, 1], F32)
        exp_tab = sb("exp_tab", [P, TAB], I32)
        row_tab = sb("row_tab", [P, TAB], I32)

        mix = ExitStack()
        with mix:
            def mb(name, shape, dt):
                return sb(name, shape, dt, mix)

            win = mb("win", [P, 2, DC, D], F16)
            wattn = mb("wattn", [P, 2, DC, NL], F16)
            wout = mb("wout", [P, 2, DC, D], F16)
            wg_sb = mb("wg_sb", [P, DC, E], F32)
            bg_sb = mb("bg_sb", [P, E], F32)
            sw_sb = mb("sw_sb", [P, 2], F32)
            sw_tmp = mb("sw_tmp", [P, 4], F32)
            XT = mb("XT", [P, 2, DC, T], F16)
            KT = mb("KT", [P, 2, DC, T], F16)
            stage = mb("stage", [P, 2, 1024], F32)
            xrow = mb("xrow", [P, 4, D], F32)
            xi = mb("xi", [P, NT, 2, D], F16)
            rT = mb("rT", [P, 2, DC, P], F16)
            ee = mb("ee", [P, NL], F32)
            mx = mb("mx", [P, 2, HEADS], F32)
            sm = mb("sm", [P, 2, HEADS], F32)
            t0 = mb("t0", [P, HEADS, C0], F32)
            wwin = mb("wwin", [P, 2, HEADS, C1], F32)
            band = mb("band", [P, 2, SIDE + BROW + SIDE], F32)
            xc = mb("xc", [2 * SIDE, 2, 2, D], F16)
            bt = mb("bt", [P, 2, HEADS, P], F16)
            bs = mb("bs", [2 * SIDE, 2, HEADS + 1, 2, SIDE], F16)
            oT = mb("oT", [P, 2, DC, P], F16)
            z = mb("z", [P, D], F32)
            st = mb("st", [P, 12], F32)
            y1 = mb("y1", [P, 4, D], F32)
            y1s = mb("y1s", [P, NT, 2, D], F16)
            NBLK = NT * (NT + 1) // 2
            PT = mb("PT", [P, 2, NBLK * P], F16)
            yrow = mb("yrow", [P, NT, ROWLEN], F32)
            yT = mb("yT", [P, DC, P], F32)
            lg = mb("lg", [P, NT, E], F32)
            rt1 = mb("rt1", [P, NT, E], F32)
            rt2 = mb("rt2", [P, NT, E], F32)
            onehot = mb("onehot", [P, NT, E], F16)
            cum = mb("cum", [P, NT + 1, E], F32)
            m8 = mb("m8", [P, 4, NT], F32)
            slot = mb("slot", [P, NT], I32)
            tokid = mb("tokid", [P, NT], F32)
            e_less = mb("e_less", [P, NT, E], F32)
            e_base = mb("e_base", [P, NT, E], F32)
            tri = mb("tri", [P, P], F16)
            ones = mb("ones", [P, P], F16)
            zrow = mb("zrow", [P, ROWLEN], F32)
            zband = mb("zband", [P, SKEW], F32)
            pad_idx = mb("pad_idx", [P, E], I32)
            pad_off = mb("pad_off", [P, E], F32)
            pages = mb("pages", [P, 4, E], F32)
            pages_i = mb("pages_i", [P, 2, E], I32)
            karr = mb("karr", [P, TAB], F32)
            passed = mb("passed", [P, 2, TAB, E], F32)
            tabf = mb("tabf", [P, 2, TAB], F32)

            passed_wait = sem("passed_wait")
            consts = sem("consts")
            consts_in = sem("consts_in")
            zero_out = sem("zero_out")
            stage_in = [sem("stage_in0"), sem("stage_in1")]
            split_h = sem("split_h")
            split_l = sem("split_l")
            x_in = [sem(f"x_in{i}") for i in range(4)]
            xi_ready = sem("xi_ready")
            xih_done = sem("xih_done")
            xil_done = sem("xil_done")
            xit_ready = sem("xit_ready")
            rth_done = sem("rth_done")
            rt_done = sem("rt_done")
            logits_ready = sem("logits_ready")
            lsub_done = sem("lsub_done")
            exp_done = sem("exp_done")
            inv_done = sem("inv_done")
            wsum_done = sem("wsum_done")
            skew_out = [sem("skew_out0"), sem("skew_out1")]
            band_in = [sem("band_in0"), sem("band_in1")]
            xc_done = sem("xc_done")
            outT_ready = sem("outT_ready")
            oth_done = sem("oth_done")
            otl_done = sem("otl_done")
            prod_ready = sem("prod_ready")
            z_done = sem("z_done")
            var_done = sem("var_done")
            rstd_done = sem("rstd_done")
            y1_done = sem("y1_done")
            y1h_done = sem("y1h_done")
            y1l_done = sem("y1l_done")
            masked = sem("masked")
            y2_done = sem("y2_done")
            ring_full = sem("ring_full")
            ring_h = sem("ring_h")
            ring_done = sem("ring_done")
            dve_chain = sem("dve_chain")
            pool_chain = sem("pool_chain")
            rlog_done = sem("rlog_done")
            rexp_done = sem("rexp_done")
            onehot_done = sem("onehot_done")
            slot_done = sem("slot_done")
            rows_out = sem("rows_out")
            tables_done = sem("tables_done")
            pads_out = sem("pads_out")

            def halves(buf, c, n, width):
                return [buf[:, k, c:c + n, 0:width] for k in range(2)]

            def w_piece(src, buf, c, cols, dst_cols):
                return (src, buf, c, cols, dst_cols)

            setup_pieces = []
            for c in range(0, DC, 2):
                setup_pieces.append(("w", winT, win, c, ((0, 0, D),)))
            for c in range(DC):
                setup_pieces.append(("t", xT, XT, c, None))
            for c in range(DC):
                setup_pieces.append(("t", ctxT, KT, c, None))
            for c in range(0, DC, 2):
                setup_pieces.append(("w", wattnT, wattn, c, ((0, 0, L0), (L1_AT, L0, L1))))
            for c in range(0, DC, 2):
                setup_pieces.append(("w", woutT, wout, c, ((0, 0, D),)))
            NSETUP = len(setup_pieces)
            batch_pieces = [("t", xT, XT, c, None) for c in range(DC)] + [("t", ctxT, KT, c, None) for c in range(DC)]
            NPIECE = len(batch_pieces)
            def piece_dmas(p):
                return len(p[4]) if p[0] == "w" else 1

            slot_count = [0, 0]
            piece_level = []
            for n, p in enumerate(setup_pieces):
                slot_count[n % 2] += 16 * piece_dmas(p)
                piece_level.append(slot_count[n % 2])
            SETUP_LEVEL = list(slot_count)
            assert NSETUP % 2 == 0 and NPIECE % 2 == 0

            def piece_views(p, n):
                kind, _, buf, c, cols = p
                if kind == "t":
                    return stage[:, n % 2, :], buf[:, 0, c, :], buf[:, 1, c, :], 1.0
                w = sum(x[2] for x in cols)
                return (stage[:, n % 2, 0:2 * w].rearrange("p (c n) -> p c n", c=2),
                        buf[:, 0, c:c + 2, :], buf[:, 1, c:c + 2, :], WEIGHT_SCALE)

            def at(b, per, k):
                return b * per + (max(k, 0) + 1)

            STEPS = NT + 6

            def alone(eng):
                eng.sem_inc(passed_wait, 1)

            def score_pieces(j):
                n = (NT - j) * P
                first = n - 512 if n > 512 else n
                return [(0, first)] + ([(first, 512)] if n > 512 else [])

            BAND_ITEMS = [("own", h, 4) for h in range(0, HEADS, 4)] + [("sides", j, min(4, HEADS + 1 - j)) for j in range(0, HEADS + 1, 4)]

            def band_views(n, bank):
                kind, j0, k = BAND_ITEMS[n]
                blocks = bank[:, 0:k * P].rearrange("p (j t) -> p j t", j=k)
                if kind == "own":
                    return [blocks] + [bt[:, a, j0:j0 + k, :] for a in range(2)]
                src = bank[0:2 * SIDE, 0:k * P].rearrange("p (j a t) -> p j a t", j=k, t=SIDE)[:, :, 0:4:3, :]
                return [src] + [bs[:, a, j0:j0 + k, :, :] for a in range(2)]

            def ring_of(s):
                items = []
                if 5 <= s < NT + 5:
                    items.append(("y2T", s - 5, 0))
                if s < NT:
                    items += [("scores", s, n) for n in range(len(score_pieces(s)))]
                if 2 <= s < NT + 2:
                    items += [("band", s - 2, n) for n in range(len(BAND_ITEMS))]
                if 5 <= s < NT + 5:
                    items.append(("gate", s - 5, 0))
                if s == STEPS - 1:
                    items.append(("rank", 0, 0))
                return items

            ORDER = [it for s in range(STEPS) for it in ring_of(s)]
            NUMBER = {it: n for n, it in enumerate(ORDER)}
            N_RING = len(ORDER)
            SPLIT = [it for it in ORDER if it[0] in ("scores", "band")]
            SPLIT_NUMBER = {it: n for n, it in enumerate(SPLIT)}
            N_SPLIT = len(SPLIT)
            BLK = [sum(NT - jj for jj in range(j)) for j in range(NT)]

            def ring_bank(it):
                return banks[3 + NUMBER[it] % RING] if it in NUMBER else None

            def pre(s):
                return [2 * (s - NT), 2 * (s - NT) + 1] if NT <= s < NT + 4 else []

            xi_bank, xit_bank, logit_bank, outT_bank, prod_bank = banks[0], banks[1], banks[2], banks[6], banks[7]
            xit = xit_bank[:, :].bitcast(F16).rearrange("p (k c t) -> p k c t", k=2, c=DC)
            outT = outT_bank[:, :].rearrange("p (c t) -> p c t", c=DC)

            def prods(s):
                return ([("mix", s - 4)] if 4 <= s < NT + 4 else []) + ([("wout", s - 2)] if 2 <= s < NT + 2 else [])

            PRODS = [p for s in range(STEPS) for p in prods(s)]
            PROD_NUMBER = {p: n for n, p in enumerate(PRODS)}
            N_PROD = len(PRODS)

            DVE_SETUP, DVE_PER = 5, 100
            POOL_PER = 8

            block = mix.enter_context(nc.Block())

            @block.sync
            def _(sp):
                def load(p, n, b):
                    kind, src, _, c, cols = p
                    if kind == "t":
                        flat = src.rearrange("b d t -> (b d) t")
                        row0 = b * D + c * P
                        sp.dma_start(stage[:, n % 2, :], flat[bass.ds(row0, P), :]).then_inc(stage_in[n % 2], 16)
                    else:
                        w = sum(x[2] for x in cols)
                        dst = stage[:, n % 2, 0:2 * w].rearrange("p (c n) -> p c n", c=2)
                        for s0, d0, k in cols:
                            sp.dma_start(dst[:, :, d0:d0 + k],
                                         src[c * P:(c + 2) * P, s0:s0 + k].rearrange("(c p) n -> p c n", p=P)
                                         ).then_inc(stage_in[n % 2], 16)

                sp.dma_start(sw_sb[:, :], scale_w.rearrange("(a n) -> a n", a=1).broadcast_to([P, 2])).then_inc(consts_in, 16)
                sp.dma_start(bg_sb[:, :], bg.rearrange("(a n) -> a n", a=1).broadcast_to([P, E])).then_inc(consts_in, 16)
                sp.dma_start(wg_sb[:, :, :], wg.rearrange("(c p) e -> p c e", p=P)).then_inc(consts_in, 16)
                for n, p in enumerate(setup_pieces):
                    if n >= 2:
                        sp.wait_ge(split_l, n - 1)
                    load(p, n, 0)
                sp.wait_ge(consts, 1)
                for k in range(2):
                    sp.dma_start(skew_dram[k, :].rearrange("(p n) -> p n", p=P), zband[:, :]).then_inc(zero_out, 16)
                sp.dma_start(sorted_dram[E * REGION:ROWS, :], zrow[:, :]).then_inc(zero_out, 16)
                sp.wait_ge(zero_out, 48)
                with sp.Fori(0, B) as b:
                    for s in range(STEPS):
                        if s < NT:
                            i = s
                            sp.wait_ge(z_done, at(b, N_PROD, PROD_NUMBER[("wout", i - 4)] + 1 if i >= 4 else 0))
                            sp.dma_start(xrow[:, i % 4, :],
                                         x.rearrange("b t d -> (b t) d")[bass.ds(b * T + i * P, P), :]
                                         ).then_inc(x_in[i % 4], 16)
                            sp.wait_ge(wsum_done, at(b, NT, i + 1))
                            alone(sp)
                            if i >= 2:
                                sp.wait_ge(band_in[i % 2], b * 64 + 16 * (i // 2))
                            else:
                                sp.wait_ge(outT_ready, at(b, NT, 0))
                            rows = skew_dram[i % 2, :].rearrange("(t n) -> t n", n=SKEW)[:, 0:BROW]
                            sp.dma_start(rows.rearrange("t (h n) -> t h n", h=HEADS)[:, :, SHIFT:SHIFT + C1],
                                         wwin[:, i % 2, :, :]).then_inc(skew_out[i % 2], 16)
                            sp.wait_ge(skew_out[i % 2], b * 64 + 16 * (i // 2 + 1))
                            sp.wait_ge(outT_ready, at(b, NT, i - 1))
                            flat = skew_dram[i % 2, 0:P * BROW].rearrange("(t n) -> t n", n=BROW)
                            sp.dma_start(band[:, i % 2, SIDE:SIDE + BROW], flat).then_inc(band_in[i % 2], 16)
                        for m in pre(s):
                            n = NSETUP + m
                            sp.wait_ge(split_l, b * NPIECE + (NSETUP + m - 1))
                            load(batch_pieces[m], n, (b + 1) % B)

            @block.scalar
            def _(act):
                def split_piece(p, n, level):
                    act.wait_ge(stage_in[n % 2], level)
                    src, hi, _, scale = piece_views(p, n)
                    nc.scalar.activation(hi, src, ACT.Copy, scale=scale).then_inc(split_h, 1)

                for s_ in (xih_done, rth_done, exp_done, oth_done, y1h_done, ring_h, rexp_done):
                    act.sem_inc(s_, 1)
                for n, p in enumerate(setup_pieces):
                    split_piece(p, n, piece_level[n])
                act.wait_ge(dve_chain, 2)
                nc.scalar.activation(sw_tmp[:, 2:4], sw_tmp[:, 0:2], ACT.Exp).then_inc(rexp_done, 1)
                with act.Fori(0, B) as b:
                    for s in range(STEPS):
                        if s < NT:
                            act.wait_ge(xi_ready, at(b, NT, s + 1))
                            nc.scalar.activation(xi[:, s, 0, :], xi_bank[:, :], ACT.Copy,
                                                 scale=1.0 / WEIGHT_SCALE).then_inc(xih_done, 1)
                            for n, (c0, w) in enumerate(score_pieces(s)):
                                it = ("scores", s, n)
                                act.wait_ge(ring_full, at(b, N_RING, NUMBER[it] + 1))
                                o = BLK[s] * P + c0
                                nc.scalar.activation(PT[:, 0, o:o + w], ring_bank(it)[:, 0:w], ACT.Copy,
                                                     scale=SCORE_SCALE).then_inc(ring_h, 1)
                            act.wait_ge(xit_ready, at(b, NT, s + 1))
                            nc.scalar.activation(rT[:, 0, :, :], xit[:, 0, :, :], ACT.Relu).then_inc(rth_done, 1)
                        if 2 <= s < NT + 2:
                            for n in range(len(BAND_ITEMS)):
                                it = ("band", s - 2, n)
                                act.wait_ge(ring_full, at(b, N_RING, NUMBER[it] + 1))
                                src, hi, _ = band_views(n, ring_bank(it))
                                nc.scalar.activation(hi, src, ACT.Copy).then_inc(ring_h, 1)
                        if s < NT:
                            act.wait_ge(lsub_done, at(b, 2 * NT, 2 * s + 2))
                            nc.scalar.activation(ee[:, :], ee[:, :], ACT.Exp,
                                                 scale=1.0 / WEIGHT_SCALE).then_inc(exp_done, 1)
                        if 2 <= s < NT + 2:
                            i = s - 2
                            act.wait_ge(outT_ready, at(b, NT, i + 1))
                            nc.scalar.activation(oT[:, 0, :, :], outT, ACT.Copy).then_inc(oth_done, 1)
                            act.wait_ge(y1_done, at(b, NT, i + 1))
                            nc.scalar.activation(y1s[:, i, 0, :], y1[:, i % 4, :], ACT.Copy).then_inc(y1h_done, 1)
                        for m in pre(s):
                            n = NSETUP + m
                            split_piece(batch_pieces[m], n, b * (8 * NPIECE) + (SETUP_LEVEL[m % 2] + 16 * (m // 2 + 1)))
                        if s == STEPS - 1:
                            act.wait_ge(rlog_done, at(b, 1, 1))
                            nc.scalar.activation(rt2[:, :, :], rt1[:, :, :], ACT.Exp).then_inc(rexp_done, 1)

            @block.tensor
            def _(pe):
                def split_product(dst, stat, mov, chunks, first=True, last=True):
                    n = 0
                    total = 3 * chunks
                    for c in range(chunks):
                        for a, m in ((0, 0), (0, 1), (1, 0)):
                            ins = nc.tensor.matmul(dst, stat(a, c), mov(m, c), start=(first and n == 0),
                                                   stop=(last and n == total - 1))
                            n += 1
                    return ins

                for s_ in (xi_ready, xit_ready, logits_ready, outT_ready, prod_ready, ring_full):
                    pe.sem_inc(s_, 1)

                with pe.Fori(0, B) as b:
                    def acquire(it):
                        pe.wait_ge(ring_done, at(b, N_RING, NUMBER[it] - RING + 1))
                        return ring_bank(it)

                    pe.wait_ge(consts, 3)
                    for s in range(STEPS):
                        if s < NT:
                            if s == 0:
                                pe.wait_ge(split_l, b * NPIECE + NSETUP)
                            pe.wait_ge(xil_done, at(b, NT, s))
                            split_product(xi_bank[:, :], lambda a, c: XT[:, a, c, s * P:(s + 1) * P],
                                          lambda m, c: win[:, m, c, :], DC).then_inc(xi_ready, 1)
                        if 5 <= s < NT + 5:
                            i = s - 5
                            pe.wait_ge(y2_done, at(b, NT, i + 1))
                            bank = acquire(("y2T", i, 0))
                            for c in range(DC):
                                ins = nc.tensor.transpose(bank[:, c * P:(c + 1) * P], yrow[:, i, c * P:(c + 1) * P], ident[:, :])
                            ins.then_inc(ring_full, 1)
                        if s < NT:
                            for n, (c0, w) in enumerate(score_pieces(s)):
                                bank = acquire(("scores", s, n))
                                t0_ = s * P + c0
                                split_product(bank[:, 0:w], lambda a, c: KT[:, a, c, s * P:(s + 1) * P],
                                              lambda m, c: KT[:, m, c, t0_:t0_ + w], DC).then_inc(ring_full, 1)
                            pe.wait_ge(xil_done, at(b, NT, s + 1))
                            pe.wait_ge(rt_done, at(b, NT, s))
                            for k in range(2):
                                for c in range(DC):
                                    ins = nc.tensor.transpose(xit[:, k, c, :], xi[:, s, k, c * P:(c + 1) * P], ident16[:, :])
                            ins.then_inc(xit_ready, 1)
                        if 2 <= s < NT + 2:
                            i = s - 2
                            pe.wait_ge(band_in[i % 2], b * 64 + 16 * (i // 2 + 1))
                            for n, (kind, j0, k) in enumerate(BAND_ITEMS):
                                bank = acquire(("band", i, n))
                                alone(pe)
                                for j in range(j0, j0 + k):
                                    o = (j - j0) * P
                                    if kind == "own":
                                        c0 = SIDE + j * BAND + SIDE
                                        ins = nc.tensor.transpose(bank[:, o:o + P], band[:, i % 2, c0:c0 + P], ident[:, :])
                                    else:
                                        c0 = j * BAND
                                        ins = nc.tensor.transpose(bank[0:2 * SIDE, o:o + P], band[:, i % 2, c0:c0 + 2 * SIDE], ident[:, :])
                                ins.then_inc(ring_full, 1)
                        if 5 <= s < NT + 5:
                            i = s - 5
                            pe.wait_ge(ring_done, at(b, N_RING, NUMBER[("y2T", i, 0)] + 1))
                            bank = acquire(("gate", i, 0))
                            for c in range(DC):
                                ins = nc.tensor.matmul(bank[:, 0:E], yT[:, c, :], wg_sb[:, c, :], start=(c == 0), stop=(c == DC - 1))
                            ins.then_inc(ring_full, 1)
                        if s < NT:
                            pe.wait_ge(rt_done, at(b, NT, s + 1))
                            pe.wait_ge(lsub_done, at(b, 2 * NT, 2 * s))
                            split_product(logit_bank[:, 0:NL], lambda a, c: rT[:, a, c, :],
                                          lambda m, c: wattn[:, m, c, :], DC).then_inc(logits_ready, 1)
                        if 2 <= s < NT + 2:
                            i = s - 2
                            pe.wait_ge(ring_done, at(b, N_RING, NUMBER[("band", i, len(BAND_ITEMS) - 1)] + 1))
                            pe.wait_ge(xc_done, at(b, NT, i + 1))
                            pe.wait_ge(otl_done, at(b, NT, i))

                            def side_cols(m, h):
                                flat = bs[:, m, :, :, :].rearrange("p j a t -> p (j a) t")
                                return flat[:, 2 * h:2 * h + 4:3, :]

                            for h in range(HEADS):
                                q = 64 * (h % 2)
                                dst = outT[q:q + HD, h // 2, :]
                                split_product(dst, lambda a, c: xi[:, i, a, h * HD:(h + 1) * HD],
                                              lambda m, c: bt[:, m, h, :], 1, last=False)
                                sides = dst.rearrange("p (a n) -> p a n", n=SIDE)[:, 0:4:3, :]
                                ins = split_product(sides, lambda a, c: xc[:, i % 2, a, h * HD:(h + 1) * HD],
                                                    lambda m, c: side_cols(m, h), 1, first=False)
                            ins.then_inc(outT_ready, 1)
                        for what, i in prods(s):
                            pe.wait_ge(z_done, at(b, N_PROD, PROD_NUMBER[(what, i)]))
                            if what == "mix":
                                pe.wait_ge(y1l_done, at(b, NT, i + 1))
                                pe.wait_ge(masked, at(b, NT, i + 1))
                                split_product(prod_bank[:, :],
                                              lambda a, j: PT[:, a, (BLK[j] + i - j) * P:(BLK[j] + i - j + 1) * P],
                                              lambda m, j: y1s[:, j, m, :], i + 1).then_inc(prod_ready, 1)
                            else:
                                pe.wait_ge(otl_done, at(b, NT, i + 1))
                                split_product(prod_bank[:, :], lambda a, c: oT[:, a, c, :],
                                              lambda m, c: wout[:, m, c, :], DC).then_inc(prod_ready, 1)
                        if s == STEPS - 1:
                            pe.wait_ge(onehot_done, at(b, 1, 1))
                            bank = acquire(("rank", 0, 0))
                            oh = onehot[:, :, :].rearrange("p i e -> p (i e)")
                            nc.tensor.matmul(bank[:, 0:NT * E], tri[:, :], oh, start=True, stop=True)
                            nc.tensor.matmul(bank[:, NT * E:2 * NT * E], ones[:, :], oh, start=True, stop=True).then_inc(ring_full, 1)

            @block.gpsimd
            def _(pool):
                for s_ in (wsum_done, rstd_done, masked):
                    pool.sem_inc(s_, 1)
                n_pool = [0]

                def link(ins, base=0):
                    n_pool[0] += 1
                    ins.then_inc(pool_chain, 1)
                    pool.wait_ge(pool_chain, base + n_pool[0])

                link(nc.gpsimd.memset(zrow[:, :], 0.0))
                nc.gpsimd.memset(zrow[:, D + 1:D + 2], float(NO_TOKEN))
                link(nc.gpsimd.memset(zband[:, :], 0.0))
                pool.sem_inc(consts, 1)
                link(nc.gpsimd.memset(ident[:, :], 0.0))
                link(nc.gpsimd.affine_select(out=ident[:, :], in_=ident[:, :], compare_op=ALU.not_equal, fill=1.0,
                                             base=0, pattern=[[-1, P]], channel_multiplier=1))
                nc.gpsimd.tensor_copy(ident16[:, :], ident[:, :])
                nc.gpsimd.memset(half_neg[:, :], -0.5)
                link(nc.gpsimd.memset(ones[:, :], 1.0))
                link(nc.gpsimd.affine_select(out=tri[:, :], in_=ones[:, :], compare_op=ALU.is_ge, fill=0.0,
                                             base=-1, pattern=[[1, P]], channel_multiplier=-1))
                pool.sem_inc(consts, 1)
                link(nc.gpsimd.memset(band[:, :, :], 0.0))
                link(nc.gpsimd.memset(xc[:, :, :, :], 0.0))
                pool.sem_inc(consts, 1)
                iota_kw = dict(allow_small_or_imprecise_dtypes=True)
                nc.gpsimd.iota(e_less[:, :, :], pattern=[[0, NT], [1, E]], base=-E, channel_multiplier=0, **iota_kw)
                nc.gpsimd.iota(e_base[:, :, :], pattern=[[0, NT], [REGION, E]], base=0, channel_multiplier=0, **iota_kw)
                nc.gpsimd.iota(pad_off[:, :], pattern=[[REGION, E]], base=0, channel_multiplier=1, **iota_kw)
                nc.gpsimd.iota(karr[:, :], pattern=[[1, TAB]], base=0, channel_multiplier=0, **iota_kw)
                nc.gpsimd.memset(cum[:, NT, :], 0.0)
                nc.gpsimd.memset(yrow[:, :, D:ROWLEN], 0.0)
                link(nc.gpsimd.iota(tokid[:, :], pattern=[[P, NT]], base=0, channel_multiplier=1, **iota_kw))
                pool.sem_inc(consts, 1)
                pool_setup = n_pool[0]

                with pool.Fori(0, B) as b:
                    n_pool[0] = 0
                    base = b * POOL_PER + pool_setup
                    for s in range(STEPS):
                        if s < NT:
                            pool.wait_ge(ring_done, at(b, N_RING, NUMBER[("scores", s, 0)] + 1))
                            alone(pool)
                            for k in range(2):
                                o = BLK[s] * P
                                ins = nc.gpsimd.affine_select(out=PT[:, k, o:o + P], in_=PT[:, k, o:o + P],
                                                              compare_op=ALU.is_ge, fill=0.0, base=0,
                                                              pattern=[[1, P]], channel_multiplier=-1)
                            ins.then_inc(masked, 1)
                        def rstd(what, i):
                            k = PROD_NUMBER[(what, i)]
                            pool.wait_ge(var_done, at(b, N_PROD, k + 1))
                            nc.gpsimd.tensor_tensor(st[:, 9:10], st[:, 8:9], half_neg[:, :], ALU.pow).then_inc(rstd_done, 1)

                        if 4 <= s < NT + 4:
                            rstd("mix", s - 4)
                        if s < NT:
                            i = s
                            pool.wait_ge(inv_done, at(b, NT, i + 1))
                            e0 = ee[:, 0:L0].rearrange("p (h c) -> p h c", h=HEADS)
                            e1 = ee[:, L0:NL].rearrange("p (h c) -> p h c", h=HEADS)
                            nc.gpsimd.tensor_tensor(t0[:, :, :], e0, sm[:, 0, :].unsqueeze(2).broadcast_to([P, HEADS, C0]), ALU.mult)
                            if i >= 2:
                                pool.wait_ge(skew_out[i % 2], b * 64 + 16 * (i // 2))
                            link(nc.gpsimd.tensor_tensor(wwin[:, i % 2, :, :], e1, sm[:, 1, :].unsqueeze(2).broadcast_to([P, HEADS, C1]), ALU.mult), base)
                            mid = wwin[:, i % 2, :, (C1 - C0) // 2:(C1 + C0) // 2]
                            nc.gpsimd.tensor_tensor(mid, mid, t0[:, :, :], ALU.add).then_inc(wsum_done, 1)
                        if 2 <= s < NT + 2:
                            rstd("wout", s - 2)
                        if s == STEPS - 1:
                            pool.wait_ge(slot_done, at(b, 1, 1))
                            alone(pool)
                            for i in range(NT):
                                nc.gpsimd.indirect_dma_start(out=sorted_dram, out_offset=bass.IndirectOffsetOnAxis(ap=slot[:, i:i + 1], axis=0),
                                                             in_=yrow[:, i, :], in_offset=None).then_inc(rows_out, 16)
                            pool.wait_ge(rows_out, b * (16 * NT) + 16 * NT)
                            alone(pool)
                    assert n_pool[0] == POOL_PER, n_pool[0]
                pool.wait_ge(tables_done, 1)
                for e in range(E):
                    nc.gpsimd.indirect_dma_start(out=sorted_dram, out_offset=bass.IndirectOffsetOnAxis(ap=pad_idx[:, e:e + 1], axis=0),
                                                 in_=zrow[:, :], in_offset=None).then_inc(pads_out, 16)
                pool.wait_ge(pads_out, 16 * E)

            @block.vector
            def _(dve):
                for s_ in (xil_done, xc_done, rt_done, lsub_done, inv_done, otl_done, z_done, var_done, y1_done, y1l_done,
                           y2_done, ring_done, rlog_done, onehot_done, slot_done):
                    dve.sem_inc(s_, 1)
                n_dve = [0]
                base = [0]

                def link(ins, own=False):
                    n_dve[0] += 1
                    ins.then_inc(dve_chain, 1)
                    dve.wait_ge(dve_chain, base[0] + n_dve[0])
                    if own:
                        alone(dve)

                def split_piece(p, n, k):
                    dve.wait_ge(split_h, k)
                    src, hi, lo, scale = piece_views(p, n)
                    nc.vector.scalar_tensor_tensor(out=lo, in0=src, scalar=scale, in1=hi, op0=ALU.mult,
                                                   op1=ALU.subtract).then_inc(split_l, 1)

                def invert(to, of):
                    return nc.vector.reciprocal(to, of)

                for n, p in enumerate(setup_pieces):
                    split_piece(p, n, n + 1)
                dve.wait_ge(consts_in, 48)
                dve.wait_ge(consts, 4)
                swm = st[:, 0:1]
                link(nc.vector.reduce_max(swm, sw_sb[:, :], axis=AX))
                link(nc.vector.tensor_scalar(sw_tmp[:, 0:2], sw_sb[:, :], swm, None, ALU.subtract))
                dve.wait_ge(rexp_done, 2)
                link(nc.vector.reduce_sum(st[:, 1:2], sw_tmp[:, 2:4], axis=AX))
                link(invert(st[:, 2:3], st[:, 1:2]))
                link(nc.vector.tensor_scalar(sw_sb[:, :], sw_tmp[:, 2:4], st[:, 2:3], None, ALU.mult))
                assert n_dve[0] == DVE_SETUP

                with dve.Fori(0, B) as b:
                    n_dve[0] = 0
                    base[0] = b * DVE_PER + DVE_SETUP

                    def normed(what, i, src, eps, to):
                        k = PROD_NUMBER[(what, i)]
                        dve.wait_ge(z_done, at(b, N_PROD, k + 1))
                        link(nc.vector.bn_stats(st[:, 0:6], src), own=True)
                        link(nc.vector.bn_aggr(st[:, 6:8], st[:, 0:6]))
                        nc.vector.tensor_scalar(st[:, 8:9], st[:, 7:8], eps, None, ALU.add).then_inc(var_done, 1)
                        dve.wait_ge(rstd_done, at(b, N_PROD, k + 1))
                        return nc.vector.tensor_scalar(to, src, st[:, 6:7], st[:, 9:10], ALU.subtract, ALU.mult)

                    for s in range(STEPS):
                        if s < NT:
                            dve.wait_ge(xih_done, at(b, NT, s + 1))
                            nc.vector.scalar_tensor_tensor(out=xi[:, s, 1, :], in0=xi_bank[:, :], scalar=1.0 / WEIGHT_SCALE,
                                                           in1=xi[:, s, 0, :], op0=ALU.mult, op1=ALU.subtract).then_inc(xil_done, 1)
                        if 2 <= s < NT + 2:
                            i = s - 2
                            dve.wait_ge(outT_ready, at(b, NT, i - 1))
                            dve.wait_ge(xil_done, at(b, NT, min(i + 2, NT)))
                            if i > 0:
                                link(nc.vector.tensor_copy(xc[SIDE:2 * SIDE, i % 2, :, :], xi[P - SIDE:P, i - 1, :, :]))
                            else:
                                link(nc.vector.tensor_scalar(xc[SIDE:2 * SIDE, i % 2, :, :], xi[P - SIDE:P, i, :, :], 0.0, None, ALU.mult))
                            if i < NT - 1:
                                ins = nc.vector.tensor_copy(xc[0:SIDE, i % 2, :, :], xi[0:SIDE, i + 1, :, :])
                            else:
                                ins = nc.vector.tensor_scalar(xc[0:SIDE, i % 2, :, :], xi[0:SIDE, i, :, :], 0.0, None, ALU.mult)
                            ins.then_inc(xc_done, 1)
                        if 5 <= s < NT + 5:
                            it = ("y2T", s - 5, 0)
                            dve.wait_ge(ring_full, at(b, N_RING, NUMBER[it] + 1))
                            nc.vector.tensor_copy(yT[:, :, :].rearrange("p c t -> p (c t)"), ring_bank(it)[:, :]).then_inc(ring_done, 1)
                        if s < NT:
                            for n, (c0, w) in enumerate(score_pieces(s)):
                                it = ("scores", s, n)
                                dve.wait_ge(ring_h, at(b, N_SPLIT, SPLIT_NUMBER[it] + 1))
                                o = BLK[s] * P + c0
                                nc.vector.scalar_tensor_tensor(out=PT[:, 1, o:o + w], in0=ring_bank(it)[:, 0:w], scalar=SCORE_SCALE,
                                                               in1=PT[:, 0, o:o + w], op0=ALU.mult, op1=ALU.subtract).then_inc(ring_done, 1)
                            dve.wait_ge(rth_done, at(b, NT, s + 1))
                            nc.vector.scalar_tensor_tensor(out=rT[:, 1, :, :], in0=rT[:, 0, :, :], scalar=0.0, in1=xit[:, 1, :, :],
                                                           op0=ALU.is_gt, op1=ALU.mult).then_inc(rt_done, 1)
                        if 2 <= s < NT + 2:
                            for n in range(len(BAND_ITEMS)):
                                it = ("band", s - 2, n)
                                dve.wait_ge(ring_h, at(b, N_SPLIT, SPLIT_NUMBER[it] + 1))
                                src, hi, lo = band_views(n, ring_bank(it))
                                nc.vector.tensor_tensor(lo, src, hi, ALU.subtract).then_inc(ring_done, 1)
                        if 5 <= s < NT + 5:
                            i = s - 5
                            it = ("gate", i, 0)
                            dve.wait_ge(ring_full, at(b, N_RING, NUMBER[it] + 1))
                            nc.vector.tensor_tensor(lg[:, i, :], ring_bank(it)[:, 0:E], bg_sb[:, :], ALU.add).then_inc(ring_done, 1)
                        if s < NT:
                            dve.wait_ge(logits_ready, at(b, NT, s + 1))
                            ls = [logit_bank[:, 0:L0].rearrange("p (h c) -> p h c", h=HEADS),
                                  logit_bank[:, L0:NL].rearrange("p (h c) -> p h c", h=HEADS)]
                            es = [ee[:, 0:L0].rearrange("p (h c) -> p h c", h=HEADS),
                                  ee[:, L0:NL].rearrange("p (h c) -> p h c", h=HEADS)]
                            for k in range(2):
                                link(nc.vector.reduce_max(mx[:, k, :], ls[k], axis=AX))
                            dve.wait_ge(wsum_done, at(b, NT, s))
                            for k in range(2):
                                nc.vector.tensor_tensor(es[k], ls[k], mx[:, k, :].unsqueeze(2).broadcast_to([P, HEADS, SIZES[k]]),
                                                        ALU.subtract).then_inc(lsub_done, 1)
                        if 2 <= s < NT + 2:
                            i = s - 2
                            dve.wait_ge(oth_done, at(b, NT, i + 1))
                            nc.vector.tensor_tensor(oT[:, 1, :, :], outT, oT[:, 0, :, :], ALU.subtract).then_inc(otl_done, 1)
                        if 4 <= s < NT + 4:
                            i = s - 4
                            dve.wait_ge(prod_ready, at(b, N_PROD, PROD_NUMBER[("mix", i)] + 1))
                            nc.vector.scalar_tensor_tensor(out=z[:, :], in0=prod_bank[:, :], scalar=0.5 / SCORE_SCALE, in1=y1[:, i % 4, :],
                                                           op0=ALU.mult, op1=ALU.add).then_inc(z_done, 1)
                            normed("mix", i, z[:, :], EPS / 4, yrow[:, i, 0:D]).then_inc(y2_done, 1)
                        if s < NT:
                            dve.wait_ge(exp_done, at(b, NT, s + 1))
                            for k in range(2):
                                link(nc.vector.reduce_sum(sm[:, k, :], es[k], axis=AX))
                            link(nc.vector.reciprocal(sm[:, :, :], sm[:, :, :]))
                            nc.vector.tensor_tensor(sm[:, :, :], sm[:, :, :], sw_sb[:, :].unsqueeze(2).broadcast_to([P, 2, HEADS]),
                                                    ALU.mult).then_inc(inv_done, 1)
                        if 2 <= s < NT + 2:
                            i = s - 2
                            dve.wait_ge(prod_ready, at(b, N_PROD, PROD_NUMBER[("wout", i)] + 1))
                            dve.wait_ge(x_in[i % 4], b * 32 + 16 * (i // 4 + 1))
                            dve.wait_ge(y2_done, at(b, NT, min(s - 3, NT)))
                            nc.vector.scalar_tensor_tensor(out=z[:, :], in0=prod_bank[:, :], scalar=1.0 / WEIGHT_SCALE, in1=xrow[:, i % 4, :],
                                                           op0=ALU.mult, op1=ALU.add).then_inc(z_done, 1)
                            normed("wout", i, z[:, :], EPS, y1[:, i % 4, :]).then_inc(y1_done, 1)
                            dve.wait_ge(y1_done, at(b, NT, i + 1))
                            dve.wait_ge(y1h_done, at(b, NT, i + 1))
                            nc.vector.tensor_tensor(y1s[:, i, 1, :], y1[:, i % 4, :], y1s[:, i, 0, :], ALU.subtract).then_inc(y1l_done, 1)
                        for m in pre(s):
                            split_piece(batch_pieces[m], NSETUP + m, b * NPIECE + (NSETUP + m + 1))

                    it = ("gate", NT - 1, 0)
                    dve.wait_ge(ring_done, at(b, N_RING, NUMBER[it] + 1))
                    top, den, km, pw = (m8[:, k, :] for k in range(4))

                    def over_e(a):
                        return a.unsqueeze(2).broadcast_to([P, NT, E])

                    link(nc.vector.reduce_max(top, lg[:, :, :], axis=AX))
                    nc.vector.tensor_tensor(rt1[:, :, :], lg[:, :, :], over_e(top), ALU.subtract).then_inc(rlog_done, 1)
                    dve.wait_ge(rexp_done, b + 3)
                    link(nc.vector.reduce_sum(den, rt2[:, :, :], axis=AX))
                    link(nc.vector.reciprocal(pw, den))
                    link(nc.vector.scalar_tensor_tensor(out=rt2[:, :, :], in0=rt1[:, :, :], scalar=0.0, in1=e_less[:, :, :],
                                                        op0=ALU.is_equal, op1=ALU.mult))
                    link(nc.vector.tensor_reduce(km, rt2[:, :, :], AX, ALU.min))
                    nc.vector.tensor_tensor(onehot[:, :, :], e_less[:, :, :], over_e(km), ALU.is_equal).then_inc(onehot_done, 1)
                    dve.wait_ge(onehot_done, at(b, 1, 1))
                    it = ("rank", 0, 0)
                    dve.wait_ge(ring_full, at(b, N_RING, NUMBER[it] + 1))
                    rk = ring_bank(it)[:, 0:NT * E].rearrange("p (i e) -> p i e", i=NT)
                    tot = ring_bank(it)[:, NT * E:2 * NT * E].rearrange("p (i e) -> p i e", i=NT)
                    link(nc.vector.tensor_copy(cum[:, 0, :], cum[:, NT, :]))
                    for i in range(NT):
                        link(nc.vector.tensor_tensor(cum[:, i + 1, :], cum[:, i, :], tot[:, i, :], ALU.add))
                    link(nc.vector.tensor_tensor(rt1[:, :, :], rk, cum[:, 0:NT, :], ALU.add))
                    nc.vector.tensor_tensor(rt2[:, :, :], rt1[:, :, :], e_base[:, :, :], ALU.add).then_inc(ring_done, 1)
                    dve.wait_ge(ring_done, at(b, N_RING, N_RING))
                    link(nc.vector.tensor_tensor(rt1[:, :, :], rt2[:, :, :], onehot[:, :, :], ALU.mult))
                    link(nc.vector.reduce_sum(den, rt1[:, :, :], axis=AX))
                    link(nc.vector.tensor_copy(slot[:, :], den))
                    link(nc.vector.tensor_copy(yrow[:, :, D:D + 1].rearrange("p i a -> p (i a)"), pw))
                    link(nc.vector.tensor_copy(yrow[:, :, D + 1:D + 2].rearrange("p i a -> p (i a)"), tokid[:, :]))
                    nc.vector.tensor_scalar(tokid[:, :], tokid[:, :], float(T), None, ALU.add).then_inc(slot_done, 1)
                    dve.wait_ge(rows_out, b * (16 * NT) + 16 * NT)
                    assert n_dve[0] == DVE_PER, n_dve[0]

                n_dve[0] = 0
                base[0] = B * DVE_PER + DVE_SETUP
                cnt = cum[:, NT, :]
                link(nc.vector.tensor_tensor(pages[:, 0, :], cnt, pad_off[:, :], ALU.add))
                link(nc.vector.tensor_copy(pad_idx[:, :], pages[:, 0, :]))
                link(nc.vector.tensor_scalar(pages[:, 1, :], cnt, float(P - 1), None, ALU.add))
                link(nc.vector.tensor_copy(pages_i[:, 0, :], pages[:, 1, :]))
                link(nc.vector.tensor_scalar(pages_i[:, 1, :], pages_i[:, 0, :], 7, None, ALU.arith_shift_right))
                link(nc.vector.tensor_copy(pages[:, 0, :], pages_i[:, 1, :]))
                link(nc.vector.tensor_copy(pages[:, 2, 0:1], pages[:, 0, 0:1]))
                for e in range(1, E):
                    link(nc.vector.tensor_tensor(pages[:, 2, e:e + 1], pages[:, 2, e - 1:e], pages[:, 0, e:e + 1], ALU.add))
                link(nc.vector.tensor_scalar(pages[:, 3, :], pages[:, 0, :], -float(P), float(REGION), ALU.mult, ALU.add))
                full = [P, TAB, E]
                link(nc.vector.tensor_tensor(passed[:, 0, :, :], karr[:, :].unsqueeze(2).broadcast_to(full),
                                             pages[:, 2, :].unsqueeze(1).broadcast_to(full), ALU.is_ge))
                link(nc.vector.tensor_tensor(passed[:, 1, :, :], passed[:, 0, :, :],
                                             pages[:, 3, :].unsqueeze(1).broadcast_to(full), ALU.mult))
                link(nc.vector.reduce_sum(tabf[:, 0, :], passed[:, 0, :, :], axis=AX))
                link(nc.vector.tensor_scalar(exp_tab[:, :], tabf[:, 0, :], float(E - 1), None, ALU.min))
                link(nc.vector.reduce_sum(tabf[:, 1, :], passed[:, 1, :, :], axis=AX))
                link(nc.vector.scalar_tensor_tensor(out=tabf[:, 0, :], in0=karr[:, :], scalar=float(P), in1=tabf[:, 1, :],
                                                    op0=ALU.mult, op1=ALU.add))
                nc.vector.tensor_scalar(row_tab[:, :], tabf[:, 0, :], float(E * REGION), None, ALU.min).then_inc(tables_done, 1)
                dve.wait_ge(tables_done, 1)

            mix.pop_all().close()

        ffn = ExitStack()
        with ffn:
            def fb(name, shape, dt):
                return sb(name, shape, dt, ffn)

            WCOLS = DC * D
            w1s = fb("w1s", [P, 2, E * WCOLS], F16)
            w2s = fb("w2s", [P, 2, E * WCOLS], F16)
            b1s = fb("b1s", [P, E * D], F32)
            b2s = fb("b2s", [P, E * D], F32)
            HALF = WCOLS // 2
            fstage = fb("fstage", [P, 2, HALF], F32)
            page = fb("page", [P, SLOTS, ROWLEN], F32)
            pT = fb("pT", [P, SLOTS, 2, D], F16)
            hpre = fb("hpre", [P, D], F32)
            hact = fb("hact", [P, D], F32)
            hT = fb("hT", [P, 2, D], F16)
            t2 = fb("t2", [P, D], F32)
            z3 = fb("z3", [P, D], F32)
            st3 = fb("st3", [P, 12], F32)
            idx = fb("idx", [P, SLOTS], I32)

            bias_in = sem("bias_in")
            fstage_in = [sem("fstage_in0"), sem("fstage_in1")]
            wsplit_h = sem("wsplit_h")
            wsplit_l = sem("wsplit_l")
            page_in = [sem(f"page_in{i}") for i in range(SLOTS)]
            pT_ready = sem("pT_ready")
            pTh_done = sem("pTh_done")
            pTl_done = sem("pTl_done")
            h_ready = sem("h_ready")
            hpre_done = sem("hpre_done")
            gelu_done = sem("gelu_done")
            hT_ready = sem("hT_ready")
            hTh_done = sem("hTh_done")
            hTl_done = sem("hTl_done")
            o_ready = sem("o_ready")
            o_read = sem("o_read")
            fvar_done = sem("fvar_done")
            frstd_done = sem("frstd_done")
            y3_done = sem("y3_done")
            f_chain = sem("f_chain")
            out_done = [sem(f"out_done{i}") for i in range(SLOTS)]

            pT_bank, h_bank, hT_bank, o_bank = banks[0], banks[1], banks[2], banks[3]
            wpieces = []
            for e in range(E):
                for src, dst in ((w1, w1s), (w2, w2s)):
                    for k in range(2):
                        wpieces.append((src, dst, e, k))
            F_PER = SLOTS * 4

            block = ffn.enter_context(nc.Block())

            @block.sync
            def _(sp):
                sp.dma_start(b1s[:, :], b1.rearrange("(a e) n -> a (e n)", a=1).broadcast_to([P, E * D])).then_inc(bias_in, 16)
                sp.dma_start(b2s[:, :], b2.rearrange("(a e) n -> a (e n)", a=1).broadcast_to([P, E * D])).then_inc(bias_in, 16)
                for n, (src, dst, e, k) in enumerate(wpieces):
                    if n >= 2:
                        sp.wait_ge(wsplit_l, n - 1)
                    sp.dma_start(fstage[:, n % 2, :].rearrange("p (c n) -> p c n", c=DC // 2),
                                 src[e, k * (D // 2):(k + 1) * (D // 2), :].rearrange("(c p) n -> p c n", p=P)
                                 ).then_inc(fstage_in[n % 2], 16)

                def load(k, u):
                    row = sp.value_load(row_tab[0:1, bass.ds(k, 1)], min_val=0, max_val=ROWS - P)
                    sp.dma_start(page[:, u, :], sorted_dram[bass.ds(row, P), :]).then_inc(page_in[u], 16)

                for k in range(SLOTS):
                    load(k, k)
                with sp.Fori(0, GROUPS) as g:
                    for u in range(SLOTS):
                        sp.wait_ge(out_done[u], g * 16 + 16)
                        alone(sp)
                        load(g * SLOTS + (u + SLOTS), u)
                for u in range(SLOTS):
                    sp.wait_ge(page_in[u], 16 * (GROUPS + 1))

            @block.scalar
            def _(act):
                for n, (src, dst, e, k) in enumerate(wpieces):
                    act.wait_ge(fstage_in[n % 2], 16 * (n // 2 + 1))
                    o = e * WCOLS + k * HALF
                    nc.scalar.activation(dst[:, 0, o:o + HALF], fstage[:, n % 2, :], ACT.Copy, scale=WEIGHT_SCALE).then_inc(wsplit_h, 1)

                def pT_high(k, u):
                    act.wait_ge(pT_ready, k + 1)
                    nc.scalar.activation(pT[:, u, 0, :], pT_bank[:, :], ACT.Copy).then_inc(pTh_done, 1)

                def gelu(k):
                    act.wait_ge(hpre_done, k + 1)
                    nc.scalar.activation(hact[:, :], hpre[:, :], ACT.Gelu).then_inc(gelu_done, 1)

                pT_high(0, 0)
                pT_high(1, 1)
                gelu(0)
                with act.Fori(0, GROUPS) as g:
                    for u in range(SLOTS):
                        k = g * SLOTS + u
                        pT_high(g * SLOTS + (u + 2), (u + 2) % SLOTS)
                        act.wait_ge(hT_ready, k + 1)
                        nc.scalar.activation(hT[:, 0, :], hT_bank[:, :], ACT.Copy).then_inc(hTh_done, 1)
                        gelu(g * SLOTS + (u + 1))

            @block.tensor
            def _(pe):
                def transposes(bank, src, signal):
                    for c in range(DC):
                        ins = nc.tensor.transpose(bank[:, c * P:(c + 1) * P], src[:, c * P:(c + 1) * P], ident[:, :])
                    ins.then_inc(signal, 1)

                def product(bank, stat, w, k):
                    alone(pe)
                    e = pe.value_load(exp_tab[0:1, bass.ds(k, 1)], min_val=0, max_val=E - 1)
                    col = pe.snap(e * WCOLS)
                    n = 0
                    for c in range(DC):
                        for a, m in ((0, 0), (0, 1), (1, 0)):
                            ins = nc.tensor.matmul(bank[:, :], stat(a, c), w[:, m, bass.ds(col + c * D, D)],
                                                   start=(n == 0), stop=(n == 3 * DC - 1))
                            n += 1
                    return ins

                def first(k, u):
                    pe.wait_ge(pTl_done, k + 1)
                    if not isinstance(k, int) or k > 0:
                        pe.wait_ge(hpre_done, k)
                    product(h_bank, lambda a, c: pT[:, u, a, c * P:(c + 1) * P], w1s, k).then_inc(h_ready, 1)

                pe.wait_ge(page_in[0], 16)
                transposes(pT_bank, page[:, 0, :], pT_ready)
                pe.wait_ge(pTl_done, 1)
                pe.wait_ge(page_in[1], 16)
                transposes(pT_bank, page[:, 1, :], pT_ready)
                pe.wait_ge(wsplit_l, len(wpieces))
                first(0, 0)
                with pe.Fori(0, GROUPS) as g:
                    for u in range(SLOTS):
                        k = g * SLOTS + u
                        v = (u + 2) % SLOTS
                        pe.wait_ge(page_in[v], g * 16 + (16 if u + 2 < SLOTS else 32))
                        pe.wait_ge(pTl_done, g * SLOTS + (u + 2))
                        transposes(pT_bank, page[:, v, :], pT_ready)
                        pe.wait_ge(gelu_done, g * SLOTS + (u + 1))
                        transposes(hT_bank, hact, hT_ready)
                        first(g * SLOTS + (u + 1), (u + 1) % SLOTS)
                        pe.wait_ge(hTl_done, g * SLOTS + (u + 1))
                        product(o_bank, lambda a, c: hT[:, a, c * P:(c + 1) * P], w2s, k).then_inc(o_ready, 1)

            @block.gpsimd
            def _(pool):
                with pool.Fori(0, GROUPS) as g:
                    for u in range(SLOTS):
                        pool.wait_ge(fvar_done, g * SLOTS + (u + 1))
                        nc.gpsimd.tensor_tensor(st3[:, 9:10], st3[:, 8:9], half_neg[:, :], ALU.pow).then_inc(frstd_done, 1)
                        pool.wait_ge(y3_done, g * SLOTS + (u + 1))
                        alone(pool)
                        nc.gpsimd.indirect_dma_start(out=out_rows, out_offset=bass.IndirectOffsetOnAxis(ap=idx[:, u:u + 1], axis=0),
                                                     in_=page[:, u, 0:D], in_offset=None, bounds_check=NTOK - 1,
                                                     oob_is_err=False).then_inc(out_done[u], 16)
                for u in range(SLOTS):
                    pool.wait_ge(out_done[u], 16 * GROUPS)

            @block.vector
            def _(dve):
                for n, (src, dst, e, k) in enumerate(wpieces):
                    dve.wait_ge(wsplit_h, n + 1)
                    o = e * WCOLS + k * HALF
                    nc.vector.scalar_tensor_tensor(out=dst[:, 1, o:o + HALF], in0=fstage[:, n % 2, :], scalar=WEIGHT_SCALE,
                                                   in1=dst[:, 0, o:o + HALF], op0=ALU.mult, op1=ALU.subtract).then_inc(wsplit_l, 1)
                dve.wait_ge(bias_in, 32)

                def expert(k):
                    e = dve.value_load(exp_tab[0:1, bass.ds(k, 1)], min_val=0, max_val=E - 1)
                    return dve.snap(e * D)

                def pT_low(k, u):
                    dve.wait_ge(pTh_done, k + 1)
                    nc.vector.tensor_tensor(pT[:, u, 1, :], pT_bank[:, :], pT[:, u, 0, :], ALU.subtract).then_inc(pTl_done, 1)

                def hidden(k):
                    col = expert(k)
                    dve.wait_ge(h_ready, k + 1)
                    nc.vector.scalar_tensor_tensor(out=hpre[:, :], in0=h_bank[:, :], scalar=1.0 / WEIGHT_SCALE,
                                                   in1=b1s[:, bass.ds(col, D)], op0=ALU.mult, op1=ALU.add).then_inc(hpre_done, 1)

                pT_low(0, 0)
                pT_low(1, 1)
                hidden(0)
                with dve.Fori(0, GROUPS) as g:
                    n_f = [0]

                    def link(ins, own=False):
                        n_f[0] += 1
                        ins.then_inc(f_chain, 1)
                        dve.wait_ge(f_chain, g * F_PER + n_f[0])
                        if own:
                            alone(dve)

                    def finish(g, u):
                        dve.wait_ge(frstd_done, g * SLOTS + (u + 1))
                        nc.vector.tensor_scalar(page[:, u, 0:D], z3[:, :], st3[:, 6:7], st3[:, 9:10], ALU.subtract, ALU.mult).then_inc(y3_done, 1)
                        dve.wait_ge(y3_done, g * SLOTS + (u + 1))

                    for u in range(SLOTS):
                        k = g * SLOTS + u
                        pT_low(g * SLOTS + (u + 2), (u + 2) % SLOTS)
                        dve.wait_ge(hTh_done, g * SLOTS + (u + 1))
                        nc.vector.tensor_tensor(hT[:, 1, :], hT_bank[:, :], hT[:, 0, :], ALU.subtract).then_inc(hTl_done, 1)
                        if u > 0:
                            finish(g, u - 1)
                        hidden(g * SLOTS + (u + 1))
                        col = expert(k)
                        dve.wait_ge(o_ready, g * SLOTS + (u + 1))
                        nc.vector.scalar_tensor_tensor(out=t2[:, :], in0=o_bank[:, :], scalar=1.0 / WEIGHT_SCALE,
                                                       in1=b2s[:, bass.ds(col, D)], op0=ALU.mult, op1=ALU.add).then_inc(o_read, 1)
                        dve.wait_ge(o_read, g * SLOTS + (u + 1))
                        link(nc.vector.scalar_tensor_tensor(out=z3[:, :], in0=t2[:, :], scalar=page[:, u, D:D + 1],
                                                            in1=page[:, u, 0:D], op0=ALU.mult, op1=ALU.add))
                        link(nc.vector.bn_stats(st3[:, 0:6], z3[:, :]), own=True)
                        link(nc.vector.bn_aggr(st3[:, 6:8], st3[:, 0:6]))
                        nc.vector.tensor_scalar(st3[:, 8:9], st3[:, 7:8], EPS, None, ALU.add).then_inc(fvar_done, 1)
                        link(nc.vector.tensor_copy(idx[:, u:u + 1], page[:, u, D + 1:D + 2]))
                        if u == SLOTS - 1:
                            finish(g, u)
                    assert n_f[0] == F_PER, n_f[0]


def kernel(**inputs):
    import numpy as _np
    import concourse.bacc as _bacc
    from concourse import mybir as _mybir
    from concourse.bass_utils import run_bass_kernel_spmd as _run

    a = {k: _np.asarray(v) for k, v in inputs.items()}
    given = {
        "x": a["x"],
        "xT": a["x"].transpose(0, 2, 1),
        "ctxT": a["ctx_1024"].transpose(0, 2, 1),
        "winT": a["L0_attn_W_in"].T,
        "wattnT": a["L0_attn_W_attn"].T,
        "woutT": a["L0_attn_W_out"].T,
        "scale_w": a["L0_attn_scale_weights"],
        "wg": a["L0_ffn_Wg"],
        "bg": a["L0_ffn_bg"],
        "w1": a["L0_ffn_W1"],
        "b1": a["L0_ffn_b1"],
        "w2": a["L0_ffn_W2"],
        "b2": a["L0_ffn_b2"],
    }
    nc = _bacc.Bacc("TRN2", target_bir_lowering=False, num_devices=1)
    arrays, args = {}, []
    for name, v in given.items():
        v = _np.ascontiguousarray(v)
        arrays[f"in_{name}"] = v
        args.append(nc.dram_tensor(f"in_{name}", v.shape, _mybir.dt.from_np(v.dtype), kind="ExternalInput").ap())
    args.append(nc.dram_tensor("out", a["x"].shape, _mybir.dt.from_np(_np.dtype("float32")), kind="ExternalOutput").ap())
    decoder_layer(nc, *args)
    r = _run(nc, [arrays], core_ids=[0])
    return r.results[0]["out"]
```

```python
from contextlib import ExitStack

import numpy as np
import concourse.bass as bass
from concourse import mybir

F32 = mybir.dt.float32
F16 = mybir.dt.float16
I32 = mybir.dt.int32
ALU = mybir.AluOpType
ACT = mybir.ActivationFunctionType
AX = mybir.AxisListType.X

P = 128
EPS = 1e-5
WEIGHT_SCALE = 64.0
SCORE_SCALE = 1.0 / 16.0
RING = 3


def decoder_layer(nc, x, xT, ctxT, winT, wattnT, woutT, scale_w, wg, bg, w1, b1, w2, b2, out):
    B, T, D = x.shape
    E = wg.shape[1]
    NT = T // P
    DC = D // P
    NTOK = B * T
    SIZES = (21, 41)
    HEADS = 8
    HD = D // HEADS
    C0, C1 = SIZES
    L0, L1 = HEADS * C0, HEADS * C1
    NL = L0 + L1
    L1_AT = HEADS * C1
    assert wattnT.shape[1] == 2 * HEADS * C1 and NT == 8 and DC == 4

    SIDE = 32
    BAND = P + 2 * SIDE
    SHIFT = SIDE - (C1 - 1) // 2
    BROW = HEADS * BAND
    SKEW = BROW + 1

    REGION = NTOK + P
    SLOTS = 5
    GROUPS = -(-(NTOK // P + E - 1) // SLOTS)
    PAGES = GROUPS * SLOTS
    TAB = PAGES + SLOTS
    ROWS = E * REGION + P
    ROWLEN = D + 4
    NO_TOKEN = 2 * NTOK

    skew_dram = nc.dram_tensor("skew_dram", (2, P * SKEW), F32, kind="Internal").ap()
    sorted_dram = nc.dram_tensor("sorted_dram", (ROWS, ROWLEN), F32, kind="Internal").ap()

    wsplit_dram = nc.dram_tensor("wsplit_dram", (E, DC, P, 4 * D), F16, kind="Internal").ap()
    wsplit_rows = wsplit_dram.rearrange("e c p n -> (e c p) n")

    out_rows = out.rearrange("b t d -> (b t) d")

    ctx = ExitStack()
    with ctx:
        def sb(name, shape, dt, stack=ctx):
            return stack.enter_context(nc.sbuf_tensor(name, shape, dt))

        def sem(name):
            return ctx.enter_context(nc.semaphore(name))

        banks = [ctx.enter_context(nc.psum_tensor(f"bank{i}", [P, 512], F32)) for i in range(8)]

        EXPERT = DC * 4 * D
        W_AT = (nc.sbuf_top - 2 * E * EXPERT) // 32 * 32
        ws = nc.alloc_sbuf_tensor_at("ws", [P, E * EXPERT], F16, offset=W_AT)
        EARLY_E = 2
        early_in = sem("early_in")
        late_in = sem("late_in")
        need_tab = sb("need_tab", [P, TAB], I32)

        def load_expert(eng, e):
            o = (E - 1 - e) * EXPERT
            eng.dma_start(ws[:, o:o + EXPERT].rearrange("p (c n) -> p c n", c=DC),
                          wsplit_dram[e, :, :, :].rearrange("c p n -> p c n")).then_inc(early_in if e < EARLY_E else late_in, 16)

        ident = sb("ident", [P, P], F32)
        ident16 = sb("ident16", [P, P], F16)
        half_neg = sb("half_neg", [P, 1], F32)
        exp_tab = sb("exp_tab", [P, TAB], I32)
        row_tab = sb("row_tab", [P, TAB], I32)

        mix = ExitStack()
        with mix:
            def mb(name, shape, dt):
                return sb(name, shape, dt, mix)

            win = mb("win", [P, 2, DC, D], F16)
            wattn = mb("wattn", [P, 2, DC, NL], F16)
            wout = mb("wout", [P, 2, DC, D], F16)
            wg_sb = mb("wg_sb", [P, DC, E], F32)
            bg_sb = mb("bg_sb", [P, E], F32)
            sw_sb = mb("sw_sb", [P, 2], F32)
            sw_tmp = mb("sw_tmp", [P, 4], F32)
            XT = mb("XT", [P, 2, 4, DC, P], F16)
            KT = mb("KT", [P, 2, DC, T], F16)
            stage = mb("stage", [P, 2, 1024], F32)
            xstage = mb("xstage", [P, DC, P], F32)
            kstage = mb("kstage", [P, DC, P], F32)
            ehalf = mb("ehalf", [P, 2, 2, 2 * D], F16)
            xrow = mb("xrow", [P, 4, D], F32)
            xi = mb("xi", [P, 4, 2, D], F16)
            rT = mb("rT", [P, 2, DC, P], F16)
            ee = mb("ee", [P, NL], F32)
            mx = mb("mx", [P, 2, HEADS], F32)
            sm = mb("sm", [P, 2, HEADS], F32)
            t0 = mb("t0", [P, HEADS, C0], F32)
            wwin = mb("wwin", [P, 2, HEADS, C1], F32)
            band = mb("band", [P, 2, SIDE + BROW + SIDE], F32)
            xc = mb("xc", [2 * SIDE, 2, 2, D], F16)
            bt = mb("bt", [P, 2, HEADS, P], F16)
            bs = mb("bs", [2 * SIDE, 2, HEADS + 1, 2, SIDE], F16)
            oT = mb("oT", [P, 2, DC, P], F16)
            z = mb("z", [P, D], F32)
            st = mb("st", [P, 12], F32)
            y1 = mb("y1", [P, 4, D], F32)
            y1s = mb("y1s", [P, NT, 2, D], F16)
            NBLK = NT * (NT + 1) // 2
            PT = mb("PT", [P, 2, NBLK * P], F16)
            yrow = mb("yrow", [P, 4, ROWLEN], F32)
            yT = mb("yT", [P, DC, P], F32)
            lg = mb("lg", [P, E], F32)
            less_top = mb("less_top", [P, E], F32)
            rexp = mb("rexp", [P, E], F32)
            rden = mb("rden", [P, 1], F32)
            rkey = mb("rkey", [P, E], F32)
            rmin = mb("rmin", [P, 1], F32)
            onehot = mb("onehot", [P, E], F16)
            place = mb("place", [P, 2, E], F32)
            placef = mb("placef", [P, 1], F32)
            filled = mb("filled", [P, E], F32)
            slot = mb("slot", [P, 4], I32)
            e_less = mb("e_less", [P, E], F32)
            tri = mb("tri", [P, P], F16)
            ones = mb("ones", [P, P], F16)
            zrow = mb("zrow", [P, ROWLEN], F32)
            pad_idx = mb("pad_idx", [P, E], I32)
            pad_off = mb("pad_off", [P, 1], F32)
            region0 = mb("region0", [P, E], F32)
            pages = mb("pages", [P, 4, E], F32)
            pages_i = mb("pages_i", [P, 2, E], I32)
            karr = mb("karr", [P, TAB], F32)
            passed = stage[:, 0, 0:2 * TAB * E].rearrange("p (k n e) -> p k n e", k=2, e=E)
            tabf = mb("tabf", [P, 2, TAB], F32)

            first_early = W_AT + 2 * (E - EARLY_E) * EXPERT
            assert nc.sbuf_base <= first_early, (nc.sbuf_base, first_early)

            passed_wait = sem("passed_wait")
            consts = sem("consts")
            consts_in = sem("consts_in")
            zero_out = sem("zero_out")
            stage_in = [sem("stage_in0"), sem("stage_in1")]
            split_h = sem("split_h")
            split_l = sem("split_l")
            xt_in = sem("xt_in")
            kt_in = sem("kt_in")
            xt_h = sem("xt_h")
            xt_l = sem("xt_l")
            kt_h = sem("kt_h")
            kt_l = sem("kt_l")
            e_in = [sem("e_in0"), sem("e_in1")]
            e_h = sem("e_h")
            e_l = sem("e_l")
            e_out = [sem("e_out0"), sem("e_out1")]
            x_in = [sem(f"x_in{i}") for i in range(4)]
            xi_ready = sem("xi_ready")
            xih_done = sem("xih_done")
            xil_done = sem("xil_done")
            xit_ready = sem("xit_ready")
            rth_done = sem("rth_done")
            rt_done = sem("rt_done")
            logits_ready = sem("logits_ready")
            lsub_done = sem("lsub_done")
            exp_done = sem("exp_done")
            inv_done = sem("inv_done")
            wsum_done = sem("wsum_done")
            skew_out = [sem("skew_out0"), sem("skew_out1")]
            band_in = [sem("band_in0"), sem("band_in1")]
            xc_done = sem("xc_done")
            outT_ready = sem("outT_ready")
            oth_done = sem("oth_done")
            otl_done = sem("otl_done")
            prod_ready = sem("prod_ready")
            z_done = sem("z_done")
            var_done = sem("var_done")
            rstd_done = sem("rstd_done")
            y1_done = sem("y1_done")
            y1h_done = sem("y1h_done")
            y1l_done = sem("y1l_done")
            masked = sem("masked")
            y2_done = sem("y2_done")
            ring_full = sem("ring_full")
            ring_h = sem("ring_h")
            ring_done = sem("ring_done")
            dve_chain = sem("dve_chain")
            pool_chain = sem("pool_chain")
            rlog_done = sem("rlog_done")
            rexp_done = sem("rexp_done")
            onehot_done = sem("onehot_done")
            slot_done = sem("slot_done")
            rows_out = [sem(f"rows_out{i}") for i in range(4)]
            tables_done = sem("tables_done")
            pads_out = sem("pads_out")

            KT_tiles = KT[:, :, :, :].rearrange("p k c (j t) -> p k j c t", t=P)

            def w_piece(src, buf, c, cols):
                return ("w", src, buf[:, 0, c:c + 2, :], buf[:, 1, c:c + 2, :], c, cols)

            def t_piece(src, buf, tile_, slot_):
                return ("t", src, buf[:, 0, slot_, :, :], buf[:, 1, slot_, :, :], tile_, None)

            WIN = [w_piece(winT, win, c, ((0, 0, D),)) for c in range(0, DC, 2)]
            WATTN = [w_piece(wattnT, wattn, c, ((0, 0, L0), (L1_AT, L0, L1))) for c in range(0, DC, 2)]
            WOUT = [w_piece(woutT, wout, c, ((0, 0, D),)) for c in range(0, DC, 2)]
            XLEAD = 3
            pieces = WIN + [t_piece(xT, XT, i, i) for i in range(XLEAD)] + WATTN + WOUT + \
                [t_piece(ctxT, KT_tiles, i, i) for i in range(NT)]
            X0_SPLIT = len(WIN) + 1
            WATTN_SPLIT = len(WIN) + XLEAD + len(WATTN)

            slot_level = [0, 0]
            piece_level = []
            for n, p in enumerate(pieces):
                slot_level[n % 2] += 16 * (len(p[5]) if p[0] == "w" else 1)
                piece_level.append(slot_level[n % 2])

            def staged(n):
                p = pieces[n]
                if p[0] == "t":
                    return stage[:, n % 2, 0:DC * P].rearrange("p (c t) -> p c t", c=DC), 1.0
                w = sum(x[2] for x in p[5])
                return stage[:, n % 2, 0:2 * w].rearrange("p (c n) -> p c n", c=2), WEIGHT_SCALE

            TAIL = 5
            BACK, MIX, GATE, ROUTE = 2, 3, 4, 5

            def tile(s, b, phase, lag=0):
                i = s - lag
                if phase == "last":
                    return (i, b) if 0 <= i < NT else None
                if i >= 0:
                    return i, b
                return (i + NT, b - 1) if phase == "loop" else None

            def steps(eng, step):
                for s in range(NT):
                    step(s, 0, "first")
                mark = counts()
                with eng.Fori(1, B) as b:
                    restart(mark, b)
                    for s in range(NT):
                        step(s, b, "loop")
                    per = per_loop(mark)
                end_loop(mark, per)
                for s in range(NT, NT + TAIL):
                    step(s, B - 1, "last")

            chain = {"n": 0, "base": 0}
            CHAIN_PER = {"dve": 152, "pool": 8, "none": 0}

            def counts():
                return chain["n"]

            def restart(mark, b):
                chain["base"] = (b - 1) * CHAIN_PER[chain["who"]]

            def per_loop(mark):
                return chain["n"] - mark

            def end_loop(mark, per):
                if per:
                    assert per == CHAIN_PER[chain["who"]], per
                    chain["base"] = (B - 2) * per

            def linked(eng, signal, ins, own=False):
                chain["n"] += 1
                ins.then_inc(signal, 1)
                eng.wait_ge(signal, chain["base"] + chain["n"])
                if own:
                    alone(eng)

            def at(b, k, m=1):
                return b * (NT * m) + (k * m + 1)

            def dma_at(b, i, n):
                return b * (16 * NT // n) + 16 * (i // n + 1)

            class Order:

                def __init__(self, of):
                    self.at = {}
                    self.size = {}
                    for phase, r in (("first", range(NT)), ("loop", range(NT)), ("last", range(NT, NT + TAIL))):
                        n = 0
                        for s in r:
                            for it in of(s, phase):
                                self.at[(phase, s) + it] = n
                                n += 1
                        self.size[phase] = n

                def number(self, phase, s, b, *it):
                    n = self.at[(phase, s) + it]
                    if phase == "first":
                        return n
                    loops = b - 1 if phase == "loop" else b
                    return loops * self.size["loop"] + (self.size["first"] + n)

                def done(self, phase, s, b, *it):
                    return self.number(phase, s, b, *it) + 2

                def all_before(self, phase, s, b):
                    it = min((n, key[2:]) for key, n in self.at.items() if key[:2] == (phase, s))[1]
                    return self.number(phase, s, b, *it) + 1

                def before(self, eng, signal, back, phase, s, b, *it):
                    n = self.number(phase, s, b, *it)
                    if not isinstance(n, int) or n >= back:
                        eng.wait_ge(signal, n - back + 2)

            SCORE_WIDTHS = [(512, 512), (384, 512), (256, 512), (128, 512), (256, 256), (128, 256), (256,), (128,)]

            def score_pieces(j):
                widths = SCORE_WIDTHS[j]
                assert sum(widths) == (NT - j) * P
                return [(sum(widths[:n]), w) for n, w in enumerate(widths)]

            BAND_ITEMS = [("own", h, 4) for h in range(0, HEADS, 4)] + [("sides", j, min(4, HEADS + 1 - j)) for j in range(0, HEADS + 1, 4)]
            EARLY = 3

            def band_views(n, bank):
                kind, j0, k = BAND_ITEMS[n]
                blocks = bank[:, 0:k * P].rearrange("p (j t) -> p j t", j=k)
                if kind == "own":
                    return [blocks] + [bt[:, a, j0:j0 + k, :] for a in range(2)]
                src = bank[0:2 * SIDE, 0:k * P].rearrange("p (j a t) -> p j a t", j=k, t=SIDE)[:, :, 0:4:3, :]
                return [src] + [bs[:, a, j0:j0 + k, :, :] for a in range(2)]

            def ring_of(s, phase):
                items = []
                if tile(s, 1, phase, BACK):
                    items += [("band", n) for n in range(len(BAND_ITEMS))]
                if tile(s, 1, phase, GATE):
                    items.append(("y2T", 0))
                if tile(s, 1, phase, ROUTE):
                    items.append(("rank", 0))
                if t := tile(s, 1, phase, MIX):
                    items += [("scores", n) for n in range(len(score_pieces(t[0])))]
                if tile(s, 1, phase, GATE):
                    items.append(("gate", 0))
                return items

            def split_of(s, phase):
                return [it for it in ring_of(s, phase) if it[0] in ("band", "scores")]

            def prods_of(s, phase):
                return [(w,) for w, lag in (("mix", MIX), ("wout", BACK)) if tile(s, 1, phase, lag)]

            ring, splits, prods = Order(ring_of), Order(split_of), Order(prods_of)
            BLK = [sum(NT - jj for jj in range(j)) for j in range(NT)]

            def ring_bank(phase, s, *it):
                n = ring.at[(phase, s) + it]
                if phase != "first":
                    n += ring.size["first"]
                assert ring.size["loop"] % RING == 0
                return banks[3 + n % RING]

            def alone(eng):
                eng.sem_inc(passed_wait, 1)

            xi_bank, xit_bank, logit_bank, outT_bank, prod_bank = banks[0], banks[1], banks[2], banks[6], banks[7]
            xit = xit_bank[:, :].bitcast(F16).rearrange("p (k c t) -> p k c t", k=2, c=DC)
            outT = outT_bank[:, :].rearrange("p (c t) -> p c t", c=DC)

            assert E == 2 * B and NT == 2 * DC
            w1_rows = w1.rearrange("e d n -> (e d) n")
            w2_rows = w2.rearrange("e d n -> (e d) n")

            block = mix.enter_context(nc.Block())

            @block.sync
            def _(sp):
                chain.update(n=0, base=0, who="none")
                sp.dma_start(sw_sb[:, :], scale_w.rearrange("(a n) -> a n", a=1).broadcast_to([P, 2])).then_inc(consts_in, 16)
                sp.dma_start(bg_sb[:, :], bg.rearrange("(a n) -> a n", a=1).broadcast_to([P, E])).then_inc(consts_in, 16)
                sp.dma_start(wg_sb[:, :, :], wg.rearrange("(c p) e -> p c e", p=P)).then_inc(consts_in, 16)
                for n, (kind, src, _, _, c, cols) in enumerate(pieces):
                    if n >= 2:
                        sp.wait_ge(split_l, n - 1)
                    dst, _ = staged(n)
                    if kind == "t":
                        sp.dma_start(dst, src[0, :, c * P:(c + 1) * P].rearrange("(c p) t -> p c t", p=P)).then_inc(stage_in[n % 2], 16)
                    else:
                        for s0, d0, k in cols:
                            sp.dma_start(dst[:, :, d0:d0 + k],
                                         src[c * P:(c + 2) * P, s0:s0 + k].rearrange("(c p) n -> p c n", p=P)
                                         ).then_inc(stage_in[n % 2], 16)
                sp.wait_ge(consts, 1)
                for k in range(2):
                    sp.dma_start(skew_dram[k, :].rearrange("(p n) -> p n", p=P), band[:, k, 0:SKEW]).then_inc(zero_out, 16)
                sp.dma_start(sorted_dram[E * REGION:ROWS, :], zrow[:, :]).then_inc(zero_out, 16)
                sp.wait_ge(zero_out, 48)
                sp.wait_ge(split_l, len(pieces))

                x_rows = x.rearrange("b t d -> (b t) d")
                xT_rows = xT.rearrange("b d t -> (b d) t")
                ctxT_rows = ctxT.rearrange("b d t -> (b d) t")

                def step(s, b, phase):
                    if t := tile(s, b, phase):
                        i, tb = t
                        ahead = i + XLEAD
                        rows = (b if ahead < NT else (b + 1) % B) * D
                        if phase == "loop" or s > 0:
                            sp.wait_ge(xt_l, at(b, s))
                        alone(sp)
                        sp.dma_start(xstage[:, :, :], xT_rows[bass.ds(rows, D), (ahead % NT) * P:(ahead % NT + 1) * P]
                                     .rearrange("(c p) t -> p c t", p=P)).then_inc(xt_in, 16)
                        if kt := tile(s, b, phase, MIX):
                            j, jb = kt
                            if phase == "loop" or j > 0:
                                sp.wait_ge(kt_l, at(jb, j))
                            alone(sp)
                            sp.dma_start(kstage[:, :, :], ctxT_rows[bass.ds(((jb + 1) % B) * D, D), j * P:(j + 1) * P]
                                         .rearrange("(c p) t -> p c t", p=P)).then_inc(kt_in, 16)
                        if phase == "loop" or s >= 2:
                            sp.wait_ge(e_l, at(b, s - 1))
                        alone(sp)
                        row = (b * 2 + s // DC) * D + (s % DC) * P
                        for k, w_rows in enumerate((w1_rows, w2_rows)):
                            sp.dma_start(stage[:, s % 2, k * D:(k + 1) * D], w_rows[bass.ds(row, P), :]).then_inc(e_in[s % 2], 16)
                        if phase == "loop" or i >= 4:
                            sp.wait_ge(y1_done, at(b, i - 3))
                            alone(sp)
                        sp.dma_start(xrow[:, i % 4, :], x_rows[bass.ds(b * T + i * P, P), :]).then_inc(x_in[i % 4], 16)
                        sp.wait_ge(wsum_done, at(b, i + 1))
                        alone(sp)
                        if phase == "loop" or i >= 2:
                            sp.wait_ge(band_in[i % 2], dma_at(b, i - 2, 2))
                        alone(sp)
                        rows = skew_dram[i % 2, :].rearrange("(t n) -> t n", n=SKEW)[:, 0:BROW]
                        sp.dma_start(rows.rearrange("t (h n) -> t h n", h=HEADS)[:, :, SHIFT:SHIFT + C1],
                                     wwin[:, i % 2, :, :]).then_inc(skew_out[i % 2], 16)
                        sp.wait_ge(skew_out[i % 2], dma_at(b, i, 2))
                        alone(sp)
                        if phase == "loop" or i >= 2:
                            sp.wait_ge(outT_ready, at(b, i - 1))
                            alone(sp)
                        flat = skew_dram[i % 2, 0:P * BROW].rearrange("(t n) -> t n", n=BROW)
                        sp.dma_start(band[:, i % 2, SIDE:SIDE + BROW], flat).then_inc(band_in[i % 2], 16)
                        sp.wait_ge(e_l, at(b, s + 1))
                        alone(sp)
                        sp.dma_start(wsplit_rows[bass.ds(row, P), :], ehalf[:, s % 2, :, :].rearrange("p k n -> p (k n)")
                                     ).then_inc(e_out[s % 2], 16)
                    if phase == "last" and s < NT + EARLY_E:
                        if s == NT:
                            for k in range(2):
                                sp.wait_ge(e_out[k], 16 * (B * NT // 2))
                        load_expert(sp, s - NT)

                steps(sp, step)
                sp.wait_ge(xt_in, 16 * B * NT)
                sp.wait_ge(kt_in, 16 * (B * NT - MIX))

            @block.scalar
            def _(act):
                chain.update(n=0, base=0, who="none")
                for s_ in (xih_done, rth_done, exp_done, oth_done, y1h_done, ring_h, rexp_done, xt_h, kt_h, e_h):
                    act.sem_inc(s_, 1)
                for n, p in enumerate(pieces):
                    act.wait_ge(stage_in[n % 2], piece_level[n])
                    src, scale = staged(n)
                    nc.scalar.activation(p[2], src, ACT.Copy, scale=scale).then_inc(split_h, 1)
                act.wait_ge(dve_chain, 2)
                nc.scalar.activation(sw_tmp[:, 2:4], sw_tmp[:, 0:2], ACT.Exp).then_inc(rexp_done, 1)

                def high(s, b, phase, kind, n, dst, src, scale):
                    act.wait_ge(ring_full, ring.done(phase, s, b, kind, n))
                    nc.scalar.activation(dst, src, ACT.Copy, scale=scale).then_inc(ring_h, 1)

                def step(s, b, phase):
                    def bands(lo, hi_):
                        for n in range(lo, hi_):
                            src, hi, _ = band_views(n, ring_bank(phase, s, "band", n))
                            high(s, b, phase, "band", n, hi, src, 1.0)

                    front, back = tile(s, b, phase), tile(s, b, phase, BACK)
                    if back:
                        bands(0, EARLY)
                    if front:
                        act.wait_ge(xi_ready, at(b, s + 1))
                        nc.scalar.activation(xi[:, s % 4, 0, :], xi_bank[:, :], ACT.Copy,
                                             scale=1.0 / WEIGHT_SCALE).then_inc(xih_done, 1)
                    if back:
                        bands(EARLY, len(BAND_ITEMS))
                    if t := tile(s, b, phase, ROUTE):
                        act.wait_ge(rlog_done, at(t[1], t[0] + 1))
                        nc.scalar.activation(rexp[:, :], less_top[:, :], ACT.Exp).then_inc(rexp_done, 1)
                    if t := tile(s, b, phase, MIX):
                        for n, (c0, w) in enumerate(score_pieces(t[0])):
                            o = BLK[t[0]] * P + c0
                            high(s, b, phase, "scores", n, PT[:, 0, o:o + w], ring_bank(phase, s, "scores", n)[:, 0:w], SCORE_SCALE)
                    if back:
                        act.wait_ge(outT_ready, at(back[1], back[0] + 1))
                        nc.scalar.activation(oT[:, 0, :, :], outT, ACT.Copy).then_inc(oth_done, 1)
                    if front:
                        act.wait_ge(xit_ready, at(b, s + 1))
                        nc.scalar.activation(rT[:, 0, :, :], xit[:, 0, :, :], ACT.Relu).then_inc(rth_done, 1)
                        act.wait_ge(xt_in, b * (16 * NT) + 16 * (s + 1))
                        nc.scalar.activation(XT[:, 0, (s + XLEAD) % 4, :, :], xstage[:, :, :], ACT.Copy).then_inc(xt_h, 1)
                        if t := tile(s, b, phase, MIX):
                            act.wait_ge(kt_in, t[1] * (16 * NT) + 16 * (t[0] + 1))
                            nc.scalar.activation(KT_tiles[:, 0, t[0], :, :], kstage[:, :, :], ACT.Copy).then_inc(kt_h, 1)
                        act.wait_ge(e_in[s % 2], b * (16 * NT) + 32 * (s // 2 + 1))
                        if phase == "loop" or s >= 2:
                            act.wait_ge(e_out[s % 2], dma_at(b, s - 2, 2))
                        nc.scalar.activation(ehalf[:, s % 2, 0, :], stage[:, s % 2, :], ACT.Copy, scale=WEIGHT_SCALE).then_inc(e_h, 1)
                        act.wait_ge(lsub_done, at(b, s + 1, 2))
                        nc.scalar.activation(ee[:, :], ee[:, :], ACT.Exp, scale=1.0 / WEIGHT_SCALE).then_inc(exp_done, 1)
                    if back:
                        i, tb = back
                        act.wait_ge(y1_done, at(tb, i + 1))
                        nc.scalar.activation(y1s[:, i, 0, :], y1[:, i % 4, :], ACT.Copy).then_inc(y1h_done, 1)

                steps(act, step)

            @block.tensor
            def _(pe):
                chain.update(n=0, base=0, who="none")

                def split_product(dst, stat, mov, chunks, first=True, last=True):
                    n = 0
                    for c in range(chunks):
                        for a, m in ((0, 0), (0, 1), (1, 0)):
                            ins = nc.tensor.matmul(dst, stat(a, c), mov(m, c), start=(first and n == 0),
                                                   stop=(last and n == 3 * chunks - 1))
                            n += 1
                    return ins

                for s_ in (xi_ready, xit_ready, logits_ready, outT_ready, prod_ready, ring_full):
                    pe.sem_inc(s_, 1)
                pe.wait_ge(consts, 3)

                def step(s, b, phase):
                    def acquire(*it):
                        ring.before(pe, ring_done, RING, phase, s, b, *it)
                        return ring_bank(phase, s, *it)

                    def bands(lo, hi_):
                        i = back[0]
                        for n in range(lo, hi_):
                            kind, j0, k = BAND_ITEMS[n]
                            bank = acquire("band", n)
                            alone(pe)
                            for j in range(j0, j0 + k):
                                o = (j - j0) * P
                                if kind == "own":
                                    c0 = SIDE + j * BAND + SIDE
                                    ins = nc.tensor.transpose(bank[:, o:o + P], band[:, i % 2, c0:c0 + P], ident[:, :])
                                else:
                                    c0 = j * BAND
                                    ins = nc.tensor.transpose(bank[0:2 * SIDE, o:o + P], band[:, i % 2, c0:c0 + 2 * SIDE], ident[:, :])
                            ins.then_inc(ring_full, 1)

                    front, back = tile(s, b, phase), tile(s, b, phase, BACK)
                    mixed, gate, route = (tile(s, b, phase, lag) for lag in (MIX, GATE, ROUTE))
                    if back:
                        pe.wait_ge(band_in[back[0] % 2], dma_at(back[1], back[0], 2))
                        bands(0, EARLY)
                    if front:
                        if phase == "first" and s < XLEAD:
                            pe.wait_ge(split_l, X0_SPLIT + s)
                        else:
                            pe.wait_ge(xt_l, at(b, s - XLEAD + 1))
                        if phase == "loop" or s > 0:
                            pe.wait_ge(xil_done, at(b, s))
                        split_product(xi_bank[:, :], lambda a, c: XT[:, a, s % 4, c, :],
                                      lambda m, c: win[:, m, c, :], DC).then_inc(xi_ready, 1)
                    if back:
                        bands(EARLY, len(BAND_ITEMS))
                    if gate:
                        pe.wait_ge(y2_done, at(gate[1], gate[0] + 1))
                        bank = acquire("y2T", 0)
                        for c in range(DC):
                            ins = nc.tensor.transpose(bank[:, c * P:(c + 1) * P], yrow[:, gate[0] % 4, c * P:(c + 1) * P], ident[:, :])
                        ins.then_inc(ring_full, 1)
                    if route:
                        pe.wait_ge(onehot_done, at(route[1], route[0] + 1))
                        bank = acquire("rank", 0)
                        nc.tensor.matmul(bank[:, 0:E], tri[:, :], onehot[:, :], start=True, stop=True)
                        nc.tensor.matmul(bank[:, E:2 * E], ones[:, :], onehot[:, :], start=True, stop=True).then_inc(ring_full, 1)
                    if mixed:
                        j = mixed[0]
                        if phase == "first":
                            pe.wait_ge(split_l, len(pieces))
                        else:
                            pe.wait_ge(kt_l, at(mixed[1] - 1, NT))
                        for n, (c0, w) in enumerate(score_pieces(j)):
                            bank = acquire("scores", n)
                            t0_ = j * P + c0
                            split_product(bank[:, 0:w], lambda a, c: KT[:, a, c, j * P:(j + 1) * P],
                                          lambda m, c: KT[:, m, c, t0_:t0_ + w], DC).then_inc(ring_full, 1)
                    if back:
                        i, tb = back
                        pe.wait_ge(ring_done, ring.done(phase, s, b, "band", len(BAND_ITEMS) - 1))
                        pe.wait_ge(xc_done, at(tb, i + 1))
                        if phase != "first" or i > 0:
                            pe.wait_ge(otl_done, at(tb, i))

                        def side_cols(m, h):
                            flat = bs[:, m, :, :, :].rearrange("p j a t -> p (j a) t")
                            return flat[:, 2 * h:2 * h + 4:3, :]

                        for h in range(HEADS):
                            q = HD * (h % 2)
                            dst = outT[q:q + HD, h // 2, :]
                            split_product(dst, lambda a, c: xi[:, i % 4, a, h * HD:(h + 1) * HD],
                                          lambda m, c: bt[:, m, h, :], 1, last=False)
                            sides = dst.rearrange("p (a n) -> p a n", n=SIDE)[:, 0:4:3, :]
                            ins = split_product(sides, lambda a, c: xc[:, i % 2, a, h * HD:(h + 1) * HD],
                                                lambda m, c: side_cols(m, h), 1, first=False)
                        ins.then_inc(outT_ready, 1)
                    if front:
                        pe.wait_ge(xil_done, at(b, s + 1))
                        if phase == "loop" or s > 0:
                            pe.wait_ge(rt_done, at(b, s))
                        for k in range(2):
                            for c in range(DC):
                                ins = nc.tensor.transpose(xit[:, k, c, :], xi[:, s % 4, k, c * P:(c + 1) * P], ident16[:, :])
                        ins.then_inc(xit_ready, 1)
                    if mixed:
                        i, tb = mixed
                        pe.wait_ge(y1l_done, at(tb, i + 1))
                        pe.wait_ge(masked, at(tb, i + 1))
                        prods.before(pe, z_done, 1, phase, s, b, "mix")
                        split_product(prod_bank[:, :],
                                      lambda a, j: PT[:, a, (BLK[j] + i - j) * P:(BLK[j] + i - j + 1) * P],
                                      lambda m, j: y1s[:, j, m, :], i + 1).then_inc(prod_ready, 1)
                    if front:
                        pe.wait_ge(rt_done, at(b, s + 1))
                        if phase == "first" and s == 0:
                            pe.wait_ge(split_l, WATTN_SPLIT)
                        else:
                            pe.wait_ge(lsub_done, at(b, s, 2))
                        split_product(logit_bank[:, 0:NL], lambda a, c: rT[:, a, c, :],
                                      lambda m, c: wattn[:, m, c, :], DC).then_inc(logits_ready, 1)
                    if gate:
                        pe.wait_ge(ring_done, ring.done(phase, s, b, "y2T", 0))
                        bank = acquire("gate", 0)
                        for c in range(DC):
                            ins = nc.tensor.matmul(bank[:, 0:E], yT[:, c, :], wg_sb[:, c, :], start=(c == 0), stop=(c == DC - 1))
                        ins.then_inc(ring_full, 1)
                    if back:
                        i, tb = back
                        pe.wait_ge(otl_done, at(tb, i + 1))
                        prods.before(pe, z_done, 1, phase, s, b, "wout")
                        split_product(prod_bank[:, :], lambda a, c: oT[:, a, c, :],
                                      lambda m, c: wout[:, m, c, :], DC).then_inc(prod_ready, 1)

                pe.wait_ge(consts_in, 48)
                steps(pe, step)

            @block.gpsimd
            def _(pool):
                chain.update(n=0, base=0, who="pool")
                for s_ in (wsum_done, rstd_done, masked, xt_l, kt_l):
                    pool.sem_inc(s_, 1)

                def link(ins):
                    linked(pool, pool_chain, ins)

                link(nc.gpsimd.memset(zrow[:, :], 0.0))
                nc.gpsimd.memset(zrow[:, D + 1:D + 2], float(NO_TOKEN))
                link(nc.gpsimd.memset(band[:, :, :], 0.0))
                pool.sem_inc(consts, 1)
                link(nc.gpsimd.memset(ident[:, :], 0.0))
                link(nc.gpsimd.affine_select(out=ident[:, :], in_=ident[:, :], compare_op=ALU.not_equal, fill=1.0,
                                             base=0, pattern=[[-1, P]], channel_multiplier=1))
                nc.gpsimd.tensor_copy(ident16[:, :], ident[:, :])
                nc.gpsimd.memset(half_neg[:, :], -0.5)
                link(nc.gpsimd.memset(ones[:, :], 1.0))
                link(nc.gpsimd.affine_select(out=tri[:, :], in_=ones[:, :], compare_op=ALU.is_ge, fill=0.0,
                                             base=-1, pattern=[[1, P]], channel_multiplier=-1))
                pool.sem_inc(consts, 2)
                iota_kw = dict(allow_small_or_imprecise_dtypes=True)
                nc.gpsimd.iota(e_less[:, :], pattern=[[1, E]], base=-E, channel_multiplier=0, **iota_kw)
                nc.gpsimd.iota(region0[:, :], pattern=[[REGION, E]], base=0, channel_multiplier=0, **iota_kw)
                nc.gpsimd.iota(filled[:, :], pattern=[[REGION, E]], base=0, channel_multiplier=0, **iota_kw)
                nc.gpsimd.iota(pad_off[:, :], pattern=[[0, 1]], base=0, channel_multiplier=1, **iota_kw)
                nc.gpsimd.iota(karr[:, :], pattern=[[1, TAB]], base=0, channel_multiplier=0, **iota_kw)
                link(nc.gpsimd.memset(yrow[:, :, D:ROWLEN], 0.0))
                for i in range(4):
                    link(nc.gpsimd.iota(yrow[:, i, D + 1:D + 2], pattern=[[0, 1]], base=(i - 4) * P, channel_multiplier=1, **iota_kw))
                pool.sem_inc(consts, 1)

                def step(s, b, phase):
                    front, back, mixed, route = (tile(s, b, phase, lag) for lag in (0, BACK, MIX, ROUTE))

                    def rstd(what):
                        pool.wait_ge(var_done, prods.done(phase, s, b, what))
                        nc.gpsimd.tensor_tensor(st[:, 9:10], st[:, 8:9], half_neg[:, :], ALU.pow).then_inc(rstd_done, 1)

                    if route:
                        i, tb = route
                        pool.wait_ge(slot_done, at(tb, i + 1))
                        alone(pool)
                        nc.gpsimd.indirect_dma_start(out=sorted_dram, out_offset=bass.IndirectOffsetOnAxis(ap=slot[:, i % 4:i % 4 + 1], axis=0),
                                                     in_=yrow[:, i % 4, :], in_offset=None).then_inc(rows_out[i % 4], 16)
                    if mixed:
                        pool.wait_ge(ring_done, ring.done(phase, s, b, "scores", 0))
                        alone(pool)
                        for k in range(2):
                            o = BLK[mixed[0]] * P
                            ins = nc.gpsimd.affine_select(out=PT[:, k, o:o + P], in_=PT[:, k, o:o + P],
                                                          compare_op=ALU.is_ge, fill=0.0, base=0,
                                                          pattern=[[1, P]], channel_multiplier=-1)
                        ins.then_inc(masked, 1)
                    if mixed:
                        rstd("mix")
                    if front:
                        pool.wait_ge(xt_h, at(b, s + 1))
                        nc.gpsimd.tensor_tensor(XT[:, 1, (s + XLEAD) % 4, :, :], xstage[:, :, :], XT[:, 0, (s + XLEAD) % 4, :, :],
                                                ALU.subtract).then_inc(xt_l, 1)
                        if t := tile(s, b, phase, MIX):
                            pool.wait_ge(kt_h, at(t[1], t[0] + 1))
                            nc.gpsimd.tensor_tensor(KT_tiles[:, 1, t[0], :, :], kstage[:, :, :], KT_tiles[:, 0, t[0], :, :],
                                                    ALU.subtract).then_inc(kt_l, 1)
                        i = s
                        pool.wait_ge(inv_done, at(b, i + 1))
                        e0 = ee[:, 0:L0].rearrange("p (h c) -> p h c", h=HEADS)
                        e1 = ee[:, L0:NL].rearrange("p (h c) -> p h c", h=HEADS)
                        nc.gpsimd.tensor_tensor(t0[:, :, :], e0, sm[:, 0, :].unsqueeze(2).broadcast_to([P, HEADS, C0]), ALU.mult)
                        if phase == "loop" or i >= 2:
                            pool.wait_ge(skew_out[i % 2], dma_at(b, i - 2, 2))
                        link(nc.gpsimd.tensor_tensor(wwin[:, i % 2, :, :], e1, sm[:, 1, :].unsqueeze(2).broadcast_to([P, HEADS, C1]), ALU.mult))
                        win_mid = wwin[:, i % 2, :, (C1 - C0) // 2:(C1 + C0) // 2]
                        nc.gpsimd.tensor_tensor(win_mid, win_mid, t0[:, :, :], ALU.add).then_inc(wsum_done, 1)
                    if back:
                        rstd("wout")

                steps(pool, step)
                pool.wait_ge(tables_done, 1)
                for e in range(E):
                    nc.gpsimd.indirect_dma_start(out=sorted_dram, out_offset=bass.IndirectOffsetOnAxis(ap=pad_idx[:, e:e + 1], axis=0),
                                                 in_=zrow[:, :], in_offset=None).then_inc(pads_out, 16)
                pool.wait_ge(pads_out, 16 * E)
                for i in range(4):
                    pool.wait_ge(rows_out[i], 16 * (B * NT // 4))

            @block.vector
            def _(dve):
                chain.update(n=0, base=0, who="dve")
                for s_ in (xil_done, xc_done, rt_done, lsub_done, inv_done, otl_done, z_done, var_done, y1_done, y1l_done,
                           y2_done, ring_done, rlog_done, onehot_done, slot_done, e_l):
                    dve.sem_inc(s_, 1)

                def link(ins, own=False):
                    linked(dve, dve_chain, ins, own)

                for n, p in enumerate(pieces):
                    dve.wait_ge(split_h, n + 1)
                    src, scale = staged(n)
                    nc.vector.scalar_tensor_tensor(out=p[3], in0=src, scalar=scale, in1=p[2], op0=ALU.mult,
                                                   op1=ALU.subtract).then_inc(split_l, 1)
                    if n == 0:
                        dve.wait_ge(consts_in, 48)
                        link(nc.vector.reduce_max(st[:, 0:1], sw_sb[:, :], axis=AX))
                        link(nc.vector.tensor_scalar(sw_tmp[:, 0:2], sw_sb[:, :], st[:, 0:1], None, ALU.subtract))
                dve.wait_ge(rexp_done, 2)
                link(nc.vector.reduce_sum(st[:, 1:2], sw_tmp[:, 2:4], axis=AX))
                link(nc.vector.reciprocal(st[:, 2:3], st[:, 1:2]))
                link(nc.vector.tensor_scalar(sw_sb[:, :], sw_tmp[:, 2:4], st[:, 2:3], None, ALU.mult))
                dve.wait_ge(consts, 4)

                def step(s, b, phase):
                    front, back = tile(s, b, phase), tile(s, b, phase, BACK)
                    mixed, gate, route = (tile(s, b, phase, lag) for lag in (MIX, GATE, ROUTE))

                    def bands(lo, hi_):
                        for n in range(lo, hi_):
                            dve.wait_ge(ring_h, splits.done(phase, s, b, "band", n))
                            src, hi, low = band_views(n, ring_bank(phase, s, "band", n))
                            nc.vector.tensor_tensor(low, src, hi, ALU.subtract).then_inc(ring_done, 1)

                    def normed(what, eps, to):
                        dve.wait_ge(z_done, prods.done(phase, s, b, what))
                        link(nc.vector.bn_stats(st[:, 0:6], z[:, :]), own=True)
                        link(nc.vector.bn_aggr(st[:, 6:8], st[:, 0:6]))
                        nc.vector.tensor_scalar(st[:, 8:9], st[:, 7:8], eps, None, ALU.add).then_inc(var_done, 1)
                        dve.wait_ge(rstd_done, prods.done(phase, s, b, what))
                        return nc.vector.tensor_scalar(to, z[:, :], st[:, 6:7], st[:, 9:10], ALU.subtract, ALU.mult)

                    if back:
                        i, tb = back
                        if phase != "first" or i >= 2:
                            dve.wait_ge(outT_ready, at(tb, i - 1))
                        dve.wait_ge(xil_done, at(tb, min(i + 2, NT)))
                        if i > 0:
                            link(nc.vector.tensor_copy(xc[SIDE:2 * SIDE, i % 2, :, :], xi[P - SIDE:P, (i - 1) % 4, :, :]))
                        else:
                            link(nc.vector.tensor_scalar(xc[SIDE:2 * SIDE, i % 2, :, :], xi[P - SIDE:P, i % 4, :, :], 0.0, None, ALU.mult))
                        if i < NT - 1:
                            ins = nc.vector.tensor_copy(xc[0:SIDE, i % 2, :, :], xi[0:SIDE, (i + 1) % 4, :, :])
                        else:
                            ins = nc.vector.tensor_scalar(xc[0:SIDE, i % 2, :, :], xi[0:SIDE, i % 4, :, :], 0.0, None, ALU.mult)
                        ins.then_inc(xc_done, 1)
                    if route:
                        dve.wait_ge(ring_done, ring.all_before(phase, s, b))
                        link(nc.vector.reduce_max(rmin[:, :], lg[:, :], axis=AX))
                        nc.vector.tensor_scalar(less_top[:, :], lg[:, :], rmin[:, :], None, ALU.subtract).then_inc(rlog_done, 1)
                        dve.wait_ge(rlog_done, at(route[1], route[0] + 1))
                        link(nc.vector.scalar_tensor_tensor(out=rkey[:, :], in0=less_top[:, :], scalar=0.0, in1=e_less[:, :],
                                                            op0=ALU.is_equal, op1=ALU.mult))
                        link(nc.vector.tensor_reduce(rmin[:, :], rkey[:, :], AX, ALU.min))
                        nc.vector.tensor_scalar(onehot[:, :], e_less[:, :], rmin[:, :], None, ALU.is_equal).then_inc(onehot_done, 1)
                    if back:
                        bands(0, EARLY)
                    if front:
                        dve.wait_ge(xih_done, at(b, s + 1))
                        nc.vector.scalar_tensor_tensor(out=xi[:, s % 4, 1, :], in0=xi_bank[:, :], scalar=1.0 / WEIGHT_SCALE,
                                                       in1=xi[:, s % 4, 0, :], op0=ALU.mult, op1=ALU.subtract).then_inc(xil_done, 1)
                    if back:
                        bands(EARLY, len(BAND_ITEMS))
                    if gate:
                        dve.wait_ge(ring_full, ring.done(phase, s, b, "y2T", 0))
                        nc.vector.tensor_copy(yT[:, :, :].rearrange("p c t -> p (c t)"),
                                              ring_bank(phase, s, "y2T", 0)[:, :]).then_inc(ring_done, 1)
                    if route:
                        i, tb = route
                        bank = ring_bank(phase, s, "rank", 0)
                        dve.wait_ge(ring_full, ring.done(phase, s, b, "rank", 0))
                        link(nc.vector.tensor_tensor(place[:, 0, :], bank[:, 0:E], filled[:, :], ALU.add))
                        link(nc.vector.tensor_tensor(place[:, 1, :], place[:, 0, :], onehot[:, :], ALU.mult))
                        nc.vector.tensor_tensor(filled[:, :], bank[:, E:2 * E], filled[:, :], ALU.add).then_inc(ring_done, 1)
                        link(nc.vector.reduce_sum(placef[:, :], place[:, 1, :], axis=AX))
                        link(nc.vector.tensor_copy(slot[:, i % 4:i % 4 + 1], placef[:, :]))
                        dve.wait_ge(rexp_done, at(tb, i + 1) + 1)
                        link(nc.vector.reduce_sum(rden[:, :], rexp[:, :], axis=AX))
                        link(nc.vector.reciprocal(yrow[:, i % 4, D:D + 1], rden[:, :]))
                        nc.vector.tensor_scalar(yrow[:, i % 4, D + 1:D + 2], yrow[:, i % 4, D + 1:D + 2], float(4 * P), None,
                                                ALU.add).then_inc(slot_done, 1)
                    if mixed:
                        for n, (c0, w) in enumerate(score_pieces(mixed[0])):
                            dve.wait_ge(ring_h, splits.done(phase, s, b, "scores", n))
                            o = BLK[mixed[0]] * P + c0
                            nc.vector.scalar_tensor_tensor(out=PT[:, 1, o:o + w], in0=ring_bank(phase, s, "scores", n)[:, 0:w],
                                                           scalar=SCORE_SCALE, in1=PT[:, 0, o:o + w],
                                                           op0=ALU.mult, op1=ALU.subtract).then_inc(ring_done, 1)
                    if back:
                        dve.wait_ge(oth_done, at(back[1], back[0] + 1))
                        nc.vector.tensor_tensor(oT[:, 1, :, :], outT, oT[:, 0, :, :], ALU.subtract).then_inc(otl_done, 1)
                    if front:
                        dve.wait_ge(rth_done, at(b, s + 1))
                        nc.vector.scalar_tensor_tensor(out=rT[:, 1, :, :], in0=rT[:, 0, :, :], scalar=0.0, in1=xit[:, 1, :, :],
                                                       op0=ALU.is_gt, op1=ALU.mult).then_inc(rt_done, 1)
                    if mixed:
                        i, tb = mixed
                        dve.wait_ge(prod_ready, prods.done(phase, s, b, "mix"))
                        nc.vector.scalar_tensor_tensor(out=z[:, :], in0=prod_bank[:, :], scalar=0.5 / SCORE_SCALE, in1=y1[:, i % 4, :],
                                                       op0=ALU.mult, op1=ALU.add).then_inc(z_done, 1)
                        if phase != "first" or i >= 4:
                            dve.wait_ge(rows_out[i % 4], dma_at(tb, i - 4, 4))
                        normed("mix", EPS / 4, yrow[:, i % 4, 0:D]).then_inc(y2_done, 1)
                    if front:
                        dve.wait_ge(logits_ready, at(b, s + 1))
                        ls = [logit_bank[:, 0:L0].rearrange("p (h c) -> p h c", h=HEADS),
                              logit_bank[:, L0:NL].rearrange("p (h c) -> p h c", h=HEADS)]
                        es = [ee[:, 0:L0].rearrange("p (h c) -> p h c", h=HEADS),
                              ee[:, L0:NL].rearrange("p (h c) -> p h c", h=HEADS)]
                        for k in range(2):
                            link(nc.vector.reduce_max(mx[:, k, :], ls[k], axis=AX))
                        if phase == "loop" or s > 0:
                            dve.wait_ge(wsum_done, at(b, s))
                        for k in range(2):
                            nc.vector.tensor_tensor(es[k], ls[k], mx[:, k, :].unsqueeze(2).broadcast_to([P, HEADS, SIZES[k]]),
                                                    ALU.subtract).then_inc(lsub_done, 1)
                    if gate:
                        dve.wait_ge(ring_full, ring.done(phase, s, b, "gate", 0))
                        nc.vector.tensor_tensor(lg[:, :], ring_bank(phase, s, "gate", 0)[:, 0:E], bg_sb[:, :], ALU.add).then_inc(ring_done, 1)
                    if front:
                        dve.wait_ge(e_h, at(b, s + 1))
                        nc.vector.scalar_tensor_tensor(out=ehalf[:, s % 2, 1, :], in0=stage[:, s % 2, :], scalar=WEIGHT_SCALE,
                                                       in1=ehalf[:, s % 2, 0, :], op0=ALU.mult, op1=ALU.subtract).then_inc(e_l, 1)
                        dve.wait_ge(exp_done, at(b, s + 1))
                        for k in range(2):
                            link(nc.vector.reduce_sum(sm[:, k, :], es[k], axis=AX))
                        link(nc.vector.reciprocal(sm[:, :, :], sm[:, :, :]))
                        nc.vector.tensor_tensor(sm[:, :, :], sm[:, :, :], sw_sb[:, :].unsqueeze(2).broadcast_to([P, 2, HEADS]),
                                                ALU.mult).then_inc(inv_done, 1)
                    if back:
                        i, tb = back
                        dve.wait_ge(prod_ready, prods.done(phase, s, b, "wout"))
                        dve.wait_ge(x_in[i % 4], dma_at(tb, i, 4))
                        if mixed:
                            dve.wait_ge(y2_done, at(mixed[1], mixed[0] + 1))
                        nc.vector.scalar_tensor_tensor(out=z[:, :], in0=prod_bank[:, :], scalar=1.0 / WEIGHT_SCALE, in1=xrow[:, i % 4, :],
                                                       op0=ALU.mult, op1=ALU.add).then_inc(z_done, 1)
                        normed("wout", EPS, y1[:, i % 4, :]).then_inc(y1_done, 1)
                        dve.wait_ge(y1_done, at(tb, i + 1))
                        dve.wait_ge(y1h_done, at(tb, i + 1))
                        nc.vector.tensor_tensor(y1s[:, i, 1, :], y1[:, i % 4, :], y1s[:, i, 0, :], ALU.subtract).then_inc(y1l_done, 1)

                steps(dve, step)

                dve.wait_ge(ring_done, ring.done("last", NT + TAIL - 1, B - 1, "rank", 0))
                link(nc.vector.tensor_tensor(pages[:, 1, :], filled[:, :], region0[:, :], ALU.subtract))
                link(nc.vector.tensor_scalar(pages[:, 0, :], filled[:, :], pad_off[:, :], None, ALU.add))
                link(nc.vector.tensor_copy(pad_idx[:, :], pages[:, 0, :]))
                link(nc.vector.tensor_scalar(pages[:, 1, :], pages[:, 1, :], float(P - 1), None, ALU.add))
                link(nc.vector.tensor_copy(pages_i[:, 0, :], pages[:, 1, :]))
                link(nc.vector.tensor_scalar(pages_i[:, 1, :], pages_i[:, 0, :], 7, None, ALU.arith_shift_right))
                link(nc.vector.tensor_copy(pages[:, 0, :], pages_i[:, 1, :]))
                link(nc.vector.tensor_copy(pages[:, 2, 0:1], pages[:, 0, 0:1]))
                for e in range(1, E):
                    link(nc.vector.tensor_tensor(pages[:, 2, e:e + 1], pages[:, 2, e - 1:e], pages[:, 0, e:e + 1], ALU.add))
                link(nc.vector.tensor_scalar(pages[:, 3, :], pages[:, 0, :], -float(P), float(REGION), ALU.mult, ALU.add))
                full = [P, TAB, E]
                link(nc.vector.tensor_tensor(passed[:, 0, :, :], karr[:, :].unsqueeze(2).broadcast_to(full),
                                             pages[:, 2, :].unsqueeze(1).broadcast_to(full), ALU.is_ge))
                link(nc.vector.tensor_tensor(passed[:, 1, :, :], passed[:, 0, :, :],
                                             pages[:, 3, :].unsqueeze(1).broadcast_to(full), ALU.mult))
                link(nc.vector.reduce_sum(tabf[:, 0, :], passed[:, 0, :, :], axis=AX))
                link(nc.vector.tensor_scalar(exp_tab[:, :], tabf[:, 0, :], float(E - 1), None, ALU.min))
                link(nc.vector.tensor_scalar(tabf[:, 1, :], tabf[:, 0, :], float(EARLY_E), float(16 * (E - EARLY_E)),
                                             ALU.is_ge, ALU.mult))
                link(nc.vector.tensor_scalar(need_tab[:, :], tabf[:, 1, :], 1.0, None, ALU.add))
                link(nc.vector.reduce_sum(tabf[:, 1, :], passed[:, 1, :, :], axis=AX))
                link(nc.vector.scalar_tensor_tensor(out=tabf[:, 0, :], in0=karr[:, :], scalar=float(P), in1=tabf[:, 1, :],
                                                    op0=ALU.mult, op1=ALU.add))
                nc.vector.tensor_scalar(row_tab[:, :], tabf[:, 0, :], float(E * REGION), None, ALU.min).then_inc(tables_done, 1)
                dve.wait_ge(tables_done, 1)

            mix.pop_all().close()

        ffn = ExitStack()
        with ffn:
            def fb(name, shape, dt):
                return sb(name, shape, dt, ffn)

            b1s = fb("b1s", [P, E * D], F32)
            b2s = fb("b2s", [P, E * D], F32)
            page = fb("page", [P, SLOTS, ROWLEN], F32)
            pT = fb("pT", [P, SLOTS, 2, D], F16)
            hpre = fb("hpre", [P, D], F32)
            hact = fb("hact", [P, D], F32)
            hT = fb("hT", [P, 2, D], F16)
            t2 = fb("t2", [P, D], F32)
            z3 = fb("z3", [P, D], F32)
            st3 = fb("st3", [P, 12], F32)
            idx = fb("idx", [P, SLOTS], I32)

            bias_in = sem("bias_in")
            page_in = [sem(f"page_in{i}") for i in range(SLOTS)]
            pT_ready = sem("pT_ready")
            pTh_done = sem("pTh_done")
            pTl_done = sem("pTl_done")
            h_ready = sem("h_ready")
            hpre_done = sem("hpre_done")
            gelu_done = sem("gelu_done")
            hT_ready = sem("hT_ready")
            hTh_done = sem("hTh_done")
            hTl_done = sem("hTl_done")
            o_ready = sem("o_ready")
            o_read = sem("o_read")
            fvar_done = sem("fvar_done")
            frstd_done = sem("frstd_done")
            y3_done = sem("y3_done")
            f_chain = sem("f_chain")
            out_done = [sem(f"out_done{i}") for i in range(SLOTS)]

            h_bank, hT_bank, o_bank = banks[1], banks[2], banks[3]
            pT_banks = [banks[n] for n in (0, 4, 0, 4, 5)]
            assert nc.sbuf_base <= W_AT
            F_PER = SLOTS * 4

            block = ffn.enter_context(nc.Block())

            @block.sync
            def _(sp):
                sp.sem_inc(late_in, 1)
                sp.dma_start(b1s[:, :], b1.rearrange("(a e) n -> a (e n)", a=1).broadcast_to([P, E * D])).then_inc(bias_in, 16)
                sp.dma_start(b2s[:, :], b2.rearrange("(a e) n -> a (e n)", a=1).broadcast_to([P, E * D])).then_inc(bias_in, 16)
                def load(k, u):
                    row = sp.value_load(row_tab[0:1, bass.ds(k, 1)], min_val=0, max_val=ROWS - P)
                    sp.dma_start(page[:, u, :], sorted_dram[bass.ds(row, P), :]).then_inc(page_in[u], 16)

                for k in range(SLOTS):
                    load(k, k)
                for e in range(EARLY_E, E):
                    load_expert(sp, e)
                with sp.Fori(0, GROUPS) as g:
                    for u in range(SLOTS):
                        sp.wait_ge(out_done[u], g * 16 + 16)
                        alone(sp)
                        load(g * SLOTS + (u + SLOTS), u)
                for u in range(SLOTS):
                    sp.wait_ge(page_in[u], 16 * (GROUPS + 1))

            @block.scalar
            def _(act):
                def pT_high(k, u):
                    act.wait_ge(pT_ready, k + 1)
                    nc.scalar.activation(pT[:, u, 0, :], pT_banks[u][:, :], ACT.Copy).then_inc(pTh_done, 1)

                def gelu(k):
                    act.wait_ge(hpre_done, k + 1)
                    nc.scalar.activation(hact[:, :], hpre[:, :], ACT.Gelu).then_inc(gelu_done, 1)

                pT_high(0, 0)
                pT_high(1, 1)
                gelu(0)
                with act.Fori(0, GROUPS) as g:
                    for u in range(SLOTS):
                        k = g * SLOTS + u
                        pT_high(g * SLOTS + (u + 2), (u + 2) % SLOTS)
                        act.wait_ge(hT_ready, k + 1)
                        nc.scalar.activation(hT[:, 0, :], hT_bank[:, :], ACT.Copy).then_inc(hTh_done, 1)
                        gelu(g * SLOTS + (u + 1))

            @block.tensor
            def _(pe):
                def transposes(bank, src, signal):
                    for c in range(DC):
                        ins = nc.tensor.transpose(bank[:, c * P:(c + 1) * P], src[:, c * P:(c + 1) * P], ident[:, :])
                    ins.then_inc(signal, 1)

                def product(bank, stat, w, k):
                    alone(pe)
                    e = pe.value_load(exp_tab[0:1, bass.ds(k, 1)], min_val=0, max_val=E - 1)
                    need = pe.value_load(need_tab[0:1, bass.ds(k, 1)], min_val=1, max_val=16 * E + 1)
                    pe.wait_ge(late_in, need)
                    alone(pe)
                    col = pe.snap((E - 1 - e) * EXPERT)
                    n = 0
                    for c in range(DC):
                        for a, m in ((0, 0), (0, 1), (1, 0)):
                            ins = nc.tensor.matmul(bank[:, :], stat(a, c), ws[:, bass.ds(col + (c * 4 + m * 2 + w) * D, D)],
                                                   start=(n == 0), stop=(n == 3 * DC - 1))
                            n += 1
                    return ins

                def first(k, u):
                    pe.wait_ge(pTl_done, k + 1)
                    if not isinstance(k, int) or k > 0:
                        pe.wait_ge(hpre_done, k)
                    product(h_bank, lambda a, c: pT[:, u, a, c * P:(c + 1) * P], 0, k).then_inc(h_ready, 1)

                pe.wait_ge(page_in[0], 16)
                transposes(pT_banks[0], page[:, 0, :], pT_ready)
                pe.wait_ge(pTl_done, 1)
                pe.wait_ge(page_in[1], 16)
                transposes(pT_banks[1], page[:, 1, :], pT_ready)
                pe.wait_ge(early_in, 16 * EARLY_E)
                first(0, 0)
                with pe.Fori(0, GROUPS) as g:
                    for u in range(SLOTS):
                        k = g * SLOTS + u
                        v = (u + 2) % SLOTS
                        pe.wait_ge(page_in[v], g * 16 + (16 if u + 2 < SLOTS else 32))
                        pe.wait_ge(pTl_done, g * SLOTS + (u + 2))
                        transposes(pT_banks[v], page[:, v, :], pT_ready)
                        pe.wait_ge(gelu_done, g * SLOTS + (u + 1))
                        transposes(hT_bank, hact, hT_ready)
                        first(g * SLOTS + (u + 1), (u + 1) % SLOTS)
                        pe.wait_ge(hTl_done, g * SLOTS + (u + 1))
                        product(o_bank, lambda a, c: hT[:, a, c * P:(c + 1) * P], 1, k).then_inc(o_ready, 1)

            @block.gpsimd
            def _(pool):
                with pool.Fori(0, GROUPS) as g:
                    for u in range(SLOTS):
                        pool.wait_ge(fvar_done, g * SLOTS + (u + 1))
                        nc.gpsimd.tensor_tensor(st3[:, 9:10], st3[:, 8:9], half_neg[:, :], ALU.pow).then_inc(frstd_done, 1)
                        pool.wait_ge(y3_done, g * SLOTS + (u + 1))
                        alone(pool)
                        nc.gpsimd.indirect_dma_start(out=out_rows, out_offset=bass.IndirectOffsetOnAxis(ap=idx[:, u:u + 1], axis=0),
                                                     in_=page[:, u, 0:D], in_offset=None, bounds_check=NTOK - 1,
                                                     oob_is_err=False).then_inc(out_done[u], 16)
                for u in range(SLOTS):
                    pool.wait_ge(out_done[u], 16 * GROUPS)

            @block.vector
            def _(dve):
                dve.wait_ge(bias_in, 32)

                def expert(k):
                    e = dve.value_load(exp_tab[0:1, bass.ds(k, 1)], min_val=0, max_val=E - 1)
                    return dve.snap(e * D)

                def pT_low(k, u):
                    dve.wait_ge(pTh_done, k + 1)
                    nc.vector.tensor_tensor(pT[:, u, 1, :], pT_banks[u][:, :], pT[:, u, 0, :], ALU.subtract).then_inc(pTl_done, 1)

                def hidden(k):
                    col = expert(k)
                    dve.wait_ge(h_ready, k + 1)
                    nc.vector.scalar_tensor_tensor(out=hpre[:, :], in0=h_bank[:, :], scalar=1.0 / WEIGHT_SCALE,
                                                   in1=b1s[:, bass.ds(col, D)], op0=ALU.mult, op1=ALU.add).then_inc(hpre_done, 1)

                pT_low(0, 0)
                pT_low(1, 1)
                hidden(0)
                with dve.Fori(0, GROUPS) as g:
                    n_f = [0]

                    def link(ins, own=False):
                        n_f[0] += 1
                        ins.then_inc(f_chain, 1)
                        dve.wait_ge(f_chain, g * F_PER + n_f[0])
                        if own:
                            alone(dve)

                    def finish(g, u):
                        dve.wait_ge(frstd_done, g * SLOTS + (u + 1))
                        nc.vector.tensor_scalar(page[:, u, 0:D], z3[:, :], st3[:, 6:7], st3[:, 9:10], ALU.subtract, ALU.mult).then_inc(y3_done, 1)
                        dve.wait_ge(y3_done, g * SLOTS + (u + 1))

                    for u in range(SLOTS):
                        k = g * SLOTS + u
                        pT_low(g * SLOTS + (u + 2), (u + 2) % SLOTS)
                        dve.wait_ge(hTh_done, g * SLOTS + (u + 1))
                        nc.vector.tensor_tensor(hT[:, 1, :], hT_bank[:, :], hT[:, 0, :], ALU.subtract).then_inc(hTl_done, 1)
                        if u > 0:
                            finish(g, u - 1)
                        hidden(g * SLOTS + (u + 1))
                        col = expert(k)
                        dve.wait_ge(o_ready, g * SLOTS + (u + 1))
                        nc.vector.scalar_tensor_tensor(out=t2[:, :], in0=o_bank[:, :], scalar=1.0 / WEIGHT_SCALE,
                                                       in1=b2s[:, bass.ds(col, D)], op0=ALU.mult, op1=ALU.add).then_inc(o_read, 1)
                        dve.wait_ge(o_read, g * SLOTS + (u + 1))
                        link(nc.vector.scalar_tensor_tensor(out=z3[:, :], in0=t2[:, :], scalar=page[:, u, D:D + 1],
                                                            in1=page[:, u, 0:D], op0=ALU.mult, op1=ALU.add))
                        link(nc.vector.bn_stats(st3[:, 0:6], z3[:, :]), own=True)
                        link(nc.vector.bn_aggr(st3[:, 6:8], st3[:, 0:6]))
                        nc.vector.tensor_scalar(st3[:, 8:9], st3[:, 7:8], EPS, None, ALU.add).then_inc(fvar_done, 1)
                        link(nc.vector.tensor_copy(idx[:, u:u + 1], page[:, u, D + 1:D + 2]))
                        if u == SLOTS - 1:
                            finish(g, u)
                    assert n_f[0] == F_PER, n_f[0]


def kernel(**inputs):
    import numpy as _np
    import concourse.bacc as _bacc
    from concourse import mybir as _mybir
    from concourse.bass_utils import run_bass_kernel_spmd as _run

    a = {k: _np.asarray(v) for k, v in inputs.items()}
    given = {
        "x": a["x"],
        "xT": a["x"].transpose(0, 2, 1),
        "ctxT": a["ctx_1024"].transpose(0, 2, 1),
        "winT": a["L0_attn_W_in"].T,
        "wattnT": a["L0_attn_W_attn"].T,
        "woutT": a["L0_attn_W_out"].T,
        "scale_w": a["L0_attn_scale_weights"],
        "wg": a["L0_ffn_Wg"],
        "bg": a["L0_ffn_bg"],
        "w1": a["L0_ffn_W1"],
        "b1": a["L0_ffn_b1"],
        "w2": a["L0_ffn_W2"],
        "b2": a["L0_ffn_b2"],
    }
    nc = _bacc.Bacc("TRN2", target_bir_lowering=False, num_devices=1)
    arrays, args = {}, []
    for name, v in given.items():
        v = _np.ascontiguousarray(v)
        arrays[f"in_{name}"] = v
        args.append(nc.dram_tensor(f"in_{name}", v.shape, _mybir.dt.from_np(v.dtype), kind="ExternalInput").ap())
    args.append(nc.dram_tensor("out", a["x"].shape, _mybir.dt.from_np(_np.dtype("float32")), kind="ExternalOutput").ap())
    decoder_layer(nc, *args)
    r = _run(nc, [arrays], core_ids=[0])
    return r.results[0]["out"]
```

```python
from contextlib import ExitStack

import numpy as np
import concourse.bass as bass
from concourse import mybir

F32 = mybir.dt.float32
F16 = mybir.dt.float16
I32 = mybir.dt.int32
ALU = mybir.AluOpType
ACT = mybir.ActivationFunctionType
AX = mybir.AxisListType.X

P = 128
EPS = 1e-5
WEIGHT_SCALE = 64.0
SCORE_SCALE = 1.0 / 16.0
RING = 4


def decoder_layer(nc, x, xT, ctxT, winT, wattnT, woutT, scale_w, wg, bg, w1, b1, w2, b2, out):
    B, T, D = x.shape
    E = wg.shape[1]
    NT = T // P
    DC = D // P
    NTOK = B * T
    SIZES = (21, 41)
    HEADS = 8
    HD = D // HEADS
    C0, C1 = SIZES
    L0, L1 = HEADS * C0, HEADS * C1
    NL = L0 + L1
    L1_AT = HEADS * C1
    assert wattnT.shape[1] == 2 * HEADS * C1 and NT == 8 and DC == 4

    SIDE = 32
    BAND = P + 2 * SIDE
    SHIFT = SIDE - (C1 - 1) // 2
    BROW = HEADS * BAND
    SKEW = BROW + 1

    REGION = NTOK + P
    SLOTS = 8
    GROUPS = -(-(NTOK // P + E - 1) // SLOTS)
    PAGES = GROUPS * SLOTS
    TAB = (GROUPS + 1) * SLOTS
    ROWS = E * REGION + P
    ROWLEN = D + 4
    NO_TOKEN = 2 * NTOK

    skew_dram = nc.dram_tensor("skew_dram", (2, P * SKEW), F32, kind="Internal").ap()
    sorted_dram = nc.dram_tensor("sorted_dram", (ROWS, ROWLEN), F32, kind="Internal").ap()

    wsplit_dram = nc.dram_tensor("wsplit_dram", (E, DC, P, 4 * D), F16, kind="Internal").ap()
    wsplit_rows = wsplit_dram.rearrange("e c p n -> (e c p) n")

    out_rows = out.rearrange("b t d -> (b t) d")

    ctx = ExitStack()
    with ctx:
        def sb(name, shape, dt, stack=ctx):
            return stack.enter_context(nc.sbuf_tensor(name, shape, dt))

        def sem(name):
            return ctx.enter_context(nc.semaphore(name))

        banks = [ctx.enter_context(nc.psum_tensor(f"bank{i}", [P, 512], F32)) for i in range(8)]

        EXPERT = DC * 4 * D
        W_AT = (nc.sbuf_top - 2 * E * EXPERT) // 32 * 32
        ws = nc.alloc_sbuf_tensor_at("ws", [P, E * EXPERT], F16, offset=W_AT)
        EARLY_E = 2
        early_in = sem("early_in")
        late_in = sem("late_in")

        def load_expert(eng, e):
            o = (E - 1 - e) * EXPERT
            eng.dma_start(ws[:, o:o + EXPERT].rearrange("p (c n) -> p c n", c=DC),
                          wsplit_dram[e, :, :, :].rearrange("c p n -> p c n")).then_inc(early_in if e < EARLY_E else late_in, 16)

        ident = sb("ident", [P, P], F32)
        ident16 = sb("ident16", [P, P], F16)
        half_neg = sb("half_neg", [P, 1], F32)
        row_tab = sb("row_tab", [P, TAB], I32)
        expert_tab = sb("expert_tab", [P, GROUPS], I32)

        def page_rows(g):
            return nc.values_load_multi_w_load_instructions(row_tab[0:1, bass.ds(g * SLOTS, SLOTS)], engines=(mybir.EngineType.SP,),
                                                            min_val=0, max_val=ROWS - P)[1]

        first_pages = []
        EXPERT_BITS = 3
        assert E == 1 << EXPERT_BITS and EXPERT_BITS * SLOTS <= 24

        def experts(eng, g):
            packed = eng.value_load(expert_tab[0:1, bass.ds(g, 1)], min_val=0, max_val=(1 << EXPERT_BITS * (SLOTS + 1)) - 1)
            return [eng.snap((packed >> (EXPERT_BITS * u)) & (E - 1), min_val=0, max_val=E - 1) for u in range(SLOTS + 1)]

        FRONT_W = 2 * DC * (D + NL)
        shared = sb("shared", [P, max(FRONT_W, 2 * E * D) + 2 * DC * T], F16)
        b1s = shared[:, 0:2 * E * D].bitcast(F32)
        KT_AT = max(FRONT_W, 2 * E * D)
        b2s = shared[:, KT_AT:KT_AT + 2 * E * D].bitcast(F32)
        assert DC * T == E * D
        bias_in = sem("bias_in")

        mix = ExitStack()
        with mix:
            def mb(name, shape, dt):
                return sb(name, shape, dt, mix)

            win = shared[:, 0:2 * DC * D].rearrange("p (k c n) -> p k c n", k=2, c=DC)
            wattn = shared[:, 2 * DC * D:FRONT_W].rearrange("p (k c n) -> p k c n", k=2, c=DC)
            wout = mb("wout", [P, 2, DC, D], F16)
            wg_sb = mb("wg_sb", [P, DC, E], F32)
            bg_sb = mb("bg_sb", [P, E], F32)
            sw_sb = mb("sw_sb", [P, 2], F32)
            sw_tmp = mb("sw_tmp", [P, 4], F32)
            XT = mb("XT", [P, 2, 4, DC, P], F16)
            KT = shared[:, KT_AT:KT_AT + 2 * DC * T].rearrange("p (k c t) -> p k c t", k=2, c=DC)
            stage = mb("stage", [P, 2, 1024], F32)
            xstage = mb("xstage", [P, DC, P], F32)
            kstage = mb("kstage", [P, DC, P], F32)
            ehalf = mb("ehalf", [P, 2, 2, 2 * D], F16)
            xrow = mb("xrow", [P, 4, D], F32)
            xi = mb("xi", [P, 4, 2, D], F16)
            rT = mb("rT", [P, 2, DC, P], F16)
            ee = mb("ee", [P, NL], F32)
            mx = mb("mx", [P, 2, HEADS], F32)
            sm = mb("sm", [P, 2, HEADS], F32)
            t0 = mb("t0", [P, HEADS, C0], F32)
            wwin = mb("wwin", [P, 2, HEADS, C1], F32)
            band = mb("band", [P, 2, SIDE + BROW + SIDE], F32)
            xc = mb("xc", [2 * SIDE, 2, 2, D], F16)
            bt = mb("bt", [P, 2, HEADS, P], F16)
            bs = mb("bs", [2 * SIDE, 2, HEADS + 1, 2, SIDE], F16)
            oT = mb("oT", [P, 2, DC, P], F16)
            z = mb("z", [P, D], F32)
            st = mb("st", [P, 12], F32)
            y1 = mb("y1", [P, 4, D], F32)
            y1s = mb("y1s", [P, NT, 2, D], F16)
            NBLK = NT * (NT + 1) // 2
            PT = mb("PT", [P, 2, NBLK * P], F16)
            yrow = mb("yrow", [P, 4, ROWLEN], F32)
            yT = mb("yT", [P, DC, P], F32)
            lg = mb("lg", [P, E], F32)
            less_top = mb("less_top", [P, E], F32)
            rexp = mb("rexp", [P, E], F32)
            rden = mb("rden", [P, 1], F32)
            rkey = mb("rkey", [P, E], F32)
            rmin = mb("rmin", [P, 1], F32)
            onehot = mb("onehot", [P, E], F16)
            place = mb("place", [P, 2, E], F32)
            placef = mb("placef", [P, 1], F32)
            filled = mb("filled", [P, E], F32)
            slot = mb("slot", [P, 4], I32)
            e_less = mb("e_less", [P, E], F32)
            tri = mb("tri", [P, P], F16)
            ones = mb("ones", [P, P], F16)
            zrow = mb("zrow", [P, ROWLEN], F32)
            pad_row = mb("pad_row", [P, E], I32)
            region0 = mb("region0", [P, E], F32)
            pages = mb("pages", [P, 4, E], F32)
            pages_i = mb("pages_i", [P, 2, E], I32)
            karr = mb("karr", [P, TAB], F32)
            expert_scale = mb("expert_scale", [P, SLOTS], F32)
            placed = mb("placed", [P, GROUPS + 1], F32)
            packed_i = mb("packed_i", [P, 2, GROUPS + 1], I32)
            passed = stage[:, :, :].rearrange("p a n -> p (a n)")[:, 0:2 * TAB * E].rearrange("p (k n e) -> p k n e", k=2, e=E)
            tabf = kstage[:, 0:2, 0:TAB]

            first_early = W_AT + 2 * (E - EARLY_E) * EXPERT
            assert nc.sbuf_base <= first_early, (nc.sbuf_base, first_early)

            passed_wait = sem("passed_wait")
            consts = sem("consts")
            consts_in = sem("consts_in")
            zero_out = sem("zero_out")
            stage_in = [sem(f"stage_in{i}") for i in range(6)]
            split_h = sem("split_h")
            split_l = sem("split_l")
            xt_in = sem("xt_in")
            kt_in = sem("kt_in")
            xt_h = sem("xt_h")
            xt_l = sem("xt_l")
            kt_h = sem("kt_h")
            kt_l = sem("kt_l")
            e_in = [sem("e_in0"), sem("e_in1")]
            e_h = sem("e_h")
            e_l = sem("e_l")
            e_out = [sem("e_out0"), sem("e_out1")]
            x_in = [sem(f"x_in{i}") for i in range(4)]
            xi_ready = sem("xi_ready")
            xih_done = sem("xih_done")
            xil_done = sem("xil_done")
            xit_ready = sem("xit_ready")
            rth_done = sem("rth_done")
            rt_done = sem("rt_done")
            logits_ready = sem("logits_ready")
            lsub_done = sem("lsub_done")
            exp_done = sem("exp_done")
            inv_done = sem("inv_done")
            wsum_done = sem("wsum_done")
            skew_out = [sem("skew_out0"), sem("skew_out1")]
            band_in = [sem("band_in0"), sem("band_in1")]
            xc_done = sem("xc_done")
            outT_ready = sem("outT_ready")
            oth_done = sem("oth_done")
            otl_done = sem("otl_done")
            prod_ready = sem("prod_ready")
            z_done = sem("z_done")
            var_done = sem("var_done")
            rstd_done = sem("rstd_done")
            y1_done = sem("y1_done")
            y1h_done = sem("y1h_done")
            y1l_done = sem("y1l_done")
            masked = sem("masked")
            y2_done = sem("y2_done")
            ring_full = sem("ring_full")
            ring_h = sem("ring_h")
            ring_done = sem("ring_done")
            dve_chain = sem("dve_chain")
            pool_chain = sem("pool_chain")
            rlog_done = sem("rlog_done")
            rexp_done = sem("rexp_done")
            onehot_done = sem("onehot_done")
            slot_done = sem("slot_done")
            rows_out = [sem(f"rows_out{i}") for i in range(4)]
            pads_known = sem("pads_known")
            tables_done = sem("tables_done")
            pads_out = sem("pads_out")

            PT_stage = PT[:, :, :].rearrange("p k n -> p (k n)").bitcast(F32)
            STAGES = 6

            KT_tiles = KT[:, :, :, :].rearrange("p k c (j t) -> p k j c t", t=P)

            def w_piece(src, buf, c, cols):
                return ("w", src, buf[:, 0, c:c + 2, :], buf[:, 1, c:c + 2, :], c, cols)

            def t_piece(src, buf, tile_, slot_):
                return ("t", src, buf[:, 0, slot_, :, :], buf[:, 1, slot_, :, :], tile_, None)

            WIN = [w_piece(winT, win, c, ((0, 0, D),)) for c in range(0, DC, 2)]
            WATTN = [w_piece(wattnT, wattn, c, ((0, 0, L0), (L1_AT, L0, L1))) for c in range(0, DC, 2)]
            WOUT = [w_piece(woutT, wout, c, ((0, 0, D),)) for c in range(0, DC, 2)]
            XLEAD = 3
            KTP = [t_piece(ctxT, KT_tiles, i, i) for i in range(NT)]
            piece_groups = [WIN + [t_piece(xT, XT, i, i) for i in range(XLEAD)] + WATTN,
                            WOUT + KTP[0:2], KTP[2:5], KTP[5:8]]
            pieces = sum(piece_groups, [])
            group_at = [sum(len(g) for g in piece_groups[:k]) for k in range(len(piece_groups) + 1)]
            assert len(piece_groups) - 1 <= 3
            X0_SPLIT = len(WIN) + 1
            WATTN_SPLIT = len(WIN) + XLEAD + len(WATTN)
            WOUT_SPLIT = group_at[1] + len(WOUT)

            def piece_slot(n):
                return n if n < 2 else 2 + (n - 2) % 4

            slot_level = [0] * STAGES
            piece_level = []
            for n, p in enumerate(pieces):
                slot_level[piece_slot(n)] += 16 * (len(p[5]) if p[0] == "w" else 1)
                piece_level.append(slot_level[piece_slot(n)])

            def staged(n):
                p, k = pieces[n], piece_slot(n)
                buf = stage[:, k, :] if k < 2 else PT_stage[:, (k - 2) * 1024:(k - 1) * 1024]
                if p[0] == "t":
                    return buf[:, 0:DC * P].rearrange("p (c t) -> p c t", c=DC), 1.0
                w = sum(x[2] for x in p[5])
                return buf[:, 0:2 * w].rearrange("p (c n) -> p c n", c=2), WEIGHT_SCALE

            SOFT = 1
            BACK = 2
            MIX = 3
            GATE = 4
            ROUTE = 5
            TAIL = ROUTE

            def tile(s, b, phase, lag=0):
                i = s - lag
                if phase == "last":
                    return (i, b) if 0 <= i < NT else None
                if i >= 0:
                    return i, b
                return (i + NT, b - 1) if phase == "loop" else None

            def steps(eng, step):
                for s in range(NT):
                    step(s, 0, "first")
                mark = counts()
                with eng.Fori(1, B) as b:
                    restart(mark, b)
                    for s in range(NT):
                        step(s, b, "loop")
                    per = per_loop(mark)
                end_loop(mark, per)
                for s in range(NT, NT + TAIL):
                    step(s, B - 1, "last")

            chain = {"n": 0, "base": 0}
            CHAIN_PER = {"dve": 152, "pool": 8, "none": 0}

            def counts():
                return chain["n"]

            def restart(mark, b):
                chain["base"] = (b - 1) * CHAIN_PER[chain["who"]]

            def per_loop(mark):
                return chain["n"] - mark

            def end_loop(mark, per):
                if per:
                    assert per == CHAIN_PER[chain["who"]], per
                    chain["base"] = (B - 2) * per

            def linked(eng, signal, ins, own=False):
                chain["n"] += 1
                ins.then_inc(signal, 1)
                eng.wait_ge(signal, chain["base"] + chain["n"])
                if own:
                    alone(eng)

            def at(b, k, m=1):
                return b * (NT * m) + (k * m + 1)

            def dma_at(b, i, n):
                return b * (16 * NT // n) + 16 * (i // n + 1)

            class Order:

                def __init__(self, of):
                    self.at = {}
                    self.size = {}
                    for phase, r in (("first", range(NT)), ("loop", range(NT)), ("last", range(NT, NT + TAIL))):
                        n = 0
                        for s in r:
                            for it in of(s, phase):
                                self.at[(phase, s) + it] = n
                                n += 1
                        self.size[phase] = n

                def number(self, phase, s, b, *it):
                    n = self.at[(phase, s) + it]
                    if phase == "first":
                        return n
                    loops = b - 1 if phase == "loop" else b
                    return loops * self.size["loop"] + (self.size["first"] + n)

                def done(self, phase, s, b, *it):
                    return self.number(phase, s, b, *it) + 2

                def all_before(self, phase, s, b):
                    it = min((n, key[2:]) for key, n in self.at.items() if key[:2] == (phase, s))[1]
                    return self.number(phase, s, b, *it) + 1

                def before(self, eng, signal, back, phase, s, b, *it):
                    n = self.number(phase, s, b, *it)
                    if not isinstance(n, int) or n >= back:
                        eng.wait_ge(signal, n - back + 2)

            SCORE_WIDTHS = [(512, 512), (384, 512), (256, 512), (128, 512), (256, 256), (128, 128, 128), (128, 128), (128,)]

            def score_pieces(j):
                widths = SCORE_WIDTHS[j]
                assert sum(widths) == (NT - j) * P
                return [(sum(widths[:n]), w) for n, w in enumerate(widths)]

            BAND_ITEMS = [("own", h, 4) for h in range(0, HEADS, 4)] + [("sides", j, min(4, HEADS + 1 - j)) for j in range(0, HEADS + 1, 4)]
            EARLY = 4

            def band_views(n, bank):
                kind, j0, k = BAND_ITEMS[n]
                blocks = bank[:, 0:k * P].rearrange("p (j t) -> p j t", j=k)
                if kind == "own":
                    return [blocks] + [bt[:, a, j0:j0 + k, :] for a in range(2)]
                src = bank[0:2 * SIDE, 0:k * P].rearrange("p (j a t) -> p j a t", j=k, t=SIDE)[:, :, 0:4:3, :]
                return [src] + [bs[:, a, j0:j0 + k, :, :] for a in range(2)]

            def ring_of(s, phase):
                items = []
                if tile(s, 1, phase, BACK):
                    items += [("band", n) for n in range(len(BAND_ITEMS))]
                if tile(s, 1, phase, GATE):
                    items.append(("y2T", 0))
                if tile(s, 1, phase, ROUTE):
                    items.append(("rank", 0))
                if t := tile(s, 1, phase, MIX):
                    items += [("scores", n) for n in range(len(score_pieces(t[0])))]
                if tile(s, 1, phase, GATE):
                    items.append(("gate", 0))
                return items

            def split_of(s, phase):
                return [it for it in ring_of(s, phase) if it[0] in ("band", "scores")]

            def prods_of(s, phase):
                return [(w,) for w, lag in (("mix", MIX), ("wout", BACK)) if tile(s, 1, phase, lag)]

            ring, splits, prods = Order(ring_of), Order(split_of), Order(prods_of)
            BLK = [sum(NT - jj for jj in range(j)) for j in range(NT)]

            def ring_bank(phase, s, *it):
                n = ring.at[(phase, s) + it]
                if phase != "first":
                    n += ring.size["first"]
                assert ring.size["loop"] % RING == 0
                return banks[2 + n % RING]

            def alone(eng):
                eng.sem_inc(passed_wait, 1)

            xi_bank, logit_bank, outT_bank, prod_bank = banks[0], banks[1], banks[6], banks[7]
            xit = xi_bank[:, :].bitcast(F16).rearrange("p (k c t) -> p k c t", k=2, c=DC)
            outT = outT_bank[:, :].rearrange("p (c t) -> p c t", c=DC)

            assert E == 2 * B and NT == 2 * DC
            w1_rows = w1.rearrange("e d n -> (e d) n")
            w2_rows = w2.rearrange("e d n -> (e d) n")

            block = mix.enter_context(nc.Block())

            @block.sync
            def _(sp):
                chain.update(n=0, base=0, who="none")
                def load_pieces(group):
                    for n in range(group_at[group], group_at[group + 1]):
                        kind, src, _, _, c, cols = pieces[n]
                        if n >= STAGES:
                            sp.wait_ge(split_l, n - 3)
                        dst, _ = staged(n)
                        if kind == "t":
                            sp.dma_start(dst, src[0, :, c * P:(c + 1) * P].rearrange("(c p) t -> p c t", p=P)
                                         ).then_inc(stage_in[piece_slot(n)], 16)
                        else:
                            for s0, d0, k in cols:
                                sp.dma_start(dst[:, :, d0:d0 + k],
                                             src[c * P:(c + 2) * P, s0:s0 + k].rearrange("(c p) n -> p c n", p=P)
                                             ).then_inc(stage_in[piece_slot(n)], 16)
                        if n == 2:
                            sp.dma_start(sw_sb[:, :], scale_w.rearrange("(a n) -> a n", a=1).broadcast_to([P, 2])).then_inc(consts_in, 16)
                            sp.dma_start(bg_sb[:, :], bg.rearrange("(a n) -> a n", a=1).broadcast_to([P, E])).then_inc(consts_in, 16)
                            sp.dma_start(wg_sb[:, :, :], wg.rearrange("(c p) e -> p c e", p=P)).then_inc(consts_in, 16)

                load_pieces(0)
                sp.wait_ge(consts, 1)
                for k in range(2):
                    sp.dma_start(skew_dram[k, :].rearrange("(p n) -> p n", p=P), band[:, k, 0:SKEW]).then_inc(zero_out, 16)
                sp.dma_start(sorted_dram[E * REGION:ROWS, :], zrow[:, :]).then_inc(zero_out, 16)
                sp.wait_ge(split_l, 2)

                x_rows = x.rearrange("b t d -> (b t) d")
                xT_rows = xT.rearrange("b d t -> (b d) t")
                ctxT_rows = ctxT.rearrange("b d t -> (b d) t")

                def step(s, b, phase):
                    if t := tile(s, b, phase):
                        i, tb = t
                        ahead = i + XLEAD
                        rows = (b if ahead < NT else (b + 1) % B) * D
                        if phase == "loop" or s > 0:
                            sp.wait_ge(xt_l, at(b, s))
                        alone(sp)
                        sp.dma_start(xstage[:, :, :], xT_rows[bass.ds(rows, D), (ahead % NT) * P:(ahead % NT + 1) * P]
                                     .rearrange("(c p) t -> p c t", p=P)).then_inc(xt_in, 16)
                        if kt := tile(s, b, phase, MIX):
                            j, jb = kt
                            if phase == "loop" or j > 0:
                                sp.wait_ge(kt_l, at(jb, j))
                            alone(sp)
                            sp.dma_start(kstage[:, :, :], ctxT_rows[bass.ds(((jb + 1) % B) * D, D), j * P:(j + 1) * P]
                                         .rearrange("(c p) t -> p c t", p=P)).then_inc(kt_in, 16)
                        if phase == "loop" or s >= 2:
                            sp.wait_ge(e_l, at(b, s - 1))
                        alone(sp)
                        row = (b * 2 + s // DC) * D + (s % DC) * P
                        for k, w_rows in enumerate((w1_rows, w2_rows)):
                            sp.dma_start(stage[:, s % 2, k * D:(k + 1) * D], w_rows[bass.ds(row, P), :]).then_inc(e_in[s % 2], 16)
                        if phase == "loop" or i >= 4:
                            sp.wait_ge(y1_done, at(b, i - 3))
                            alone(sp)
                        sp.dma_start(xrow[:, i % 4, :], x_rows[bass.ds(b * T + i * P, P), :]).then_inc(x_in[i % 4], 16)
                        if phase == "first" and s + 1 < len(piece_groups):
                            load_pieces(s + 1)
                    if t := tile(s, b, phase, SOFT):
                        i, tb = t
                        if phase == "first" and i == 0:
                            sp.wait_ge(zero_out, 48)
                        sp.wait_ge(wsum_done, at(tb, i + 1))
                        alone(sp)
                        if phase != "first" or i >= 2:
                            sp.wait_ge(band_in[i % 2], dma_at(tb, i - 2, 2))
                        alone(sp)
                        rows = skew_dram[i % 2, :].rearrange("(t n) -> t n", n=SKEW)[:, 0:BROW]
                        sp.dma_start(rows.rearrange("t (h n) -> t h n", h=HEADS)[:, :, SHIFT:SHIFT + C1],
                                     wwin[:, i % 2, :, :]).then_inc(skew_out[i % 2], 16)
                        sp.wait_ge(skew_out[i % 2], dma_at(tb, i, 2))
                        alone(sp)
                        if phase != "first" or i >= 2:
                            sp.wait_ge(outT_ready, at(tb, i - 1))
                            alone(sp)
                        flat = skew_dram[i % 2, 0:P * BROW].rearrange("(t n) -> t n", n=BROW)
                        sp.dma_start(band[:, i % 2, SIDE:SIDE + BROW], flat).then_inc(band_in[i % 2], 16)
                    if tile(s, b, phase):
                        sp.wait_ge(e_l, at(b, s + 1))
                        alone(sp)
                        sp.dma_start(wsplit_rows[bass.ds(row, P), :], ehalf[:, s % 2, :, :].rearrange("p k n -> p (k n)")
                                     ).then_inc(e_out[s % 2], 16)
                    if phase == "last" and s < NT + EARLY_E:
                        if s == NT:
                            for k in range(2):
                                sp.wait_ge(e_out[k], 16 * (B * NT // 2))
                        load_expert(sp, s - NT)
                    for last_use, dst, src in ((NT, b1s, b1), (NT + MIX - 1, b2s, b2)):
                        if phase == "last" and s == last_use:
                            if s == NT:
                                sp.wait_ge(logits_ready, at(b, NT))
                            else:
                                sp.wait_ge(ring_full, ring.done(phase, s, b, "scores", len(score_pieces(NT - 1)) - 1))
                            sp.dma_start(dst, src.rearrange("e n -> (e n)").rearrange("(a n) -> a n", a=1).broadcast_to([P, E * D])
                                         ).then_inc(bias_in, 16)

                steps(sp, step)
                sp.wait_ge(pads_known, 1)
                pad_rows = nc.values_load_multi_w_load_instructions(pad_row[0:1, :], engines=(mybir.EngineType.SP,),
                                                                    min_val=0, max_val=E * REGION - P)[1]
                for e in range(E):
                    sp.dma_start(sorted_dram[bass.ds(pad_rows[e], P), :], zrow[:, :]).then_inc(pads_out, 16)
                sp.wait_ge(tables_done, 1)
                first_pages.extend(page_rows(0))
                sp.wait_ge(pads_out, 16 * E)
                sp.wait_ge(xt_in, 16 * B * NT)
                sp.wait_ge(kt_in, 16 * (B * NT - MIX))

            @block.scalar
            def _(act):
                chain.update(n=0, base=0, who="none")
                for s_ in (xih_done, rth_done, exp_done, oth_done, y1h_done, ring_h, rexp_done, xt_h, kt_h, e_h):
                    act.sem_inc(s_, 1)
                def split_pieces(group):
                    for n in range(group_at[group], group_at[group + 1]):
                        act.wait_ge(stage_in[piece_slot(n)], piece_level[n])
                        src, scale = staged(n)
                        nc.scalar.activation(pieces[n][2], src, ACT.Copy, scale=scale).then_inc(split_h, 1)

                split_pieces(0)
                act.wait_ge(dve_chain, 2)
                nc.scalar.activation(sw_tmp[:, 2:4], sw_tmp[:, 0:2], ACT.Exp).then_inc(rexp_done, 1)

                def high(s, b, phase, kind, n, dst, src, scale):
                    act.wait_ge(ring_full, ring.done(phase, s, b, kind, n))
                    nc.scalar.activation(dst, src, ACT.Copy, scale=scale).then_inc(ring_h, 1)

                def step(s, b, phase):
                    def bands(lo, hi_):
                        for n in range(lo, hi_):
                            src, hi, _ = band_views(n, ring_bank(phase, s, "band", n))
                            high(s, b, phase, "band", n, hi, src, 1.0)

                    front, back = tile(s, b, phase), tile(s, b, phase, BACK)
                    if back:
                        bands(0, EARLY)
                    if front:
                        act.wait_ge(xi_ready, at(b, s + 1))
                        nc.scalar.activation(xi[:, s % 4, 0, :], xi_bank[:, :], ACT.Copy,
                                             scale=1.0 / WEIGHT_SCALE).then_inc(xih_done, 1)
                    if back:
                        bands(EARLY, len(BAND_ITEMS))
                    if t := tile(s, b, phase, MIX):
                        act.wait_ge(y1_done, at(t[1], t[0] + 1))
                        nc.scalar.activation(y1s[:, t[0], 0, :], y1[:, t[0] % 4, :], ACT.Copy).then_inc(y1h_done, 1)
                        for n, (c0, w) in enumerate(score_pieces(t[0])):
                            o = BLK[t[0]] * P + c0
                            high(s, b, phase, "scores", n, PT[:, 0, o:o + w], ring_bank(phase, s, "scores", n)[:, 0:w], SCORE_SCALE)
                    if front:
                        act.wait_ge(xit_ready, at(b, s + 1))
                        nc.scalar.activation(rT[:, 0, :, :], xit[:, 0, :, :], ACT.Relu).then_inc(rth_done, 1)
                    if back:
                        act.wait_ge(outT_ready, at(back[1], back[0] + 1))
                        nc.scalar.activation(oT[:, 0, :, :], outT, ACT.Copy).then_inc(oth_done, 1)
                    if front:
                        act.wait_ge(xt_in, b * (16 * NT) + 16 * (s + 1))
                        nc.scalar.activation(XT[:, 0, (s + XLEAD) % 4, :, :], xstage[:, :, :], ACT.Copy).then_inc(xt_h, 1)
                        if t := tile(s, b, phase, MIX):
                            act.wait_ge(kt_in, t[1] * (16 * NT) + 16 * (t[0] + 1))
                            nc.scalar.activation(KT_tiles[:, 0, t[0], :, :], kstage[:, :, :], ACT.Copy).then_inc(kt_h, 1)
                        act.wait_ge(e_in[s % 2], b * (16 * NT) + 32 * (s // 2 + 1))
                        if phase == "loop" or s >= 2:
                            act.wait_ge(e_out[s % 2], dma_at(b, s - 2, 2))
                        nc.scalar.activation(ehalf[:, s % 2, 0, :], stage[:, s % 2, :], ACT.Copy, scale=WEIGHT_SCALE).then_inc(e_h, 1)
                        act.wait_ge(lsub_done, at(b, s + 1, 2))
                        nc.scalar.activation(ee[:, :], ee[:, :], ACT.Exp, scale=1.0 / WEIGHT_SCALE).then_inc(exp_done, 1)
                        if phase == "first" and s + 1 < len(piece_groups):
                            split_pieces(s + 1)
                    if t := tile(s, b, phase, GATE):
                        act.wait_ge(rlog_done, at(t[1], t[0] + 1))
                        nc.scalar.activation(rexp[:, :], less_top[:, :], ACT.Exp).then_inc(rexp_done, 1)

                steps(act, step)

            @block.tensor
            def _(pe):
                chain.update(n=0, base=0, who="none")

                def split_product(dst, stat, mov, chunks, first=True, last=True):
                    n = 0
                    for c in range(chunks):
                        for a, m in ((0, 0), (0, 1), (1, 0)):
                            ins = nc.tensor.matmul(dst, stat(a, c), mov(m, c), start=(first and n == 0),
                                                   stop=(last and n == 3 * chunks - 1))
                            n += 1
                    return ins

                for s_ in (xi_ready, xit_ready, logits_ready, outT_ready, prod_ready, ring_full):
                    pe.sem_inc(s_, 1)
                pe.wait_ge(consts, 3)

                def step(s, b, phase):
                    def acquire(*it):
                        ring.before(pe, ring_done, RING, phase, s, b, *it)
                        return ring_bank(phase, s, *it)

                    def bands(lo, hi_):
                        i = back[0]
                        for n in range(lo, hi_):
                            kind, j0, k = BAND_ITEMS[n]
                            bank = acquire("band", n)
                            alone(pe)
                            for j in range(j0, j0 + k):
                                o = (j - j0) * P
                                if kind == "own":
                                    c0 = SIDE + j * BAND + SIDE
                                    ins = nc.tensor.transpose(bank[:, o:o + P], band[:, i % 2, c0:c0 + P], ident[:, :])
                                else:
                                    c0 = j * BAND
                                    ins = nc.tensor.transpose(bank[0:2 * SIDE, o:o + P], band[:, i % 2, c0:c0 + 2 * SIDE], ident[:, :])
                            ins.then_inc(ring_full, 1)

                    front, back = tile(s, b, phase), tile(s, b, phase, BACK)
                    mixed, gate, route = (tile(s, b, phase, lag) for lag in (MIX, GATE, ROUTE))
                    if back:
                        pe.wait_ge(band_in[back[0] % 2], dma_at(back[1], back[0], 2))
                        bands(0, EARLY)
                    if front:
                        if phase == "first" and s < XLEAD:
                            pe.wait_ge(split_l, X0_SPLIT + s)
                        else:
                            pe.wait_ge(xt_l, at(b, s - XLEAD + 1))
                        if phase == "loop" or s > 0:
                            pe.wait_ge(rt_done, at(b, s))
                        split_product(xi_bank[:, :], lambda a, c: XT[:, a, s % 4, c, :],
                                      lambda m, c: win[:, m, c, :], DC).then_inc(xi_ready, 1)
                    if back:
                        bands(EARLY, len(BAND_ITEMS))
                    if gate:
                        pe.wait_ge(y2_done, at(gate[1], gate[0] + 1))
                        bank = acquire("y2T", 0)
                        for c in range(DC):
                            ins = nc.tensor.transpose(bank[:, c * P:(c + 1) * P], yrow[:, gate[0] % 4, c * P:(c + 1) * P], ident[:, :])
                        ins.then_inc(ring_full, 1)
                    if route:
                        pe.wait_ge(onehot_done, at(route[1], route[0] + 1))
                        bank = acquire("rank", 0)
                        nc.tensor.matmul(bank[:, 0:E], tri[:, :], onehot[:, :], start=True, stop=True)
                        nc.tensor.matmul(bank[:, E:2 * E], ones[:, :], onehot[:, :], start=True, stop=True).then_inc(ring_full, 1)
                    if mixed:
                        j = mixed[0]
                        if phase == "first":
                            pe.wait_ge(split_l, len(pieces))
                        else:
                            pe.wait_ge(kt_l, at(mixed[1] - 1, NT))
                        for n, (c0, w) in enumerate(score_pieces(j)):
                            bank = acquire("scores", n)
                            t0_ = j * P + c0
                            split_product(bank[:, 0:w], lambda a, c: KT[:, a, c, j * P:(j + 1) * P],
                                          lambda m, c: KT[:, m, c, t0_:t0_ + w], DC).then_inc(ring_full, 1)
                    if front:
                        pe.wait_ge(xil_done, at(b, s + 1))
                        for k in range(2):
                            for c in range(DC):
                                ins = nc.tensor.transpose(xit[:, k, c, :], xi[:, s % 4, k, c * P:(c + 1) * P], ident16[:, :])
                        ins.then_inc(xit_ready, 1)
                    if back:
                        i, tb = back
                        pe.wait_ge(ring_done, ring.done(phase, s, b, "band", len(BAND_ITEMS) - 1))
                        pe.wait_ge(xc_done, at(tb, i + 1))
                        if phase != "first" or i > 0:
                            pe.wait_ge(otl_done, at(tb, i))

                        def side_cols(m, h):
                            flat = bs[:, m, :, :, :].rearrange("p j a t -> p (j a) t")
                            return flat[:, 2 * h:2 * h + 4:3, :]

                        for h in range(HEADS):
                            q = HD * (h % 2)
                            dst = outT[q:q + HD, h // 2, :]
                            split_product(dst, lambda a, c: xi[:, i % 4, a, h * HD:(h + 1) * HD],
                                          lambda m, c: bt[:, m, h, :], 1, last=False)
                            sides = dst.rearrange("p (a n) -> p a n", n=SIDE)[:, 0:4:3, :]
                            ins = split_product(sides, lambda a, c: xc[:, i % 2, a, h * HD:(h + 1) * HD],
                                                lambda m, c: side_cols(m, h), 1, first=False)
                        ins.then_inc(outT_ready, 1)
                    if mixed:
                        i, tb = mixed
                        prods.before(pe, z_done, 1, phase, s, b, "mix")

                        def mix_product(js, **kw):
                            return split_product(prod_bank[:, :],
                                                 lambda a, c: PT[:, a, (BLK[js[c]] + i - js[c]) * P:(BLK[js[c]] + i - js[c] + 1) * P],
                                                 lambda m, c: y1s[:, js[c], m, :], len(js), **kw)

                        if i > 0:
                            mix_product(range(i), last=False)
                        pe.wait_ge(y1l_done, at(tb, i + 1))
                        pe.wait_ge(masked, at(tb, i + 1))
                        mix_product([i], first=(i == 0)).then_inc(prod_ready, 1)
                    if front:
                        pe.wait_ge(rt_done, at(b, s + 1))
                        if phase == "first" and s == 0:
                            pe.wait_ge(split_l, WATTN_SPLIT)
                        else:
                            pe.wait_ge(lsub_done, at(b, s, 2))
                        split_product(logit_bank[:, 0:NL], lambda a, c: rT[:, a, c, :],
                                      lambda m, c: wattn[:, m, c, :], DC).then_inc(logits_ready, 1)
                    if gate:
                        pe.wait_ge(ring_done, ring.done(phase, s, b, "y2T", 0))
                        bank = acquire("gate", 0)
                        for c in range(DC):
                            ins = nc.tensor.matmul(bank[:, 0:E], yT[:, c, :], wg_sb[:, c, :], start=(c == 0), stop=(c == DC - 1))
                        ins.then_inc(ring_full, 1)
                    if back:
                        i, tb = back
                        if phase == "first" and i == 0:
                            pe.wait_ge(split_l, WOUT_SPLIT)
                        pe.wait_ge(otl_done, at(tb, i + 1))
                        prods.before(pe, z_done, 1, phase, s, b, "wout")
                        split_product(prod_bank[:, :], lambda a, c: oT[:, a, c, :],
                                      lambda m, c: wout[:, m, c, :], DC).then_inc(prod_ready, 1)

                pe.wait_ge(consts_in, 48)
                steps(pe, step)

            @block.gpsimd
            def _(pool):
                chain.update(n=0, base=0, who="pool")
                for s_ in (wsum_done, rstd_done, masked, xt_l, kt_l):
                    pool.sem_inc(s_, 1)

                def link(ins):
                    linked(pool, pool_chain, ins)

                link(nc.gpsimd.memset(zrow[:, :], 0.0))
                nc.gpsimd.memset(zrow[:, D + 1:D + 2], float(NO_TOKEN))
                link(nc.gpsimd.memset(band[:, :, :], 0.0))
                pool.sem_inc(consts, 1)
                link(nc.gpsimd.memset(ident[:, :], 0.0))
                link(nc.gpsimd.affine_select(out=ident[:, :], in_=ident[:, :], compare_op=ALU.not_equal, fill=1.0,
                                             base=0, pattern=[[-1, P]], channel_multiplier=1))
                nc.gpsimd.tensor_copy(ident16[:, :], ident[:, :])
                nc.gpsimd.memset(half_neg[:, :], -0.5)
                link(nc.gpsimd.memset(ones[:, :], 1.0))
                link(nc.gpsimd.affine_select(out=tri[:, :], in_=ones[:, :], compare_op=ALU.is_ge, fill=0.0,
                                             base=-1, pattern=[[1, P]], channel_multiplier=-1))
                pool.sem_inc(consts, 2)
                iota_kw = dict(allow_small_or_imprecise_dtypes=True)
                nc.gpsimd.iota(e_less[:, :], pattern=[[1, E]], base=-E, channel_multiplier=0, **iota_kw)
                nc.gpsimd.iota(region0[:, :], pattern=[[REGION, E]], base=0, channel_multiplier=0, **iota_kw)
                nc.gpsimd.iota(filled[:, :], pattern=[[REGION, E]], base=0, channel_multiplier=0, **iota_kw)
                nc.gpsimd.iota(karr[:, :], pattern=[[1, TAB]], base=0, channel_multiplier=0, **iota_kw)
                for u in range(SLOTS):
                    nc.gpsimd.memset(expert_scale[:, u:u + 1], float(E ** u))
                link(nc.gpsimd.memset(yrow[:, :, D:ROWLEN], 0.0))
                for i in range(4):
                    link(nc.gpsimd.iota(yrow[:, i, D + 1:D + 2], pattern=[[0, 1]], base=(i - 4) * P, channel_multiplier=1, **iota_kw))
                pool.sem_inc(consts, 1)

                def step(s, b, phase):
                    front, back, mixed, route = (tile(s, b, phase, lag) for lag in (0, BACK, MIX, ROUTE))

                    def rstd(level):
                        pool.wait_ge(var_done, level)
                        nc.gpsimd.tensor_tensor(st[:, 9:10], st[:, 8:9], half_neg[:, :], ALU.pow).then_inc(rstd_done, 1)

                    if mixed:
                        rstd(prods.done(phase, s, b, "mix") - 1)
                    if t := tile(s, b, phase, SOFT):
                        i, tb = t
                        pool.wait_ge(inv_done, at(tb, i + 1))
                        e0 = ee[:, 0:L0].rearrange("p (h c) -> p h c", h=HEADS)
                        e1 = ee[:, L0:NL].rearrange("p (h c) -> p h c", h=HEADS)
                        nc.gpsimd.tensor_tensor(t0[:, :, :], e0, sm[:, 0, :].unsqueeze(2).broadcast_to([P, HEADS, C0]), ALU.mult)
                        if phase != "first" or i >= 2:
                            pool.wait_ge(skew_out[i % 2], dma_at(tb, i - 2, 2))
                        link(nc.gpsimd.tensor_tensor(wwin[:, i % 2, :, :], e1, sm[:, 1, :].unsqueeze(2).broadcast_to([P, HEADS, C1]), ALU.mult))
                        win_mid = wwin[:, i % 2, :, (C1 - C0) // 2:(C1 + C0) // 2]
                        nc.gpsimd.tensor_tensor(win_mid, win_mid, t0[:, :, :], ALU.add).then_inc(wsum_done, 1)
                    if mixed:
                        pool.wait_ge(ring_done, ring.done(phase, s, b, "scores", 0))
                        alone(pool)
                        for k in range(2):
                            o = BLK[mixed[0]] * P
                            ins = nc.gpsimd.affine_select(out=PT[:, k, o:o + P], in_=PT[:, k, o:o + P],
                                                          compare_op=ALU.is_ge, fill=0.0, base=0,
                                                          pattern=[[1, P]], channel_multiplier=-1)
                        ins.then_inc(masked, 1)
                    if route:
                        i, tb = route
                        pool.wait_ge(slot_done, at(tb, i + 1))
                        alone(pool)
                        nc.gpsimd.indirect_dma_start(out=sorted_dram, out_offset=bass.IndirectOffsetOnAxis(ap=slot[:, i % 4:i % 4 + 1], axis=0),
                                                     in_=yrow[:, i % 4, :], in_offset=None).then_inc(rows_out[i % 4], 16)
                    if mixed:
                        rstd(prods.done(phase, s, b, "mix"))
                    if front:
                        pool.wait_ge(xt_h, at(b, s + 1))
                        nc.gpsimd.tensor_tensor(XT[:, 1, (s + XLEAD) % 4, :, :], xstage[:, :, :], XT[:, 0, (s + XLEAD) % 4, :, :],
                                                ALU.subtract).then_inc(xt_l, 1)
                        if t := tile(s, b, phase, MIX):
                            pool.wait_ge(kt_h, at(t[1], t[0] + 1))
                            nc.gpsimd.tensor_tensor(KT_tiles[:, 1, t[0], :, :], kstage[:, :, :], KT_tiles[:, 0, t[0], :, :],
                                                    ALU.subtract).then_inc(kt_l, 1)

                steps(pool, step)
                for i in range(4):
                    pool.wait_ge(rows_out[i], 16 * (B * NT // 4))

            @block.vector
            def _(dve):
                chain.update(n=0, base=0, who="dve")
                for s_ in (xil_done, xc_done, rt_done, lsub_done, inv_done, otl_done, z_done, var_done, y1_done, y1l_done,
                           y2_done, ring_done, rlog_done, onehot_done, slot_done, e_l):
                    dve.sem_inc(s_, 1)

                def link(ins, own=False):
                    linked(dve, dve_chain, ins, own)

                def split_pieces(group):
                    for n in range(group_at[group], group_at[group + 1]):
                        p = pieces[n]
                        dve.wait_ge(split_h, n + 1)
                        src, scale = staged(n)
                        nc.vector.scalar_tensor_tensor(out=p[3], in0=src, scalar=scale, in1=p[2], op0=ALU.mult,
                                                       op1=ALU.subtract).then_inc(split_l, 1)

                split_pieces(0)
                dve.wait_ge(consts_in, 48)
                link(nc.vector.reduce_max(st[:, 0:1], sw_sb[:, :], axis=AX))
                link(nc.vector.tensor_scalar(sw_tmp[:, 0:2], sw_sb[:, :], st[:, 0:1], None, ALU.subtract))
                dve.wait_ge(rexp_done, 2)
                link(nc.vector.reduce_sum(st[:, 1:2], sw_tmp[:, 2:4], axis=AX))
                link(nc.vector.reciprocal(st[:, 2:3], st[:, 1:2]))
                link(nc.vector.tensor_scalar(sw_sb[:, :], sw_tmp[:, 2:4], st[:, 2:3], None, ALU.mult))
                dve.wait_ge(consts, 4)

                ls = [logit_bank[:, 0:L0].rearrange("p (h c) -> p h c", h=HEADS),
                      logit_bank[:, L0:NL].rearrange("p (h c) -> p h c", h=HEADS)]
                es = [ee[:, 0:L0].rearrange("p (h c) -> p h c", h=HEADS),
                      ee[:, L0:NL].rearrange("p (h c) -> p h c", h=HEADS)]

                def step(s, b, phase):
                    front, back = tile(s, b, phase), tile(s, b, phase, BACK)
                    mixed, gate, route = (tile(s, b, phase, lag) for lag in (MIX, GATE, ROUTE))

                    def bands(lo, hi_):
                        for n in range(lo, hi_):
                            dve.wait_ge(ring_h, splits.done(phase, s, b, "band", n))
                            src, hi, low = band_views(n, ring_bank(phase, s, "band", n))
                            nc.vector.tensor_tensor(low, src, hi, ALU.subtract).then_inc(ring_done, 1)

                    def moments(level, eps):
                        dve.wait_ge(z_done, level)
                        link(nc.vector.bn_stats(st[:, 0:6], z[:, :]), own=True)
                        link(nc.vector.bn_aggr(st[:, 6:8], st[:, 0:6]))
                        nc.vector.tensor_scalar(st[:, 8:9], st[:, 7:8], eps, None, ALU.add).then_inc(var_done, 1)

                    def normalize(level, to):
                        dve.wait_ge(rstd_done, level)
                        return nc.vector.tensor_scalar(to, z[:, :], st[:, 6:7], st[:, 9:10], ALU.subtract, ALU.mult)

                    if back:
                        bands(0, EARLY)
                    if mixed:
                        i, tb = mixed
                        wout_prod = prods.done(phase, s, b, "mix") - 1
                        dve.wait_ge(prod_ready, wout_prod)
                        dve.wait_ge(x_in[i % 4], dma_at(tb, i, 4))
                        if gate:
                            dve.wait_ge(y2_done, at(gate[1], gate[0] + 1))
                        nc.vector.scalar_tensor_tensor(out=z[:, :], in0=prod_bank[:, :], scalar=1.0 / WEIGHT_SCALE, in1=xrow[:, i % 4, :],
                                                       op0=ALU.mult, op1=ALU.add).then_inc(z_done, 1)
                        moments(wout_prod, EPS)
                    if front:
                        dve.wait_ge(xih_done, at(b, s + 1))
                        nc.vector.scalar_tensor_tensor(out=xi[:, s % 4, 1, :], in0=xi_bank[:, :], scalar=1.0 / WEIGHT_SCALE,
                                                       in1=xi[:, s % 4, 0, :], op0=ALU.mult, op1=ALU.subtract).then_inc(xil_done, 1)
                    if back:
                        bands(EARLY, len(BAND_ITEMS))
                    if back:
                        i, tb = back
                        if phase != "first" or i >= 2:
                            dve.wait_ge(outT_ready, at(tb, i - 1))
                        dve.wait_ge(xil_done, at(tb, min(i + 2, NT)))
                        if i > 0:
                            link(nc.vector.tensor_copy(xc[SIDE:2 * SIDE, i % 2, :, :], xi[P - SIDE:P, (i - 1) % 4, :, :]))
                        else:
                            link(nc.vector.tensor_scalar(xc[SIDE:2 * SIDE, i % 2, :, :], xi[P - SIDE:P, i % 4, :, :], 0.0, None, ALU.mult))
                        if i < NT - 1:
                            ins = nc.vector.tensor_copy(xc[0:SIDE, i % 2, :, :], xi[0:SIDE, (i + 1) % 4, :, :])
                        else:
                            ins = nc.vector.tensor_scalar(xc[0:SIDE, i % 2, :, :], xi[0:SIDE, i % 4, :, :], 0.0, None, ALU.mult)
                        ins.then_inc(xc_done, 1)
                    if mixed:
                        i, tb = mixed
                        normalize(wout_prod, y1[:, i % 4, :]).then_inc(y1_done, 1)
                        dve.wait_ge(y1_done, at(tb, i + 1))
                    if gate:
                        dve.wait_ge(ring_full, ring.done(phase, s, b, "y2T", 0))
                        nc.vector.tensor_copy(yT[:, :, :].rearrange("p c t -> p (c t)"),
                                              ring_bank(phase, s, "y2T", 0)[:, :]).then_inc(ring_done, 1)
                    if route:
                        i, tb = route
                        bank = ring_bank(phase, s, "rank", 0)
                        dve.wait_ge(ring_full, ring.done(phase, s, b, "rank", 0))
                        link(nc.vector.tensor_tensor(place[:, 0, :], bank[:, 0:E], filled[:, :], ALU.add))
                        link(nc.vector.tensor_tensor(place[:, 1, :], place[:, 0, :], onehot[:, :], ALU.mult))
                        nc.vector.tensor_tensor(filled[:, :], bank[:, E:2 * E], filled[:, :], ALU.add).then_inc(ring_done, 1)
                    if t := tile(s, b, phase, SOFT):
                        i, tb = t
                        dve.wait_ge(exp_done, at(tb, i + 1))
                        for k in range(2):
                            link(nc.vector.reduce_sum(sm[:, k, :], es[k], axis=AX))
                        link(nc.vector.reciprocal(sm[:, :, :], sm[:, :, :]))
                        nc.vector.tensor_tensor(sm[:, :, :], sm[:, :, :], sw_sb[:, :].unsqueeze(2).broadcast_to([P, 2, HEADS]),
                                                ALU.mult).then_inc(inv_done, 1)
                    if route:
                        i, tb = route
                        link(nc.vector.reduce_sum(placef[:, :], place[:, 1, :], axis=AX))
                        link(nc.vector.tensor_copy(slot[:, i % 4:i % 4 + 1], placef[:, :]))
                        dve.wait_ge(rexp_done, at(tb, i + 1) + 1)
                        link(nc.vector.reduce_sum(rden[:, :], rexp[:, :], axis=AX))
                        link(nc.vector.reciprocal(yrow[:, i % 4, D:D + 1], rden[:, :]))
                        nc.vector.tensor_scalar(yrow[:, i % 4, D + 1:D + 2], yrow[:, i % 4, D + 1:D + 2], float(4 * P), None,
                                                ALU.add).then_inc(slot_done, 1)
                    if mixed:
                        i, tb = mixed
                        dve.wait_ge(y1h_done, at(tb, i + 1))
                        nc.vector.tensor_tensor(y1s[:, i, 1, :], y1[:, i % 4, :], y1s[:, i, 0, :], ALU.subtract).then_inc(y1l_done, 1)
                        for n, (c0, w) in enumerate(score_pieces(mixed[0])):
                            dve.wait_ge(ring_h, splits.done(phase, s, b, "scores", n))
                            o = BLK[mixed[0]] * P + c0
                            nc.vector.scalar_tensor_tensor(out=PT[:, 1, o:o + w], in0=ring_bank(phase, s, "scores", n)[:, 0:w],
                                                           scalar=SCORE_SCALE, in1=PT[:, 0, o:o + w],
                                                           op0=ALU.mult, op1=ALU.subtract).then_inc(ring_done, 1)
                    if front:
                        dve.wait_ge(rth_done, at(b, s + 1))
                        nc.vector.scalar_tensor_tensor(out=rT[:, 1, :, :], in0=rT[:, 0, :, :], scalar=0.0, in1=xit[:, 1, :, :],
                                                       op0=ALU.is_gt, op1=ALU.mult).then_inc(rt_done, 1)
                    if back:
                        dve.wait_ge(oth_done, at(back[1], back[0] + 1))
                        nc.vector.tensor_tensor(oT[:, 1, :, :], outT, oT[:, 0, :, :], ALU.subtract).then_inc(otl_done, 1)
                    if front:
                        dve.wait_ge(e_h, at(b, s + 1))
                        nc.vector.scalar_tensor_tensor(out=ehalf[:, s % 2, 1, :], in0=stage[:, s % 2, :], scalar=WEIGHT_SCALE,
                                                       in1=ehalf[:, s % 2, 0, :], op0=ALU.mult, op1=ALU.subtract).then_inc(e_l, 1)
                    if mixed:
                        i, tb = mixed
                        dve.wait_ge(prod_ready, prods.done(phase, s, b, "mix"))
                        nc.vector.scalar_tensor_tensor(out=z[:, :], in0=prod_bank[:, :], scalar=0.5 / SCORE_SCALE, in1=y1[:, i % 4, :],
                                                       op0=ALU.mult, op1=ALU.add).then_inc(z_done, 1)
                        if phase != "first" or i >= 4:
                            dve.wait_ge(rows_out[i % 4], dma_at(tb, i - 4, 4))
                        moments(prods.done(phase, s, b, "mix"), EPS / 4)
                        normalize(prods.done(phase, s, b, "mix"), yrow[:, i % 4, 0:D]).then_inc(y2_done, 1)
                    if front:
                        dve.wait_ge(logits_ready, at(b, s + 1))
                        for k in range(2):
                            link(nc.vector.reduce_max(mx[:, k, :], ls[k], axis=AX))
                        if phase == "loop" or s > 0:
                            dve.wait_ge(wsum_done, at(b, s))
                        for k in range(2):
                            nc.vector.tensor_tensor(es[k], ls[k], mx[:, k, :].unsqueeze(2).broadcast_to([P, HEADS, SIZES[k]]),
                                                    ALU.subtract).then_inc(lsub_done, 1)
                    if gate:
                        dve.wait_ge(ring_full, ring.done(phase, s, b, "gate", 0))
                        nc.vector.tensor_tensor(lg[:, :], ring_bank(phase, s, "gate", 0)[:, 0:E], bg_sb[:, :], ALU.add).then_inc(ring_done, 1)
                    if front:
                        if phase == "first" and s + 1 < len(piece_groups):
                            split_pieces(s + 1)
                    if gate:
                        dve.wait_ge(ring_done, ring.done(phase, s, b, "gate", 0))
                        link(nc.vector.reduce_max(rmin[:, :], lg[:, :], axis=AX))
                        nc.vector.tensor_scalar(less_top[:, :], lg[:, :], rmin[:, :], None, ALU.subtract).then_inc(rlog_done, 1)
                        dve.wait_ge(rlog_done, at(gate[1], gate[0] + 1))
                        link(nc.vector.scalar_tensor_tensor(out=rkey[:, :], in0=less_top[:, :], scalar=0.0, in1=e_less[:, :],
                                                            op0=ALU.is_equal, op1=ALU.mult))
                        link(nc.vector.tensor_reduce(rmin[:, :], rkey[:, :], AX, ALU.min))
                        nc.vector.tensor_scalar(onehot[:, :], e_less[:, :], rmin[:, :], None, ALU.is_equal).then_inc(onehot_done, 1)
                steps(dve, step)

                dve.wait_ge(ring_done, ring.done("last", NT + TAIL - 1, B - 1, "rank", 0))
                nc.vector.tensor_copy(pad_row[:, :], filled[:, :]).then_inc(pads_known, 1)
                link(nc.vector.tensor_tensor(pages[:, 1, :], filled[:, :], region0[:, :], ALU.subtract))
                link(nc.vector.tensor_scalar(pages[:, 1, :], pages[:, 1, :], float(P - 1), None, ALU.add))
                link(nc.vector.tensor_copy(pages_i[:, 0, :], pages[:, 1, :]))
                link(nc.vector.tensor_scalar(pages_i[:, 1, :], pages_i[:, 0, :], 7, None, ALU.arith_shift_right))
                link(nc.vector.tensor_copy(pages[:, 0, :], pages_i[:, 1, :]))
                link(nc.vector.tensor_copy(pages[:, 2, 0:1], pages[:, 0, 0:1]))
                for e in range(1, E):
                    link(nc.vector.tensor_tensor(pages[:, 2, e:e + 1], pages[:, 2, e - 1:e], pages[:, 0, e:e + 1], ALU.add))
                link(nc.vector.tensor_scalar(pages[:, 3, :], pages[:, 0, :], -float(P), float(REGION), ALU.mult, ALU.add))
                full = [P, TAB, E]
                link(nc.vector.tensor_tensor(passed[:, 0, :, :], karr[:, :].unsqueeze(2).broadcast_to(full),
                                             pages[:, 2, :].unsqueeze(1).broadcast_to(full), ALU.is_ge))
                link(nc.vector.tensor_tensor(passed[:, 1, :, :], passed[:, 0, :, :],
                                             pages[:, 3, :].unsqueeze(1).broadcast_to(full), ALU.mult))
                link(nc.vector.reduce_sum(tabf[:, 0, :], passed[:, 0, :, :], axis=AX))
                link(nc.vector.tensor_scalar(tabf[:, 0, :], tabf[:, 0, :], float(E - 1), None, ALU.min))
                link(nc.vector.tensor_tensor(tabf[:, 1, :].rearrange("p (g n) -> p g n", n=SLOTS), tabf[:, 0, :].rearrange("p (g n) -> p g n", n=SLOTS),
                                             expert_scale[:, :].unsqueeze(1).broadcast_to([P, GROUPS + 1, SLOTS]), ALU.mult))
                link(nc.vector.reduce_sum(placed[:, :], tabf[:, 1, :].rearrange("p (g n) -> p g n", n=SLOTS), axis=AX))
                link(nc.vector.tensor_copy(packed_i[:, 0, :], placed[:, :]))
                link(nc.vector.tensor_scalar(packed_i[:, 1, :], packed_i[:, 0, :], E - 1, EXPERT_BITS * SLOTS,
                                             ALU.bitwise_and, ALU.logical_shift_left))
                link(nc.vector.tensor_tensor(expert_tab[:, :], packed_i[:, 0, 0:GROUPS], packed_i[:, 1, 1:GROUPS + 1], ALU.bitwise_or))
                link(nc.vector.reduce_sum(tabf[:, 1, :], passed[:, 1, :, :], axis=AX))
                link(nc.vector.scalar_tensor_tensor(out=tabf[:, 0, :], in0=karr[:, :], scalar=float(P), in1=tabf[:, 1, :],
                                                    op0=ALU.mult, op1=ALU.add))
                nc.vector.tensor_scalar(row_tab[:, :], tabf[:, 0, :], float(E * REGION), None, ALU.min).then_inc(tables_done, 1)
                dve.wait_ge(tables_done, 1)

            mix.pop_all().close()

        ffn = ExitStack()
        with ffn:
            def fb(name, shape, dt):
                return sb(name, shape, dt, ffn)

            page = fb("page", [P, SLOTS, ROWLEN], F32)
            pT = fb("pT", [P, SLOTS, 2, D], F16)
            hpre = fb("hpre", [P, D], F32)
            hact = fb("hact", [P, D], F32)
            hT = fb("hT", [P, 2, D], F16)
            t2 = fb("t2", [P, D], F32)
            z3 = fb("z3", [P, D], F32)
            st3 = fb("st3", [P, 12], F32)
            idx = fb("idx", [P, SLOTS], I32)

            page_in = [sem(f"page_in{i}") for i in range(SLOTS)]
            pT_ready = sem("pT_ready")
            pTh_done = sem("pTh_done")
            pTl_done = sem("pTl_done")
            h_ready = sem("h_ready")
            hpre_done = sem("hpre_done")
            gelu_done = sem("gelu_done")
            hT_ready = sem("hT_ready")
            hTh_done = sem("hTh_done")
            hTl_done = sem("hTl_done")
            o_ready = sem("o_ready")
            o_read = sem("o_read")
            fvar_done = sem("fvar_done")
            frstd_done = sem("frstd_done")
            y3_done = sem("y3_done")
            f_chain = sem("f_chain")
            out_done = [sem(f"out_done{i}") for i in range(SLOTS)]

            h_bank, hT_bank, o_bank = banks[1], banks[2], banks[3]
            pT_banks = [banks[n] for n in (0, 4)] * (SLOTS // 2)
            assert nc.sbuf_base <= W_AT
            F_PER = SLOTS * 4

            block = ffn.enter_context(nc.Block())

            @block.sync
            def _(sp):
                sp.sem_inc(late_in, 1)

                def load(row, u):
                    sp.dma_start(page[:, u, :], sorted_dram[bass.ds(row, P), :]).then_inc(page_in[u], 16)

                for u in range(SLOTS):
                    load(first_pages[u], u)
                for e in range(EARLY_E, E):
                    load_expert(sp, e)
                with sp.Fori(0, GROUPS) as g:
                    rows = page_rows(g + 1)
                    for u in range(SLOTS):
                        sp.wait_ge(out_done[u], g * 16 + 16)
                        alone(sp)
                        load(rows[u], u)
                for u in range(SLOTS):
                    sp.wait_ge(page_in[u], 16 * (GROUPS + 1))

            @block.scalar
            def _(act):
                def pT_high(k, u):
                    act.wait_ge(pT_ready, k + 1)
                    nc.scalar.activation(pT[:, u, 0, :], pT_banks[u][:, :], ACT.Copy).then_inc(pTh_done, 1)

                def gelu(k):
                    act.wait_ge(hpre_done, k + 1)
                    nc.scalar.activation(hact[:, :], hpre[:, :], ACT.Gelu).then_inc(gelu_done, 1)

                def hT_high(k):
                    act.wait_ge(hT_ready, k + 1)
                    nc.scalar.activation(hT[:, 0, :], hT_bank[:, :], ACT.Copy).then_inc(hTh_done, 1)

                pT_high(0, 0)
                pT_high(1, 1)
                gelu(0)
                with act.Fori(0, GROUPS) as g:
                    for u in range(SLOTS):
                        pT_high(g * SLOTS + (u + 2), (u + 2) % SLOTS)
                        hT_high(g * SLOTS + u)
                        gelu(g * SLOTS + (u + 1))
                hT_high(PAGES)

            @block.tensor
            def _(pe):
                def transposes(bank, src, signal):
                    for c in range(DC):
                        ins = nc.tensor.transpose(bank[:, c * P:(c + 1) * P], src[:, c * P:(c + 1) * P], ident[:, :])
                    ins.then_inc(signal, 1)

                def weight_cols(expert):
                    return [pe.snap((E - 1 - e) * EXPERT) for e in expert]

                def product(bank, stat, w, col):
                    alone(pe)
                    n = 0
                    for c in range(DC):
                        for a, m in ((0, 0), (0, 1), (1, 0)):
                            ins = nc.tensor.matmul(bank[:, :], stat(a, c), ws[:, bass.ds(col + (c * 4 + m * 2 + w) * D, D)],
                                                   start=(n == 0), stop=(n == 3 * DC - 1))
                            n += 1
                    return ins

                def weights_there(expert):
                    late = (expert + (E - EARLY_E)) >> EXPERT_BITS
                    pe.wait_ge(late_in, pe.snap(late * (16 * (E - EARLY_E)) + 1))
                    alone(pe)

                def first(k, u, col):
                    pe.wait_ge(pTl_done, k + 1)
                    if not isinstance(k, int) or k > 0:
                        pe.wait_ge(hpre_done, k)
                    product(h_bank, lambda a, c: pT[:, u, a, c * P:(c + 1) * P], 0, col).then_inc(h_ready, 1)

                pe.wait_ge(page_in[0], 16)
                transposes(pT_banks[0], page[:, 0, :], pT_ready)
                pe.wait_ge(pTl_done, 1)
                pe.wait_ge(page_in[1], 16)
                transposes(pT_banks[1], page[:, 1, :], pT_ready)
                pe.wait_ge(early_in, 16 * EARLY_E)
                expert = experts(pe, 0)
                col = weight_cols(expert)
                weights_there(expert[0])
                first(0, 0, col[0])
                with pe.Fori(0, GROUPS) as g:
                    expert = experts(pe, g)
                    col = weight_cols(expert)
                    weights_there(expert[SLOTS])
                    for u in range(SLOTS):
                        v = (u + 2) % SLOTS
                        pe.wait_ge(page_in[v], g * 16 + (16 if u + 2 < SLOTS else 32))
                        pe.wait_ge(pTl_done, g * SLOTS + (u + 2))
                        transposes(pT_banks[v], page[:, v, :], pT_ready)
                        pe.wait_ge(gelu_done, g * SLOTS + (u + 1))
                        transposes(hT_bank, hact, hT_ready)
                        first(g * SLOTS + (u + 1), (u + 1) % SLOTS, col[u + 1])
                        pe.wait_ge(hTl_done, g * SLOTS + (u + 1))
                        product(o_bank, lambda a, c: hT[:, a, c * P:(c + 1) * P], 1, col[u]).then_inc(o_ready, 1)
                pe.wait_ge(gelu_done, PAGES + 1)
                transposes(hT_bank, hact, hT_ready)

            @block.gpsimd
            def _(pool):
                with pool.Fori(0, GROUPS) as g:
                    for u in range(SLOTS):
                        pool.wait_ge(fvar_done, g * SLOTS + (u + 1))
                        nc.gpsimd.tensor_tensor(st3[:, 9:10], st3[:, 8:9], half_neg[:, :], ALU.pow).then_inc(frstd_done, 1)
                        pool.wait_ge(y3_done, g * SLOTS + (u + 1))
                        alone(pool)
                        nc.gpsimd.indirect_dma_start(out=out_rows, out_offset=bass.IndirectOffsetOnAxis(ap=idx[:, u:u + 1], axis=0),
                                                     in_=page[:, u, 0:D], in_offset=None, bounds_check=NTOK - 1,
                                                     oob_is_err=False).then_inc(out_done[u], 16)
                for u in range(SLOTS):
                    pool.wait_ge(out_done[u], 16 * GROUPS)

            @block.vector
            def _(dve):
                def pT_low(k, u):
                    dve.wait_ge(pTh_done, k + 1)
                    nc.vector.tensor_tensor(pT[:, u, 1, :], pT_banks[u][:, :], pT[:, u, 0, :], ALU.subtract).then_inc(pTl_done, 1)

                def hT_low(k):
                    dve.wait_ge(hTh_done, k + 1)
                    nc.vector.tensor_tensor(hT[:, 1, :], hT_bank[:, :], hT[:, 0, :], ALU.subtract).then_inc(hTl_done, 1)

                def bias(b_sb, expert):
                    return b_sb[:, bass.ds(expert * D, D)]

                def hidden(k, expert):
                    dve.wait_ge(h_ready, k + 1)
                    nc.vector.scalar_tensor_tensor(out=hpre[:, :], in0=h_bank[:, :], scalar=1.0 / WEIGHT_SCALE,
                                                   in1=bias(b1s, expert), op0=ALU.mult, op1=ALU.add).then_inc(hpre_done, 1)

                def finish(g, u):
                    dve.wait_ge(frstd_done, g * SLOTS + (u + 1))
                    nc.vector.tensor_scalar(page[:, u, 0:D], z3[:, :], st3[:, 6:7], st3[:, 9:10], ALU.subtract, ALU.mult).then_inc(y3_done, 1)
                    dve.wait_ge(y3_done, g * SLOTS + (u + 1))

                pT_low(0, 0)
                pT_low(1, 1)
                expert = experts(dve, 0)
                dve.wait_ge(bias_in, 32)
                hidden(0, expert[0])
                hT_low(0)
                with dve.Fori(0, GROUPS) as g:
                    n_f = [0]

                    def link(ins, own=False):
                        n_f[0] += 1
                        ins.then_inc(f_chain, 1)
                        dve.wait_ge(f_chain, g * F_PER + n_f[0])
                        if own:
                            alone(dve)

                    expert = experts(dve, g)
                    for u in range(SLOTS):
                        hidden(g * SLOTS + (u + 1), expert[u + 1])
                        pT_low(g * SLOTS + (u + 2), (u + 2) % SLOTS)
                        if u > 0:
                            finish(g, u - 1)
                        dve.wait_ge(o_ready, g * SLOTS + (u + 1))
                        nc.vector.scalar_tensor_tensor(out=t2[:, :], in0=o_bank[:, :], scalar=1.0 / WEIGHT_SCALE,
                                                       in1=bias(b2s, expert[u]), op0=ALU.mult, op1=ALU.add).then_inc(o_read, 1)
                        dve.wait_ge(o_read, g * SLOTS + (u + 1))
                        link(nc.vector.scalar_tensor_tensor(out=z3[:, :], in0=t2[:, :], scalar=page[:, u, D:D + 1],
                                                            in1=page[:, u, 0:D], op0=ALU.mult, op1=ALU.add))
                        hT_low(g * SLOTS + (u + 1))
                        link(nc.vector.bn_stats(st3[:, 0:6], z3[:, :]), own=True)
                        link(nc.vector.bn_aggr(st3[:, 6:8], st3[:, 0:6]))
                        nc.vector.tensor_scalar(st3[:, 8:9], st3[:, 7:8], EPS, None, ALU.add).then_inc(fvar_done, 1)
                        link(nc.vector.tensor_copy(idx[:, u:u + 1], page[:, u, D + 1:D + 2]))
                        if u == SLOTS - 1:
                            finish(g, u)
                    assert n_f[0] == F_PER, n_f[0]


def kernel(**inputs):
    import numpy as _np
    import concourse.bacc as _bacc
    from concourse import mybir as _mybir
    from concourse.bass_utils import run_bass_kernel_spmd as _run

    a = {k: _np.asarray(v) for k, v in inputs.items()}
    given = {
        "x": a["x"],
        "xT": a["x"].transpose(0, 2, 1),
        "ctxT": a["ctx_1024"].transpose(0, 2, 1),
        "winT": a["L0_attn_W_in"].T,
        "wattnT": a["L0_attn_W_attn"].T,
        "woutT": a["L0_attn_W_out"].T,
        "scale_w": a["L0_attn_scale_weights"],
        "wg": a["L0_ffn_Wg"],
        "bg": a["L0_ffn_bg"],
        "w1": a["L0_ffn_W1"],
        "b1": a["L0_ffn_b1"],
        "w2": a["L0_ffn_W2"],
        "b2": a["L0_ffn_b2"],
    }
    nc = _bacc.Bacc("TRN2", target_bir_lowering=False, num_devices=1)
    arrays, args = {}, []
    for name, v in given.items():
        v = _np.ascontiguousarray(v)
        arrays[f"in_{name}"] = v
        args.append(nc.dram_tensor(f"in_{name}", v.shape, _mybir.dt.from_np(v.dtype), kind="ExternalInput").ap())
    args.append(nc.dram_tensor("out", a["x"].shape, _mybir.dt.from_np(_np.dtype("float32")), kind="ExternalOutput").ap())
    decoder_layer(nc, *args)
    r = _run(nc, [arrays], core_ids=[0])
    return r.results[0]["out"]
```
